# Optimizing a Trainium2 kernel written in Bass

```python
import numpy as np
import jax
import jax.numpy as jnp

def _softmax(x, axis=-1):
    return jax.nn.softmax(x, axis=axis)

def _gelu(x):
    return jax.nn.gelu(x, approximate=True)

def _silu(x):
    return jax.nn.silu(x)

def _sigmoid(x):
    return jax.nn.sigmoid(x)

def _layernorm(x, axis=-1, eps=1e-05):
    m = jnp.mean(x, axis=axis, keepdims=True)
    v = jnp.var(x, axis=axis, keepdims=True)
    return (x - m) / jnp.sqrt(v + eps)

def _scatter_add(tgt, idx, src, axis=0):
    return tgt.at[idx].add(src)

def _segment_sum(src, seg, n):
    return jax.ops.segment_sum(src, seg, n)
kernel_name = 'mk_prb_d2_jaxref_r8_e16edb'

def setup_inputs(seed: int=0):
    np.random.seed(seed)
    _w = jnp.asarray

    def _L0_attn_setup():
        import jax, jax.numpy as jnp
        import numpy as np
        B, T, D = (1, 256, 256)
        H, DK, DV, M = (16, 64, 128, 64)
        KEY_DIM, VALUE_DIM = (H * DK, H * DV)
        EPS = 1e-05
        CLAMP_MIN, CLAMP_MAX = (-32.0, 32.0)
        XAVIER_GAIN = 2.0 ** (-2.5)

        def _chunk_abc(q, k, v, s):
            scale = q.shape[-1] ** (-0.5)
            z = jax.lax.cumlogsumexp(s, axis=2)
            g = jnp.exp(jnp.concatenate([z[:, :, :1], z[:, :, :-1]], axis=2) - z)
            p = jnp.exp(s - z)
            tfirst = lambda x: jnp.moveaxis(x, 2, 0)
            qT, kT, vT, pT, gT = map(tfirst, (q * scale, k, v, p, g))
            b, h = (q.shape[0], q.shape[1])
            hk0 = jnp.zeros((b, h, q.shape[-1], s.shape[-1]), q.dtype)

            def step_k(hk, x):
                q_t, k_t, p_t, g_t = x
                hk = hk * g_t[:, :, None, :] + k_t[..., None] * p_t[:, :, None, :]
                return (hk, jnp.einsum('bhk,bhkm->bhm', q_t, hk))
            _, okT = jax.lax.scan(step_k, hk0, (qT, kT, pT, gT))
            pvT = jax.nn.softmax(okT, axis=-1)
            hv0 = jnp.zeros((b, h, s.shape[-1], v.shape[-1]), q.dtype)

            def step_v(hv, x):
                pv_t, v_t, p_t, g_t = x
                hv = hv * g_t[..., None] + p_t[..., None] * v_t[:, :, None, :]
                return (hv, jnp.einsum('bhm,bhmv->bhv', pv_t, hv))
            _, ovT = jax.lax.scan(step_v, hv0, (pvT, vT, pT, gT))
            return jnp.moveaxis(ovT, 0, 2)
        key = jax.random.key(seed)
        ks = jax.random.split(key, 8)

        def w(k, fan_in, fan_out):
            std = XAVIER_GAIN * np.sqrt(2.0 / (fan_in + fan_out))
            return jax.random.normal(k, (fan_in, fan_out), jnp.float32) * std
        return {'hidden_states': jax.random.normal(ks[0], (B, T, D), jnp.float32), 'Wq': w(ks[1], D, KEY_DIM), 'Wk': w(ks[2], D, KEY_DIM), 'Wv': w(ks[3], D, VALUE_DIM), 'Wg': w(ks[4], D, VALUE_DIM), 'Ws': w(ks[5], D, H * M), 'Wo': w(ks[6], VALUE_DIM, D), 'g_norm_weight': jnp.ones((DV,), jnp.float32)}
    _L0_attn_in = _L0_attn_setup()

    def _L0_ffn_setup():
        import jax, jax.numpy as jnp
        import numpy as np
        NUM_EXPERTS = 64
        TOP_K = 8
        HIDDEN = 256
        INTER = 128
        key = jax.random.key(seed)
        k1, k2, k3, k4 = jax.random.split(key, 4)
        scale = 1.0 / np.sqrt(HIDDEN)
        hidden_states = jax.random.normal(k1, (4, 256, HIDDEN), dtype=jnp.float32)
        gate_w = jax.random.normal(k2, (NUM_EXPERTS, HIDDEN), dtype=jnp.float32) * scale
        w13 = jax.random.normal(k3, (NUM_EXPERTS, 2 * INTER, HIDDEN), dtype=jnp.float32) * scale
        w2 = jax.random.normal(k4, (NUM_EXPERTS, HIDDEN, INTER), dtype=jnp.float32) * (1.0 / np.sqrt(INTER))
        return {'hidden_states': hidden_states, 'gate_w': gate_w, 'w13': w13, 'w2': w2}
    _L0_ffn_in = _L0_ffn_setup()

    def _L1_attn_setup():
        import jax, jax.numpy as jnp
        import numpy as np
        EPS = 1.1920929e-07

        def _rms(x):
            return x * jax.lax.rsqrt(jnp.mean(x * x, axis=-1, keepdims=True) + EPS)
        key = jax.random.key(seed)
        k0, k1, k2, k3 = jax.random.split(key, 4)
        B, S, D, DFF = (4, 256, 256, 1024)
        x = jax.random.normal(k0, (B, S, D), dtype=jnp.float32)
        w_qkv = jax.random.normal(k1, (3 * D, D), dtype=jnp.float32) * 0.02
        w_swiglu = jax.random.normal(k2, (2 * DFF, D), dtype=jnp.float32) * 0.02
        w_out = jax.random.normal(k3, (D, DFF), dtype=jnp.float32) * 0.02
        return {'x': x, 'w_qkv': w_qkv, 'w_swiglu': w_swiglu, 'w_out': w_out}
    _L1_attn_in = _L1_attn_setup()

    def _L1_ffn_setup():
        import jax, jax.numpy as jnp
        import numpy as np
        HID = 256
        N_EXP = 32
        F_EXP = 96
        TOP_K = 6
        F_SH = 192
        B, S = (1, 128)
        key = jax.random.key(seed)
        ks = jax.random.split(key, 8)
        s = 0.02
        return {'hidden_states': jax.random.normal(ks[0], (B, S, HID), dtype=jnp.float32), 'gate_w': jax.random.normal(ks[1], (HID, N_EXP), dtype=jnp.float32) * s, 'wg': jax.random.normal(ks[2], (N_EXP, HID, F_EXP), dtype=jnp.float32) * s, 'wu': jax.random.normal(ks[3], (N_EXP, HID, F_EXP), dtype=jnp.float32) * s, 'wd': jax.random.normal(ks[4], (N_EXP, F_EXP, HID), dtype=jnp.float32) * s, 'sg': jax.random.normal(ks[5], (HID, F_SH), dtype=jnp.float32) * s, 'su': jax.random.normal(ks[6], (HID, F_SH), dtype=jnp.float32) * s, 'sd': jax.random.normal(ks[7], (F_SH, HID), dtype=jnp.float32) * s}
    _L1_ffn_in = _L1_ffn_setup()
    _d = {'L0_attn_hidden_states': _L0_attn_in['hidden_states'], 'L0_attn_Wq': _L0_attn_in['Wq'], 'L0_attn_Wk': _L0_attn_in['Wk'], 'L0_attn_Wv': _L0_attn_in['Wv'], 'L0_attn_Wg': _L0_attn_in['Wg'], 'L0_attn_Ws': _L0_attn_in['Ws'], 'L0_attn_Wo': _L0_attn_in['Wo'], 'L0_attn_g_norm_weight': _L0_attn_in['g_norm_weight'], 'L0_ffn_gate_w': _L0_ffn_in['gate_w'], 'L0_ffn_w13': _L0_ffn_in['w13'], 'L0_ffn_w2': _L0_ffn_in['w2'], 'L1_attn_w_qkv': _L1_attn_in['w_qkv'], 'L1_attn_w_swiglu': _L1_attn_in['w_swiglu'], 'L1_attn_w_out': _L1_attn_in['w_out'], 'L1_ffn_gate_w': _L1_ffn_in['gate_w'], 'L1_ffn_wg': _L1_ffn_in['wg'], 'L1_ffn_wu': _L1_ffn_in['wu'], 'L1_ffn_wd': _L1_ffn_in['wd'], 'L1_ffn_sg': _L1_ffn_in['sg'], 'L1_ffn_su': _L1_ffn_in['su'], 'L1_ffn_sd': _L1_ffn_in['sd']}
    _x0 = _d['L0_attn_hidden_states']
    _d['L0_attn_hidden_states'] = jax.random.normal(jax.random.fold_in(jax.random.key(seed), 1), (1, 1024, 256), dtype=_x0.dtype)
    del _x0
    return _d

def reference(L0_attn_hidden_states, L0_attn_Wq, L0_attn_Wk, L0_attn_Wv, L0_attn_Wg, L0_attn_Ws, L0_attn_Wo, L0_attn_g_norm_weight, L0_ffn_gate_w, L0_ffn_w13, L0_ffn_w2, L1_attn_w_qkv, L1_attn_w_swiglu, L1_attn_w_out, L1_ffn_gate_w, L1_ffn_wg, L1_ffn_wu, L1_ffn_wd, L1_ffn_sg, L1_ffn_su, L1_ffn_sd):

    def _L0_attn_ref(hidden_states, Wq, Wk, Wv, Wg, Ws, Wo, g_norm_weight):
        import jax, jax.numpy as jnp
        import numpy as np
        B, T, D = (1, 256, 256)
        H, DK, DV, M = (16, 64, 128, 64)
        KEY_DIM, VALUE_DIM = (H * DK, H * DV)
        EPS = 1e-05
        CLAMP_MIN, CLAMP_MAX = (-32.0, 32.0)
        XAVIER_GAIN = 2.0 ** (-2.5)

        def _chunk_abc(q, k, v, s):
            scale = q.shape[-1] ** (-0.5)
            z = jax.lax.cumlogsumexp(s, axis=2)
            g = jnp.exp(jnp.concatenate([z[:, :, :1], z[:, :, :-1]], axis=2) - z)
            p = jnp.exp(s - z)
            tfirst = lambda x: jnp.moveaxis(x, 2, 0)
            qT, kT, vT, pT, gT = map(tfirst, (q * scale, k, v, p, g))
            b, h = (q.shape[0], q.shape[1])
            hk0 = jnp.zeros((b, h, q.shape[-1], s.shape[-1]), q.dtype)

            def step_k(hk, x):
                q_t, k_t, p_t, g_t = x
                hk = hk * g_t[:, :, None, :] + k_t[..., None] * p_t[:, :, None, :]
                return (hk, jnp.einsum('bhk,bhkm->bhm', q_t, hk))
            _, okT = jax.lax.scan(step_k, hk0, (qT, kT, pT, gT))
            pvT = jax.nn.softmax(okT, axis=-1)
            hv0 = jnp.zeros((b, h, s.shape[-1], v.shape[-1]), q.dtype)

            def step_v(hv, x):
                pv_t, v_t, p_t, g_t = x
                hv = hv * g_t[..., None] + p_t[..., None] * v_t[:, :, None, :]
                return (hv, jnp.einsum('bhm,bhmv->bhv', pv_t, hv))
            _, ovT = jax.lax.scan(step_v, hv0, (pvT, vT, pT, gT))
            return jnp.moveaxis(ovT, 0, 2)
        b, t, _ = hidden_states.shape
        to_heads = lambda x, d: jnp.transpose(x.reshape(b, t, H, d), (0, 2, 1, 3))
        q = to_heads(hidden_states @ Wq, DK)
        k = to_heads(hidden_states @ Wk, DK)
        v = to_heads(hidden_states @ Wv, DV)
        s = jnp.clip(to_heads(hidden_states @ Ws, M), CLAMP_MIN, CLAMP_MAX)
        o = jnp.transpose(_chunk_abc(q, k, v, s), (0, 2, 1, 3))
        g = (hidden_states @ Wg).reshape(b, t, H, DV)
        o = o * jax.lax.rsqrt(jnp.mean(jnp.square(o), axis=-1, keepdims=True) + EPS) * g_norm_weight
        o = o * (g * jax.nn.sigmoid(g))
        return o.reshape(b, t, VALUE_DIM) @ Wo

    def _L0_ffn_ref(hidden_states, gate_w, w13, w2):
        import jax, jax.numpy as jnp
        import numpy as np
        NUM_EXPERTS = 64
        TOP_K = 8
        HIDDEN = 256
        INTER = 128
        orig_shape = hidden_states.shape
        x = hidden_states.reshape(-1, HIDDEN)
        logits = jnp.einsum('th,eh->te', x, gate_w)
        probs = jax.nn.softmax(logits, axis=-1)
        topk_w, topk_idx = jax.lax.top_k(probs, TOP_K)
        combine = (jax.nn.one_hot(topk_idx, NUM_EXPERTS, dtype=x.dtype) * topk_w[..., None]).sum(axis=1)

        def step(acc, inp):
            w13_e, w2_e, c = inp
            g = x @ w13_e[:INTER].T
            u = x @ w13_e[INTER:].T
            h = jax.nn.silu(g) * u
            o = h @ w2_e.T
            return (acc + c[:, None] * o, None)
        out0 = jnp.zeros_like(x)
        out, _ = jax.lax.scan(step, out0, (w13, w2, combine.T))
        return out.reshape(orig_shape)

    def _L1_attn_ref(x, w_qkv, w_swiglu, w_out):
        import jax, jax.numpy as jnp
        import numpy as np
        EPS = 1.1920929e-07

        def _rms(x):
            return x * jax.lax.rsqrt(jnp.mean(x * x, axis=-1, keepdims=True) + EPS)
        qkv = _rms(x) @ w_qkv.T
        q, k, v = jnp.split(qkv, 3, axis=-1)
        q = _rms(q)
        k = _rms(k)
        w = jnp.exp(k)
        kv_cum = jnp.cumsum(w * v, axis=1)
        w_cum = jnp.cumsum(w, axis=1)
        y = jax.nn.sigmoid(q) * (kv_cum / (w_cum + 1e-06))
        uv = y @ w_swiglu.T
        u, g = jnp.split(uv, 2, axis=-1)
        return x + u * jax.nn.silu(g) @ w_out.T

    def _L1_ffn_ref(hidden_states, gate_w, wg, wu, wd, sg, su, sd):
        import jax, jax.numpy as jnp
        import numpy as np
        HID = 256
        N_EXP = 32
        F_EXP = 96
        TOP_K = 6
        F_SH = 192
        B, S = (1, 128)
        orig_shape = hidden_states.shape
        x = hidden_states.reshape(-1, HID)
        scores = jax.nn.sigmoid(x @ gate_w)
        topk_w, topk_i = jax.lax.top_k(scores, TOP_K)
        topk_w = topk_w / (jnp.sum(topk_w, axis=-1, keepdims=True) + 1e-20)
        combine = jnp.sum(jax.nn.one_hot(topk_i, N_EXP, dtype=topk_w.dtype) * topk_w[..., None], axis=1)
        g = jnp.einsum('td,edf->tef', x, wg)
        u = jnp.einsum('td,edf->tef', x, wu)
        act = jax.nn.silu(g) * u
        routed = jnp.einsum('tef,efd,te->td', act, wd, combine)
        routed = routed.reshape(orig_shape)
        shared = jax.nn.silu(hidden_states @ sg) * (hidden_states @ su) @ sd
        return routed + shared
    x = L0_attn_hidden_states
    xn = _layernorm(x, axis=-1)
    x = x + _L0_attn_ref(xn, L0_attn_Wq, L0_attn_Wk, L0_attn_Wv, L0_attn_Wg, L0_attn_Ws, L0_attn_Wo, L0_attn_g_norm_weight) + _L0_ffn_ref(xn, L0_ffn_gate_w, L0_ffn_w13, L0_ffn_w2)
    xn = _layernorm(x, axis=-1)
    x = x + _L1_attn_ref(xn, L1_attn_w_qkv, L1_attn_w_swiglu, L1_attn_w_out) + _L1_ffn_ref(xn, L1_ffn_gate_w, L1_ffn_wg, L1_ffn_wu, L1_ffn_wd, L1_ffn_sg, L1_ffn_su, L1_ffn_sd)
    return x

_drawn_inputs = setup_inputs


def setup_inputs(seed=0):
    import zlib

    import numpy as np

    out = dict(_drawn_inputs(seed))
    spreads = {'L0_attn_g_norm_weight': (1.0, 0.6)}
    factors = {'L0_attn_Wq': 25.153,
     'L0_attn_Wk': 25.902,
     'L0_attn_Wv': 7.463,
     'L0_attn_Wg': 7.41,
     'L0_attn_Ws': 8.0,
     'L0_attn_Wo': 7.387,
     'L1_attn_w_qkv': 8.0,
     'L1_attn_w_swiglu': 8.0,
     'L1_attn_w_out': 8.0,
     'L1_ffn_gate_w': 8.0,
     'L1_ffn_wg': 8.0,
     'L1_ffn_wu': 8.0,
     'L1_ffn_wd': 8.0,
     'L1_ffn_sg': 7.883,
     'L1_ffn_su': 7.761,
     'L1_ffn_sd': 7.778}
    for name, (base, spread) in spreads.items():
        noise = np.random.default_rng([zlib.crc32(name.encode()), seed]).standard_normal(out[name].shape)
        drawn = base * np.exp(spread * noise) if base else spread * noise
        out[name] = jnp.asarray(drawn.astype(out[name].dtype))
    for name, factor in factors.items():
        out[name] = (out[name] * factor).astype(out[name].dtype)
    return out
```

```python
from contextlib import ExitStack

import concourse.bass as bass
from concourse import mybir

F32 = mybir.dt.float32
ALU = mybir.AluOpType
ACT = mybir.ActivationFunctionType
AX = mybir.AxisListType.X

P = 128
T, D = 1024, 256
TT = T // P
KD = D // P
NP = 8
HALF = T // 2
EPS_LN, EPS_O, EPS_RMS = 1e-5, 1e-5, 1.1920929e-07
E0, TOP0, F0 = 64, 8, 128
E1, TOP1, F1, SH = 32, 6, 96, 2
ESW = 8
WROW = 4 * P + D

USES = [("s", 2, "D"), ("k", 2, "A"), ("q", 2, "D"), ("oT", 4, "D"), ("wo", 4, "D"),
        ("tr", 8, "A"), ("v", 4, "A"), ("g", 4, "D"), ("pvT", 2, "D")]
FIRST_USE, READERS = {}, []
for _name, _n, _who in USES:
    FIRST_USE[_name] = len(READERS)
    READERS += [_who] * _n
NG = len(READERS)


def readers_before(n, who):
    return sum(r == who for r in READERS[:n])


NGD, NGA = readers_before(NG, "D"), readers_before(NG, "A")


def need(eng, sem, value):
    if isinstance(value, int) and value <= 0:
        return
    eng.wait_ge(sem, value)


def build(nc, x, wqks, wvg, wo, gnw, gate0, w0, wqkv, wsw, gate1, w1, out):
    ctx = ExitStack()
    with ctx:
        def sb(name, *shape):
            return ctx.enter_context(nc.sbuf_tensor(name, [P, *shape], F32))

        def sem(name):
            return ctx.enter_context(nc.semaphore(name))

        bank = [ctx.enter_context(nc.psum_tensor(f"bank{i}", [P, 512], F32)) for i in range(8)]
        G, SC, OUT, ST_K, ST_V = bank[0:2], bank[2:4], bank[4:6], bank[6], bank[7]

        ident = sb("ident", P)
        causal = sb("causal", 2, P)
        ones = sb("ones", T)
        neg_half = sb("neg_half", 16)
        acc = sb("acc", TT, D)
        xn = sb("xn", TT, D)
        xnT = sb("xnT", KD, T)
        stats = sb("stats", TT, 6)
        mv = sb("mv", TT, 2)
        veps = sb("veps", TT)
        rstd = sb("rstd", TT)
        gate0_sb = sb("gate0_sb", KD, E0)
        gate1_sb = sb("gate1_sb", KD, E1)
        comb0 = sb("comb0", TT, E0)
        comb1 = sb("comb1", TT, E1 + SH)
        prob = sb("prob", TT, E0)
        left = sb("left", TT, E0)
        top = sb("top", TT, 8)
        rmax = sb("rmax", TT)
        rsum = sb("rsum", TT)
        wqks_sb = sb("wqks_sb", 3, KD, P)
        wvg_sb = sb("wvg_sb", KD, 2, D)
        wo_raw = sb("wo_raw", 2, D)
        wo_sb = sb("wo_sb", 2, D)
        gnw_sb = sb("gnw_sb", 1)
        sclip = sb("sclip", T)
        eT = sb("eT", T)
        zT = sb("zT", T)
        rT = sb("rT", T)
        kT = sb("kT", T)
        qbd = sb("qbd", TT, 2, P)
        pbd = sb("pbd", TT, 2, P)
        ker = sb("ker", TT, 3, P)
        v_sb = sb("v_sb", TT, D)
        th = sb("th", 2, HALF)
        gT = sb("gT", 2, T)
        masked = sb("masked", 2, 2 * P)
        sk_sb = sb("sk_sb", P)
        sv_sb = sb("sv_sb", D)
        ok = sb("ok", TT, P)
        pv = sb("pv", TT, P)
        mx = sb("mx", 16)
        sm = sb("sm", 16)
        rs = sb("rs", 16)
        ss = sb("ss", 16)
        pw = sb("pw", 16)
        sc16 = sb("sc16", 16)
        o_sb = sb("o_sb", TT, D)
        o_sq = sb("o_sq", TT, D)
        o_n = sb("o_n", TT, D)
        oT = sb("oT", 2, T)
        wex = sb("wex", 2, WROW)
        sil = sb("sil", 2, HALF)
        hT = sb("hT", 2, HALF)
        wqkv_sb = sb("wqkv_sb", KD, 3 * D)
        qkv = sb("qkv", TT, 3 * D)
        thq, thT, wcT = v_sb, gT, oT
        wk, wv = o_sb, o_n
        kvT = qbd[:].rearrange("p (k c) h t -> p k (c h t)", k=KD)
        wcum = pbd[:].rearrange("p (k c) h t -> p k (c h t)", k=KD)
        kvcum = ker[:].rearrange("p c a t -> p (c a t)")[:, 0:KD * T].rearrange("p (k t) -> p k t", k=KD)
        yT = kvcum

        s_x = sem("s_x"); s_c = sem("s_c"); s_pool = sem("s_pool"); s_dve = sem("s_dve")
        s_var = sem("s_var"); s_rstd = sem("s_rstd"); s_xn = sem("s_xn"); s_xT = sem("s_xT")
        s_xTe = sem("s_xTe"); s_lg = sem("s_lg"); s_sh = sem("s_sh"); s_ex = sem("s_ex"); s_comb = sem("s_comb")
        s_gw = sem("s_gw")
        s_wqks = sem("s_wqks"); s_wvg = sem("s_wvg"); s_wo = sem("s_wo"); s_wos = sem("s_wos")
        s_gfull = sem("s_gfull"); s_gD = sem("s_gD"); s_gA = sem("s_gA")
        s_e = sem("s_e"); s_rT = sem("s_rT"); s_sc = sem("s_sc"); s_mask = sem("s_mask")
        s_out = sem("s_out"); s_okD = sem("s_okD"); s_oA = sem("s_oA")
        s_st = sem("s_st"); s_stc = sem("s_stc"); s_sub = sem("s_sub"); s_pv = sem("s_pv")
        s_th = sem("s_th"); s_sq = sem("s_sq"); s_ms = sem("s_ms"); s_pw = sem("s_pw"); s_on = sem("s_on")
        s_att = sem("s_att")
        s_wex = [sem("s_wex0"), sem("s_wex1")]; s_gu = sem("s_gu"); s_sil = sem("s_sil"); s_h = sem("s_h"); s_y = sem("s_y"); s_acc = sem("s_acc")
        s_qkv = sem("s_qkv"); s_qkve = sem("s_qkve"); s_qsq = sem("s_qsq"); s_qms = sem("s_qms"); s_qpw = sem("s_qpw")
        s_thw = sem("s_thw"); s_wvv = sem("s_wvv"); s_t3 = sem("s_t3"); s_t3e = sem("s_t3e"); s_yT = sem("s_yT")
        s_res = sem("s_res"); s_rqk = sem("s_rqk"); s_done = sem("s_done")

        ABC_LINKS = 9
        PHASES = [(E0, F0), (E1 + SH, F1), (ESW, P)]
        BEFORE = [0, E0, E0 + E1 + SH, E0 + E1 + SH + ESW]

        def at(pair, per, k):
            j, off = pair
            v = off * per + k
            return v if isinstance(j, int) else j * per + v

        def prev(pair):
            return pair[0], pair[1] - 1

        def g_free(pe, pair, n):
            m = n - 2
            if pair[1] == NP and m >= 0:
                pe.wait_ge(s_gD, at(pair, NGD, m + 1))
                return
            if m < 0:
                pair, m = prev(pair), m + NG
                if pair[1] < 0:
                    return
            who = READERS[m]
            if who == "D":
                need(pe, s_gD, at(pair, NGD, readers_before(m + 1, "D")))
            else:
                need(pe, s_gA, at(pair, NGA, readers_before(m + 1, "A")))

        def first_of(name, pair):
            return FIRST_USE[name] - (FIRST_USE["oT"] if pair[1] == NP else 0)

        def read_by_dve(pair, n):
            return at(pair, NGD, n if pair[1] == NP else readers_before(n, "D"))

        def expert_units(n):
            return 2 * BEFORE[n], PHASES[n][0], PHASES[n][1]

        block = ctx.enter_context(nc.Block())

        @block.sync
        def _(sp):
            sp.dma_start(acc[:], x.rearrange("(c p) d -> p c d", p=P)).then_inc(s_x, 16)
            sp.dma_start(gate0_sb[:], gate0).then_inc(s_wex[0], 16)
            sp.dma_start(gnw_sb[:], gnw).then_inc(s_gw, 16)
            sp.dma_start(gate1_sb[:], gate1).then_inc(s_wex[1], 16)
            sp.dma_start(wqkv_sb[:], wqkv).then_inc(s_gw, 16)

            def load_pair(pair, p):
                need(sp, s_gfull, at(prev(pair), NG, FIRST_USE["oT"]) if pair[1] else 0)
                need(sp, s_wqks, at(prev(pair), 16, 16) if pair[1] else 0)
                sp.dma_start(wqks_sb[:], wqks[p]).then_inc(s_wqks, 16)
                need(sp, s_wos, at(prev(pair), 1, 1) if pair[1] else 0)
                need(sp, s_wo, at(prev(pair), 16, 16) if pair[1] else 0)
                sp.dma_start(wo_raw[:], wo[p]).then_inc(s_wo, 16)
                need(sp, s_gfull, at(prev(pair), NG, FIRST_USE["pvT"]) if pair[1] else 0)
                need(sp, s_wvg, at(prev(pair), 16, 16) if pair[1] else 0)
                sp.dma_start(wvg_sb[:], wvg[p]).then_inc(s_wvg, 16)

            load_pair((0, 0), 0)
            with sp.Fori(0, NP - 1) as j:
                load_pair((j, 1), j + 1)

            for n, w in enumerate((w0, w1, wsw)):
                u0, ne, f = expert_units(n)
                row = 4 * f + D
                with sp.Fori(0, ne // 2) as j:
                    for b in range(2):
                        sp.wait_ge(s_y, j * 4 + (u0 + 2 * b + 1))
                        sp.wait_ge(s_wex[b], j * 16 + (u0 // 4 + 1) * 16)
                        sp.dma_start(wex[:, b, 0:row], w[j * 2 + b]).then_inc(s_wex[b], 16)

            sp.wait_ge(s_acc, 2 + 2 * BEFORE[3])
            sp.dma_start(out.rearrange("(c p) d -> p c d", p=P), acc[:]).then_inc(s_done, 16)
            sp.wait_ge(s_done, 16)

        @block.gpsimd
        def _(pool):
            nc.gpsimd.memset(ident[:], 0.0).then_inc(s_pool, 1)
            nc.gpsimd.memset(causal[:], 1.0).then_inc(s_pool, 1)
            nc.gpsimd.memset(ones[:], 1.0).then_inc(s_c, 1)
            nc.gpsimd.memset(neg_half[:], -0.5).then_inc(s_c, 1)
            nc.gpsimd.memset(qbd[:], 0.0).then_inc(s_c, 1)
            nc.gpsimd.memset(pbd[:], 0.0).then_inc(s_c, 1)
            pool.wait_ge(s_pool, 2)
            nc.gpsimd.affine_select(out=ident[:], in_=ident[:], compare_op=ALU.not_equal, fill=1.0, base=0,
                                    pattern=[[-1, P]], channel_multiplier=1).then_inc(s_c, 1)
            nc.gpsimd.affine_select(out=causal[:], in_=causal[:], compare_op=ALU.is_ge, fill=0.0, base=0,
                                    pattern=[[0, 2], [1, P]], channel_multiplier=-1).then_inc(s_c, 1)
            pool.wait_ge(s_c, 6)

            def ln_power(n):
                pool.wait_ge(s_var, n + 1)
                nc.gpsimd.tensor_tensor(rstd[:], veps[:], neg_half[:, 0:TT], ALU.pow).then_inc(s_rstd, 1)

            ln_power(0)
            pool.wait_ge(s_gw, 32)
            nc.gpsimd.tensor_scalar(gnw_sb[:], gnw_sb[:], 0.5, None, ALU.mult).then_inc(s_c, 1)
            pool.wait_ge(s_c, 7)

            def pair_body(pair):
                need(pool, s_gfull, at(pair, NG, FIRST_USE["tr"]))
                pool.wait_ge(s_wo, at(pair, 16, 16))
                nc.gpsimd.tensor_tensor(wo_sb[:], wo_raw[:], gnw_sb[:].unsqueeze(2).broadcast_to([P, 2, D]),
                                        ALU.mult).then_inc(s_wos, 1)
                pool.wait_ge(s_oA, at(pair, TT, TT))
                nc.gpsimd.tensor_tensor(o_sq[:], o_sb[:], o_sb[:], ALU.mult).then_inc(s_sq, 1)
                pool.wait_ge(s_ms, at(pair, 1, 1))
                nc.gpsimd.tensor_tensor(pw[:], ss[:], neg_half[:], ALU.pow).then_inc(s_pw, 1)

            pair_body((0, 0))
            with pool.Fori(0, NP - 1) as j:
                pair_body((j, 1))

            ln_power(1)
            ln_power(2)
            for half in range(2):
                pool.wait_ge(s_qkve, 4 * half + 4)
                for c in range(4 * half, 4 * half + 4):
                    last = nc.gpsimd.tensor_tensor(
                        (o_sb if c < 4 else o_sq)[:].rearrange("p a b -> p (a b)")[:, (c % 4) * 512:(c % 4 + 1) * 512],
                        qkv[:, c, 0:512], qkv[:, c, 0:512], ALU.mult)
                last.then_inc(s_qsq, 1)
            pool.wait_ge(s_qms, 1)
            nc.gpsimd.tensor_tensor(pw[:], ss[:], neg_half[:], ALU.pow).then_inc(s_qpw, 1)

        @block.tensor
        def _(pe):
            mm = nc.tensor.matmul
            pe.wait_ge(s_c, 6)
            pe.sem_inc(s_y, 3)

            def transposed_tokens(n):
                for i in range(4):
                    pe.wait_ge(s_xn, n * TT + 2 * i + 2)
                    for c in range(2):
                        for k in range(KD):
                            o = (c * KD + k) * P
                            last = nc.tensor.transpose(bank[i][:, o:o + P],
                                                       xn[:, 2 * i + c, k * P:(k + 1) * P], ident[:])
                    last.then_inc(s_xT, 1)

            def logits(n, gate, ne):
                pe.wait_ge(s_xTe, 4 * n + 4)
                for c in range(TT):
                    for k in range(KD):
                        last = mm(bank[4][:, c * ne:(c + 1) * ne], xnT[:, k, c * P:(c + 1) * P], gate[:, k, :],
                                  start=k == 0, stop=k == KD - 1)
                last.then_inc(s_lg, 1)

            transposed_tokens(0)
            pe.wait_ge(s_gw, 32)
            pe.wait_ge(s_wex[0], 16)
            pe.wait_ge(s_wex[1], 16)
            logits(0, gate0_sb, E0)
            pe.wait_ge(s_sh, 1)

            def output_product(pair):
                pe.wait_ge(s_on, at(prev(pair), 1, 1))
                for i in range(4):
                    n = first_of("oT", pair) + i
                    g_free(pe, pair, n)
                    for c in range(2):
                        for h in range(2):
                            o = (h * 2 + c) * P
                            last = nc.tensor.transpose(G[n % 2][:, o:o + P],
                                                       o_n[:, 2 * i + c, h * P:(h + 1) * P], ident[:])
                    last.then_inc(s_gfull, 1)
                pe.wait_ge(s_wos, at(prev(pair), 1, 1))
                for i in range(4):
                    n = first_of("wo", pair) + i
                    g_free(pe, pair, n)
                    pe.wait_ge(s_gD, read_by_dve(pair, first_of("oT", pair) + i + 1))
                    for c in range(2):
                        for h in range(2):
                            t = (2 * i + c) * P
                            last = mm(G[n % 2][:, c * D:(c + 1) * D], oT[:, h, t:t + P], wo_sb[:, h, :],
                                      start=h == 0, stop=h == 1)
                    last.then_inc(s_gfull, 1)

            def pair_body(pair):
                pe.wait_ge(s_wqks, at(pair, 16, 16))
                for i in range(3):
                    for hf in range(2):
                        n = 2 * i + hf
                        g_free(pe, pair, n)
                        for k in range(KD):
                            last = mm(G[n % 2][:], wqks_sb[:, i, k, :], xnT[:, k, hf * HALF:(hf + 1) * HALF],
                                      start=k == 0, stop=k == KD - 1)
                        last.then_inc(s_gfull, 1)
                if pair[1] == 0:
                    for n in range(FIRST_USE["oT"], FIRST_USE["tr"]):
                        g_free(pe, pair, n)
                        nc.tensor.transpose(G[n % 2][:, 0:P], ident[:], ident[:]).then_inc(s_gfull, 1)
                else:
                    output_product(pair)
                pe.wait_ge(s_rT, at(pair, 1, 1))
                pe.wait_ge(s_gA, at(pair, NGA, 2))
                for c in range(TT):
                    n = FIRST_USE["tr"] + c
                    g_free(pe, pair, n)
                    for i, src in enumerate((kT, eT, rT)):
                        last = nc.tensor.transpose(G[n % 2][:, i * P:(i + 1) * P], src[:, c * P:(c + 1) * P], ident[:])
                    last.then_inc(s_gfull, 1)

                def scores(m, lhs, rhs):
                    if pair[1] == 0 and m < 2:
                        pass
                    else:
                        pe.wait_ge(s_mask, at(pair, 16, m - 1))
                    mm(SC[m % 2][:, 0:2 * P], lhs, rhs, start=True, stop=True).then_inc(s_sc, 1)

                def out_free(m):
                    if m in (0, 1):
                        need(pe, s_oA, at(prev(pair), 8, 7 + m) if pair[1] else 0)
                    elif m < 10:
                        pe.wait_ge(s_okD, at(pair, 8, m - 1))
                    else:
                        pe.wait_ge(s_oA, at(pair, 8, m - 9))

                pe.wait_ge(s_gD, at(pair, NGD, readers_before(6, "D")))
                sc_a = lambda c: scores(c, kT[:, c * P:(c + 1) * P], qbd[:, c, :, :])
                sc_a(0)
                for c in range(TT):
                    if c < TT - 1:
                        sc_a(c + 1)
                    out_free(c)
                    pe.wait_ge(s_mask, at(pair, 16, c + 1))
                    pe.wait_ge(s_gA, at(pair, NGA, readers_before(FIRST_USE["tr"] + c + 1, "A")))
                    if c:
                        pe.wait_ge(s_stc, at(pair, 14, c))
                    for h in range(2):
                        o = OUT[c % 2][:, h * 64:(h + 1) * 64]
                        last = mm(o, masked[:, c % 2, h * P:(h + 1) * P], ker[:, c, 1, h * 64:(h + 1) * 64],
                                  start=True, stop=c == 0)
                        if c:
                            last = mm(o, qbd[:, c, h, :], sk_sb[:, h * 64:(h + 1) * 64], start=False, stop=True)
                    last.then_inc(s_out, 1)
                    if c < TT - 1:
                        mm(ST_K[:, 0:P], ker[:, c, 0, :], ker[:, c, 1, :], start=c == 0, stop=True,
                           skip_group_check=True).then_inc(s_st, 1)

                pe.wait_ge(s_wvg, at(pair, 16, 16))
                for i in range(4):
                    n = FIRST_USE["v"] + i
                    g_free(pe, pair, n)
                    for c in range(2):
                        t = (2 * i + c) * P
                        for k in range(KD):
                            last = mm(G[n % 2][:, c * D:(c + 1) * D], xnT[:, k, t:t + P], wvg_sb[:, k, 0, :],
                                      start=k == 0, stop=k == KD - 1)
                    last.then_inc(s_gfull, 1)
                for i in range(4):
                    n = FIRST_USE["g"] + i
                    h, hf = i // 2, i % 2
                    g_free(pe, pair, n)
                    for k in range(KD):
                        last = mm(G[n % 2][:], wvg_sb[:, k, 1, h * P:(h + 1) * P], xnT[:, k, hf * HALF:(hf + 1) * HALF],
                                  start=k == 0, stop=k == KD - 1)
                    last.then_inc(s_gfull, 1)
                pe.wait_ge(s_pv, at(pair, 1, 1))
                for i in range(2):
                    n = FIRST_USE["pvT"] + i
                    g_free(pe, pair, n)
                    for c in range(4):
                        last = nc.tensor.transpose(G[n % 2][:, c * P:(c + 1) * P], pv[:, 4 * i + c, :], ident[:])
                    last.then_inc(s_gfull, 1)

                pe.wait_ge(s_gD, at(pair, NGD, readers_before(NG, "D")))
                sc_b = lambda c: scores(8 + c, eT[:, c * P:(c + 1) * P], pbd[:, c, :, :])
                sc_b(0)
                for c in range(TT):
                    if c < TT - 1:
                        sc_b(c + 1)
                    out_free(8 + c)
                    pe.wait_ge(s_mask, at(pair, 16, c + 9))
                    if c:
                        pe.wait_ge(s_stc, at(pair, 14, 7 + c))
                    for h in range(2):
                        o = OUT[c % 2][:, h * P:(h + 1) * P]
                        last = mm(o, masked[:, c % 2, h * P:(h + 1) * P], v_sb[:, c, h * P:(h + 1) * P],
                                  start=True, stop=c == 0)
                        if c:
                            last = mm(o, pbd[:, c, h, :], sv_sb[:, h * P:(h + 1) * P], start=False, stop=True)
                    last.then_inc(s_out, 1)
                    if c < TT - 1:
                        mm(ST_V[:, 0:D], ker[:, c, 1, :], v_sb[:, c, :], start=c == 0, stop=True,
                           skip_group_check=True).then_inc(s_st, 1)

            pair_body((0, 0))
            with pe.Fori(0, NP - 1) as j:
                pair_body((j, 1))
            output_product((0, NP))

            def experts(n, tokens, ready, count):
                u0, ne, f = expert_units(n)
                pe.wait_ge(ready, count)

                def gate_up(j, u, b, hf):
                    pe.wait_ge(s_h, j * 4 + (u0 + u + 1))
                    if hf == 0:
                        pe.wait_ge(s_wex[b], j * 16 + (u0 // 4 + u // 4 + 2) * 16)
                    q = (u % 2) * 2
                    for g in range(2):
                        for k in range(KD):
                            w = (g * KD + k) * f
                            last = mm(bank[q + g][0:f, :], wex[:, b, w:w + f], tokens[:, k, hf * HALF:(hf + 1) * HALF],
                                      start=k == 0, stop=k == KD - 1)
                    last.then_inc(s_gu, 1)

                def down(j, u, b):
                    pe.wait_ge(s_h, j * 4 + (u0 + u + 3))
                    pe.wait_ge(s_acc, j * 4 + (u0 + u + 1))
                    for c in range(4):
                        yb = bank[4 + (u % 2) * 2 + c // 2]
                        last = mm(yb[:, (c % 2) * D:(c % 2 + 1) * D], hT[0:f, u % 2, c * P:(c + 1) * P],
                                  wex[0:f, b, 4 * f:4 * f + D], start=True, stop=True)
                    last.then_inc(s_y, 1)

                gate_up(0, 0, 0, 0)
                def body(j, last):
                    for u in range(4):
                        if u < 3:
                            gate_up(j, u + 1, (u + 1) // 2, (u + 1) % 2)
                        elif not last:
                            gate_up(j, 4, 0, 0)
                        down(j, u, u // 2)
                with pe.Fori(0, ne // 2 - 1) as j:
                    body(j, False)
                body(ne // 2 - 1, True)

            experts(0, xnT, s_att, 1)

            transposed_tokens(1)
            logits(1, gate1_sb, E1)
            for c in range(TT):
                b0, b1 = (0, 1) if c % 2 == 0 else (2, 3)
                if c >= 2:
                    pe.wait_ge(s_qkve, c - 1)
                for k in range(KD):
                    mm(bank[b0][:], xnT[:, k, c * P:(c + 1) * P], wqkv_sb[:, k, 0:512], start=k == 0, stop=k == KD - 1)
                for k in range(KD):
                    last = mm(bank[b1][:, 0:D], xnT[:, k, c * P:(c + 1) * P], wqkv_sb[:, k, 512:768],
                              start=k == 0, stop=k == KD - 1)
                last.then_inc(s_qkv, 1)
            for i, (src, made) in enumerate(((thq, s_thw), (wk, s_thw), (wv, s_wvv))):
                pe.wait_ge(made, (8, 16, 1)[i])
                if i == 0:
                    pe.wait_ge(s_qkve, TT)
                for q in range(4):
                    n = 4 * i + q
                    if n >= 4:
                        pe.wait_ge(s_t3e, n - 3)
                    for k in range(KD):
                        for c in range(2):
                            o = (k * 2 + c) * P
                            last = nc.tensor.transpose(bank[n % 4][:, o:o + P], src[:, 2 * q + c, k * P:(k + 1) * P], ident[:])
                    last.then_inc(s_t3, 1)
            pe.wait_ge(s_t3e, 12)
            experts(1, xnT, s_comb, 2)
            experts(2, yT, s_yT, 1)

        @block.scalar
        def _(act):
            A = nc.scalar.activation

            def transposed_tokens(n):
                for i in range(4):
                    act.wait_ge(s_xT, 4 * n + i + 1)
                    nc.scalar.copy(xnT[:, :, 2 * i * P:(2 * i + 2) * P].rearrange("p k (c t) -> p k c t", c=2),
                                   bank[i][:].rearrange("p (c k t) -> p k c t", c=2, k=KD)).then_inc(s_xTe, 1)

            transposed_tokens(0)
            act.wait_ge(s_sh, 1)
            A(prob[:], left[:], ACT.Exp).then_inc(s_ex, 1)

            def pair_body(pair):
                act.wait_ge(s_gD, at(pair, NGD, 2))
                A(eT[:], sclip[:], ACT.Exp).then_inc(s_e, 1)
                for hf in range(2):
                    act.wait_ge(s_gfull, at(pair, NG, 3 + hf))
                    nc.scalar.copy(kT[:, hf * HALF:(hf + 1) * HALF], G[hf][:]).then_inc(s_gA, 1)

                def state(m, dst, src):
                    act.wait_ge(s_st, at(pair, 14, m + 1))
                    nc.scalar.copy(dst, src).then_inc(s_stc, 1)

                for c in range(TT):
                    n = FIRST_USE["tr"] + c
                    act.wait_ge(s_gfull, at(pair, NG, n + 1))
                    nc.scalar.copy(ker[:, c, :, :], G[n % 2][:, 0:3 * P].rearrange("p (a b) -> p a b", a=3)).then_inc(s_gA, 1)
                for c in range(TT - 1):
                    state(c, sk_sb[:], ST_K[:, 0:P])
                for i in range(4):
                    n = FIRST_USE["v"] + i
                    act.wait_ge(s_gfull, at(pair, NG, n + 1))
                    nc.scalar.copy(v_sb[:, 2 * i:2 * i + 2, :], G[n % 2][:].rearrange("p (a b) -> p a b", a=2)).then_inc(s_gA, 1)
                act.wait_ge(s_sub, at(pair, 1, 1))
                A(pv[:], ok[:], ACT.Exp).then_inc(s_pv, 1)
                for i in range(4):
                    n = FIRST_USE["g"] + i
                    act.wait_ge(s_gfull, at(pair, NG, n + 1))
                    if i >= 2:
                        act.wait_ge(s_gD, at(pair, NGD, readers_before(n - 1, "D")))
                    A(th[:, i % 2, :], G[n % 2][:], ACT.Tanh, scale=0.5).then_inc(s_th, 1)
                for c in range(TT):
                    m = 8 + c
                    act.wait_ge(s_out, at(pair, 16, m + 1))
                    nc.scalar.copy(o_sb[:, c, :], OUT[m % 2][:, 0:D]).then_inc(s_oA, 1)
                    if c < TT - 1:
                        state(7 + c, sv_sb[:], ST_V[:, 0:D])

            pair_body((0, 0))
            with act.Fori(0, NP - 1) as j:
                pair_body((j, 1))

            def experts(n):
                u0, ne, f = expert_units(n)
                with act.Fori(0, ne // 2) as j:
                    for u in range(4):
                        act.wait_ge(s_gu, j * 4 + (u0 + u + 1))
                        act.wait_ge(s_h, j * 4 + (u0 + u + 1))
                        A(sil[0:f, u % 2, :], bank[(u % 2) * 2][0:f, :], ACT.Silu).then_inc(s_sil, 1)

            experts(0)
            transposed_tokens(1)
            act.wait_ge(s_lg, 2)
            A(prob[:, :, 0:E1], bank[4][:, 0:TT * E1].rearrange("p (c e) -> p c e", c=TT), ACT.Sigmoid).then_inc(s_ex, 1)
            for c in range(TT):
                b0, b1 = (0, 1) if c % 2 == 0 else (2, 3)
                act.wait_ge(s_qkv, c + 1)
                if c == 0:
                    act.wait_ge(s_rstd, 3)
                A(qkv[:, c, 0:512], bank[b0][:], ACT.Copy, scale=rstd[:, c:c + 1])
                A(qkv[:, c, 512:768], bank[b1][:, 0:D], ACT.Copy, scale=rstd[:, c:c + 1]).then_inc(s_qkve, 1)
            act.wait_ge(s_rqk, 1)
            for c in range(TT):
                A(thq[:, c, :], qkv[:, c, 0:D], ACT.Tanh, scale=rs[:, c:c + 1]).then_inc(s_thw, 1)
            for c in range(TT):
                A(wk[:, c, :], qkv[:, c, D:2 * D], ACT.Exp, scale=rs[:, TT + c:TT + c + 1]).then_inc(s_thw, 1)
            for i, dst in enumerate((thT, wcT, kvT)):
                for q in range(4):
                    n = 4 * i + q
                    act.wait_ge(s_t3, n + 1)
                    nc.scalar.copy(dst[:, :, 2 * q * P:(2 * q + 2) * P],
                                   bank[n % 4][:].rearrange("p (k t) -> p k t", k=KD)).then_inc(s_t3e, 1)
            experts(1)
            experts(2)

        @block.vector
        def _(dve):
            V = nc.vector
            links = {"base": 0, "n": 0}

            def link(ins):
                links["n"] += 1
                ins.then_inc(s_dve, 1)
                dve.wait_ge(s_dve, links["base"] + links["n"])

            def layernorm(n):
                for c in range(TT):
                    last = V.bn_stats(stats[:, c, :], acc[:, c, :])
                link(last)
                for c in range(TT):
                    last = V.bn_aggr(mv[:, c, :], stats[:, c, :])
                link(last)
                V.tensor_scalar(veps[:], mv[:, :, 1], EPS_LN, None, ALU.add).then_inc(s_var, 1)
                dve.wait_ge(s_rstd, n + 1)
                for c in range(TT):
                    V.tensor_scalar(xn[:, c, :], acc[:, c, :], mv[:, c, 0:1], rstd[:, c:c + 1],
                                    ALU.subtract, ALU.mult).then_inc(s_xn, 1)

            dve.wait_ge(s_x, 16)
            layernorm(0)

            dve.wait_ge(s_lg, 1)
            lg = bank[4][:].rearrange("p (c e) -> p c e", c=TT)
            link(V.tensor_reduce(rmax[:], lg, AX, ALU.max))
            V.tensor_tensor(left[:], lg, rmax[:].unsqueeze(2).broadcast_to([P, TT, E0]), ALU.subtract).then_inc(s_sh, 1)
            dve.wait_ge(s_ex, 1)
            link(V.tensor_reduce(rsum[:], prob[:], AX, ALU.add))
            link(V.reciprocal(rsum[:], rsum[:]))
            link(V.tensor_tensor(prob[:], prob[:], rsum[:].unsqueeze(2).broadcast_to([P, TT, E0]), ALU.mult))
            for c in range(TT):
                last = V.max(top[:, c, :], prob[:, c, :])
            link(last)
            for c in range(TT):
                last = V.match_replace(left[:, c, :], top[:, c, :], prob[:, c, :], 0.0)
            link(last)
            V.tensor_tensor(comb0[:], prob[:], left[:], ALU.subtract).then_inc(s_comb, 1)
            dve.wait_ge(s_c, 6)

            def gate_and_add(pair):
                for i in range(4):
                    n = first_of("oT", pair) + i
                    dve.wait_ge(s_gfull, at(pair, NG, n + 1))
                    t = 2 * i * P
                    V.tensor_tensor(oT[:, :, t:t + 2 * P], G[n % 2][:].rearrange("p (h t) -> p h t", h=2),
                                    gT[:, :, t:t + 2 * P], ALU.mult).then_inc(s_gD, 1)
                for i in range(4):
                    n = first_of("wo", pair) + i
                    dve.wait_ge(s_gfull, at(pair, NG, n + 1))
                    a = acc[:, 2 * i:2 * i + 2, :]
                    last = V.tensor_tensor(a, a, G[n % 2][:].rearrange("p (c d) -> p c d", c=2), ALU.add)
                    last.then_inc(s_gD, 1)

            def pair_body(pair):
                for hf in range(2):
                    dve.wait_ge(s_gfull, at(pair, NG, hf + 1))
                    V.tensor_scalar(sclip[:, hf * HALF:(hf + 1) * HALF], G[hf][:], 32.0, -32.0,
                                    ALU.min, ALU.max).then_inc(s_gD, 1)
                for hf in range(2):
                    dve.wait_ge(s_gfull, at(pair, NG, 5 + hf))
                    for h in range(2):
                        r = slice(64 * h, 64 * h + 64)
                        last = V.tensor_scalar(qbd[r, 4 * hf:4 * hf + 4, h, :],
                                               G[hf][r, :].rearrange("p (c t) -> p c t", c=4), 0.125, None, ALU.mult)
                    last.then_inc(s_gD, 1)
                dve.wait_ge(s_e, at(pair, 1, 1))
                link(V.tensor_tensor_scan(zT[:], ones[:], eT[:], 0.0, ALU.mult, ALU.add))
                V.reciprocal(rT[:], zT[:]).then_inc(s_rT, 1)
                if pair[1] == 0:
                    for n in range(FIRST_USE["oT"], FIRST_USE["tr"]):
                        dve.wait_ge(s_gfull, at(pair, NG, n + 1))
                        V.tensor_copy(mx[:, n:n + 1], G[n % 2][:, 0:1]).then_inc(s_gD, 1)
                else:
                    gate_and_add(pair)

                def mask(m):
                    dve.wait_ge(s_sc, at(pair, 16, m + 1))
                    if m >= 2:
                        dve.wait_ge(s_out, at(pair, 16, m - 1))
                    V.tensor_tensor(masked[:, m % 2, :], SC[m % 2][:, 0:2 * P],
                                    causal[:].rearrange("p a b -> p (a b)"), ALU.mult).then_inc(s_mask, 1)

                mask(0)
                for c in range(TT):
                    if c < TT - 1:
                        mask(c + 1)
                    dve.wait_ge(s_out, at(pair, 16, c + 1))
                    last = V.tensor_tensor(ok[:, c, :], OUT[c % 2][:, 0:P], ker[:, c, 2, :], ALU.mult)
                    last.then_inc(s_okD, 1)
                dve.wait_ge(s_okD, at(pair, 8, 8))
                slots = ok[:].rearrange("p c (h m) -> p (c h) m", h=2)
                link(V.tensor_reduce(mx[:], slots, AX, ALU.max))
                V.tensor_tensor(slots, slots, mx[:].unsqueeze(2).broadcast_to([P, 16, 64]), ALU.subtract).then_inc(s_sub, 1)
                dve.wait_ge(s_pv, at(pair, 1, 1))
                link(V.tensor_reduce(sm[:], pv[:].rearrange("p c (h m) -> p (c h) m", h=2), AX, ALU.add))
                link(V.reciprocal(rs[:], sm[:]))
                for i in range(4):
                    h, hf = i // 2, i % 2
                    dve.wait_ge(s_th, at(pair, 4, i + 1))
                    V.scalar_tensor_tensor(gT[:, h, hf * HALF:(hf + 1) * HALF], th[:, i % 2, :], 1.0,
                                           G[(FIRST_USE["g"] + i) % 2][:], ALU.add, ALU.mult).then_inc(s_gD, 1)
                for i in range(2):
                    n = FIRST_USE["pvT"] + i
                    dve.wait_ge(s_gfull, at(pair, NG, n + 1))
                    for h in range(2):
                        r = slice(64 * h, 64 * h + 64)
                        last = V.tensor_tensor(pbd[r, 4 * i:4 * i + 4, h, :],
                                               G[n % 2][r, :].rearrange("p (c t) -> p c t", c=4),
                                               rT[r, i * HALF:(i + 1) * HALF].rearrange("p (c t) -> p c t", c=4), ALU.mult)
                    last.then_inc(s_gD, 1)
                for c in range(TT):
                    mask(8 + c)
                dve.wait_ge(s_sq, at(pair, 1, 1))
                link(V.tensor_reduce(ss[:], o_sq[:].rearrange("p c (h v) -> p (c h) v", h=2), AX, ALU.add))
                link(V.tensor_tensor(ss[:], ss[:], rs[:], ALU.mult))
                link(V.tensor_tensor(ss[:], ss[:], rs[:], ALU.mult))
                V.tensor_scalar(ss[:], ss[:], 1.0 / 128, EPS_O, ALU.mult, ALU.add).then_inc(s_ms, 1)
                dve.wait_ge(s_pw, at(pair, 1, 1))
                link(V.tensor_tensor(sc16[:], pw[:], rs[:], ALU.mult))
                V.tensor_tensor(o_n[:].rearrange("p c (h v) -> p (c h) v", h=2),
                                o_sb[:].rearrange("p c (h v) -> p (c h) v", h=2),
                                sc16[:].unsqueeze(2).broadcast_to([P, 16, P]), ALU.mult).then_inc(s_on, 1)

            before = links["n"]
            pair_body((0, 0))
            per = links["n"] - before
            with dve.Fori(0, NP - 1) as j:
                links["base"], links["n"] = j * per + (before + per), 0
                pair_body((j, 1))
            links["base"], links["n"] = 0, before + NP * per
            gate_and_add((0, NP))
            dve.wait_ge(s_gD, NP * NGD + 8)
            dve.sem_inc(s_h, 2)
            dve.sem_inc(s_acc, 2)
            dve.sem_inc(s_att, 1)

            def experts(n, comb):
                u0, ne, f = expert_units(n)
                with dve.Fori(0, ne // 2) as j:
                    for u in range(4):
                        dve.wait_ge(s_sil, j * 4 + (u0 + u + 1))
                        dve.wait_ge(s_y, j * 4 + (u0 + u + 2))
                        V.tensor_tensor(hT[0:f, u % 2, :], sil[0:f, u % 2, :], bank[(u % 2) * 2 + 1][0:f, :],
                                        ALU.mult).then_inc(s_h, 1)
                        dve.wait_ge(s_y, j * 4 + (u0 + u + 4))
                        dve.wait_ge(s_acc, j * 4 + (u0 + u + 1))
                        for c in range(4):
                            yb = bank[4 + (u % 2) * 2 + c // 2][:, (c % 2) * D:(c % 2 + 1) * D]
                            t = (u % 2) * 4 + c
                            if comb is not None:
                                last = V.scalar_tensor_tensor(acc[:, t, :], yb, comb[:, t, bass.ds(j * 2 + u // 2, 1)],
                                                              acc[:, t, :], ALU.mult, ALU.add)
                            else:
                                last = V.tensor_tensor(acc[:, t, :], acc[:, t, :], yb, ALU.add)
                        last.then_inc(s_acc, 1)

            experts(0, comb0)
            dve.wait_ge(s_acc, 2 + 2 * E0)
            layernorm(1)
            dve.wait_ge(s_xn, 2 * TT)
            for c in range(TT):
                last = V.tensor_tensor_reduce(out=o_sq[:, c, :], in0=xn[:, c, :], in1=xn[:, c, :], scale=1.0, scalar=0.0,
                                              op0=ALU.mult, op1=ALU.add, accum_out=ss[:, c:c + 1])
            link(last)
            V.tensor_scalar(veps[:], ss[:, 0:TT], 1.0 / D, EPS_RMS, ALU.mult, ALU.add).then_inc(s_var, 1)
            link(V.tensor_tensor(acc[:], acc[:], xn[:], ALU.add))

            dve.wait_ge(s_ex, 2)
            V.memset(prob[:, :, E1:E1 + 2], -1.0)
            for c in range(TT):
                last = V.max(top[:, c, :], prob[:, c, 0:E1])
            link(last)
            link(V.memset(top[:, :, TOP1:8], -1.0))
            for c in range(TT):
                last = V.match_replace(left[:, c, 0:E1 + 2], top[:, c, :], prob[:, c, 0:E1 + 2], 0.0)
            link(last)
            link(V.tensor_tensor(comb1[:], prob[:, :, 0:E1 + 2], left[:, :, 0:E1 + 2], ALU.subtract))
            link(V.tensor_reduce(rsum[:], comb1[:, :, 0:E1], AX, ALU.add))
            link(V.tensor_scalar(rsum[:], rsum[:], 1e-20, None, ALU.add))
            link(V.reciprocal(rsum[:], rsum[:]))
            link(V.tensor_tensor(comb1[:, :, 0:E1], comb1[:, :, 0:E1],
                                 rsum[:].unsqueeze(2).broadcast_to([P, TT, E1]), ALU.mult))
            V.memset(comb1[:, :, E1:E1 + SH], 1.0).then_inc(s_comb, 1)

            dve.wait_ge(s_qsq, 2)
            for i, src in enumerate((o_sb, o_sq)):
                last = V.tensor_reduce(ss[:, 8 * i:8 * i + 8],
                                       src[:].rearrange("p a d -> p (a d)").rearrange("p (n d) -> p n d", d=D), AX, ALU.add)
            link(last)
            V.tensor_scalar(ss[:], ss[:], 1.0 / D, EPS_RMS, ALU.mult, ALU.add).then_inc(s_qms, 1)
            dve.wait_ge(s_qpw, 1)
            pqk = pw[:].rearrange("p (c a) -> p a c", a=2)
            V.tensor_scalar(rs[:, 0:TT], pqk[:, 0, :], 0.5, None, ALU.mult)
            V.tensor_copy(rs[:, TT:2 * TT], pqk[:, 1, :]).then_inc(s_rqk, 1)
            dve.wait_ge(s_thw, 2 * TT)
            V.tensor_tensor(wv[:], wk[:], qkv[:, :, 2 * D:3 * D], ALU.mult).then_inc(s_wvv, 1)
            for k in range(KD):
                dve.wait_ge(s_t3e, 8)
                V.tensor_tensor_scan(wcum[:, k, :], ones[:], wcT[:, k, :], 0.0, ALU.mult, ALU.add)
            for k in range(KD):
                dve.wait_ge(s_t3e, 12)
                last = V.tensor_tensor_scan(kvcum[:, k, :], ones[:], kvT[:, k, :], 0.0, ALU.mult, ALU.add)
            link(last)
            link(V.tensor_scalar(wcum, wcum, 1e-6, 2.0, ALU.add, ALU.mult))
            link(V.reciprocal(wcum, wcum))
            link(V.tensor_tensor(kvcum, kvcum, wcum, ALU.mult))
            V.scalar_tensor_tensor(yT, thT[:], 1.0, kvcum, ALU.add, ALU.mult).then_inc(s_yT, 1)
            experts(1, comb1)
            experts(2, None)


def kernel(**inputs):
    import numpy as np
    import concourse.bacc as bacc
    from concourse.bass_utils import run_bass_kernel_spmd

    a = {k: np.asarray(v) for k, v in inputs.items()}

    def by_k(w):
        return w.reshape(KD, P, -1).transpose(1, 0, 2)

    def by_pair(w):
        return w.reshape(KD, P, NP, -1).transpose(2, 1, 0, 3)

    def by_expert(gate, up, down):
        e, _, f = gate.shape
        row = [w.reshape(e, KD, P, f).transpose(0, 2, 1, 3).reshape(e, P, KD * f) for w in (gate, up)]
        low = np.zeros((e, P, D), down.dtype)
        low[:, :f] = down
        return np.concatenate([*row, low], axis=2)

    w13 = a["L0_ffn_w13"]
    swi = a["L1_attn_w_swiglu"]
    ff = swi.shape[0] // 2
    sg, su, sd = (a[f"L1_ffn_{n}"] for n in ("sg", "su", "sd"))
    shared = [w.reshape(D, SH, F1).transpose(1, 0, 2) for w in (sg, su)]
    arrays = {
        "x": a["L0_attn_hidden_states"].reshape(T, D),
        "wqks": np.stack([by_pair(a[f"L0_attn_{n}"]) for n in ("Ws", "Wk", "Wq")], axis=2),
        "wvg": np.stack([by_pair(a["L0_attn_Wv"]), by_pair(a["L0_attn_Wg"])], axis=3),
        "wo": a["L0_attn_Wo"].reshape(NP, 2, P, D).transpose(0, 2, 1, 3),
        "gnw": a["L0_attn_g_norm_weight"].reshape(P, 1),
        "gate0": by_k(a["L0_ffn_gate_w"].T),
        "w0": by_expert(w13[:, :F0].transpose(0, 2, 1), w13[:, F0:].transpose(0, 2, 1), a["L0_ffn_w2"].transpose(0, 2, 1)),
        "wqkv": by_k(a["L1_attn_w_qkv"].T),
        "wsw": by_expert(swi[ff:].reshape(ESW, P, D).transpose(0, 2, 1), swi[:ff].reshape(ESW, P, D).transpose(0, 2, 1),
                         a["L1_attn_w_out"].T.reshape(ESW, P, D)),
        "gate1": by_k(a["L1_ffn_gate_w"]),
        "w1": by_expert(*(np.concatenate([w, s]) for w, s in (
            (a["L1_ffn_wg"], shared[0]), (a["L1_ffn_wu"], shared[1]), (a["L1_ffn_wd"], sd.reshape(SH, F1, D))))),
    }
    nc = bacc.Bacc("TRN2", target_bir_lowering=False, num_devices=1)
    args, given = [], {}
    for name, array in arrays.items():
        given[f"in_{name}"] = np.ascontiguousarray(array)
        args.append(nc.dram_tensor(f"in_{name}", array.shape, mybir.dt.from_np(array.dtype), kind="ExternalInput").ap())
    args.append(nc.dram_tensor("result", (T, D), F32, kind="ExternalOutput").ap())
    build(nc, *args)
    r = run_bass_kernel_spmd(nc, [given], core_ids=[0])
    return r.results[0]["result"].reshape(1, T, D)
```

```python
from contextlib import ExitStack

import concourse.bass as bass
from concourse import mybir

F32, F32R, I32 = mybir.dt.float32, mybir.dt.float32r, mybir.dt.int32
ALU = mybir.AluOpType
ACT = mybir.ActivationFunctionType
AX = mybir.AxisListType.X

P = 128
T, D = 1024, 256
TT = T // P
KD = D // P
NP = 8
HALF = T // 2
EPS_LN, EPS_O, EPS_RMS = 1e-5, 1e-5, 1.1920929e-07
E0, TOP0, F0 = 64, 8, 128
E1, TOP1, F1, SH = 32, 6, 96, 2
ESW = 8
WROW = 4 * P + D

CAP, HC = 192, 96
JUNK = E0 * CAP
LISTED = JUNK + T * TOP0
STEPS = 16
EXPERT_PAIRS = E0 // STEPS
EP = E0 + 4
IDX = 2 * (E0 + 6)
RING = 4

USES = [("tr", 8, "A"), ("v", 4, "A"), ("s", 2, "D"), ("k", 2, "A"), ("q", 2, "D"), ("pvT", 2, "D"),
        ("oT", 4, "D"), ("wo", 4, "D"), ("g", 4, "D")]
LAST_USES = [("tr", 8, "A"), ("v", 4, "A"), ("pvT", 2, "D"), ("oT", 4, "D"), ("wo", 4, "D"), ("g", 4, "D"),
             ("oT_end", 4, "D"), ("wo_end", 4, "D")]


def laid_out(uses):
    first, taken_by = {}, []
    for name, n, who in uses:
        first[name] = len(taken_by)
        taken_by += [who] * n
    return first, taken_by


FIRST_USE, TAKEN_BY = laid_out(USES)
LAST_FIRST, LAST_TAKEN_BY = laid_out(LAST_USES)
NG, NGD, NGA = len(TAKEN_BY), TAKEN_BY.count("D"), TAKEN_BY.count("A")
PRO, PRO_D, PRO_A = 6, 4, 2


class Pair:

    def __init__(self, j, off, experts=False, combine=False):
        self.j, self.off, self.experts, self.combine = j, off, experts, combine
        self.first = isinstance(j, int) and off == 0
        self.last = isinstance(j, int) and off == NP - 1

    def at(self, per, k):
        v = self.off * per + k
        return v if isinstance(self.j, int) else self.j * per + v

    def use(self, name, i=0):
        return (LAST_FIRST if self.last else FIRST_USE)[name] + i

    def full(self, n):
        return self.at(NG, PRO + n + 1)

    def taken(self, n):
        taken_by = LAST_TAKEN_BY if self.last else TAKEN_BY
        who = taken_by[n]
        k = taken_by[:n + 1].count(who)
        return (who, self.at(NGD, PRO_D + k)) if who == "D" else (who, self.at(NGA, PRO_A + k))


def need(eng, sem, value):
    if isinstance(value, int) and value <= 0:
        return
    eng.wait_ge(sem, value)


class Dense:

    def __init__(self, sem, name):
        self.w = [sem(f"{name}_w0"), sem(f"{name}_w1")]
        self.gu, self.sil, self.h, self.y, self.acc, self.hi, self.lo, self.tok_hi, self.tok_lo, self.made = (
            sem(f"{name}_{n}") for n in ("gu", "sil", "h", "y", "acc", "hi", "lo", "tok_hi", "tok_lo", "made"))


def build(nc, x, wqks, wvg, wo, gnw, gate0, w0, wqkv, wsw, gate1, w1, out):
    listed = nc.dram_tensor("listed", (LISTED, 1), I32, kind="Internal").ap()
    xn_rows = nc.dram_tensor("xn_rows", (T, D), F32, kind="Internal").ap()
    y_rows = nc.dram_tensor("y_rows", (JUNK + 1, D), F32, kind="Internal").ap()
    ctx = ExitStack()
    with ctx:
        def sb(name, *shape, dt=F32, stack=ctx):
            return stack.enter_context(nc.sbuf_tensor(name, [P, *shape], dt))

        def sem(name):
            return ctx.enter_context(nc.semaphore(name))

        bank = [ctx.enter_context(nc.psum_tensor(f"bank{i}", [P, 512], F32)) for i in range(8)]
        G = bank[0:2]
        SC, OUT, ST = bank[2], bank[3], bank[4]
        XT, GU, YB = bank[5], bank[6], bank[7]

        ident = sb("ident", P)
        causal = sb("causal", 2, P)
        before_t = sb("before_t", P)
        ones = sb("ones", T)
        neg_half = sb("neg_half", 16)
        slot_of = sb("slot_of", E0)
        token_id = sb("token_id", TT, dt=I32)
        junk_of = sb("junk_of", TT, 8)
        zero_i = sb("zero_i", JUNK // P, dt=I32)
        acc = sb("acc", TT, D)
        xn = sb("xn", TT, D)
        xnT = sb("xnT", KD, T)
        stats = sb("stats", TT, 6)
        mv = sb("mv", TT, 2)
        veps = sb("veps", TT)
        rstd = sb("rstd", TT)
        gate0_sb = sb("gate0_sb", KD, E0)
        gate1_sb = sb("gate1_sb", KD, E1)
        comb0 = sb("comb0", TT, E0)
        over0 = sb("over0", TT, E0)
        prob = sb("prob", TT, E0)
        left = sb("left", TT, E0)
        chosen = sb("chosen", TT, E0)
        fits = sb("fits", TT, E0)
        top = sb("top", TT, 8)
        w8 = sb("w8", TT, 8)
        slot_i = sb("slot_i", TT, 8, dt=I32)
        row_i = sb("row_i", TT, 8, dt=I32)
        rmax = sb("rmax", TT)
        rsum = sb("rsum", TT)
        over_p = sb("over_p", 1)
        over_i = sb("over_i", 1, dt=I32)
        list_i = sb("list_i", HC, dt=I32)
        list_f = sb("list_f", HC)
        idx = sb("idx", IDX, dt=I32)
        stage = sb("stage", 32, dt=I32)
        wqks_sb = sb("wqks_sb", 3, KD, P)
        wvg_sb = sb("wvg_sb", KD, 2, D)
        wo_raw = sb("wo_raw", 2, D)
        wo_sb = sb("wo_sb", 2, D)
        gnw_sb = sb("gnw_sb", 1)
        sclip = sb("sclip", T)
        kT = sb("kT", T)
        qbd = sb("qbd", TT, 2, P)
        pbd = sb("pbd", TT, 2, P)
        ker = sb("ker", TT, 3, P)
        th = sb("th", 2, HALF)
        masked = sb("masked", 2, 2 * P)
        sk_sb = sb("sk_sb", P)
        sv_sb = sb("sv_sb", D)
        mx = sb("mx", 16)
        sm = sb("sm", 16)
        rs = sb("rs", 16)
        ss = sb("ss", 16)
        pw = sb("pw", 16)
        sc16 = sb("sc16", 16)
        o_n = sb("o_n", TT, D)
        wex = sb("wex", RING, WROW)
        xg = sb("xg", RING, 2, D)
        xgT = sb("xgT", 2, KD, CAP)
        sil_s = sb("sil_s", 2, CAP)
        hT_s = sb("hT_s", 2, CAP)
        yg = sb("yg", 2, 8, D)
        first_use = ExitStack()
        eT = sb("eT", T, stack=first_use)
        eTb = sb("eTb", T, stack=first_use)
        zT = sb("zT", T, stack=first_use)
        rT = sb("rT", T, stack=first_use)
        v_sb = sb("v_sb", TT, D, stack=first_use)
        o_sb = sb("o_sb", TT, D, stack=first_use)
        y_sb = sb("y_sb", 2, 2, D, stack=first_use)
        ok = sb("ok", TT, P, stack=first_use)
        gT = sb("gT", 2, T, stack=first_use)
        oT = sb("oT", 2, T, stack=first_use)
        first_use.close()
        w_hi, w_lo = ([sb(f"w_{part}{b}", T, dt=F32R)[:] for b in range(2)] for part in ("hi", "lo"))
        x_hi, x_lo = (sb(f"x_{part}", KD, T, dt=F32R)[:] for part in ("hi", "lo"))
        h_hi, h_lo = (sb(f"h_{part}", 2, HALF, dt=F32R)[:] for part in ("hi", "lo"))
        y_hi, y_lo = (sb(f"y_{part}", KD, T, dt=F32R)[:] for part in ("hi", "lo"))
        o_sq = v_sb
        pv = ok
        comb1 = chosen[:, :, 0:E1 + SH]
        sil = th
        qkv_qk = yg[:].rearrange("p a b d -> p (a b d)").rearrange("p (c n) -> p c n", c=TT)
        qkv_v = xg[:].rearrange("p a b d -> p (a b) d")
        wqkv_sb = wex[:, 2:4, :].rearrange("p a n -> p (a n)")
        wqkv_v = wqkv_sb.rearrange("p (k n) -> p k n", k=KD)
        thq, thT, wcT = v_sb, gT, oT
        h_f32 = kT[:].rearrange("p (a t) -> p a t", a=2)
        wk, wv = o_sb, o_n
        kvT = qbd[:].rearrange("p (k c) h t -> p k (c h t)", k=KD)
        wcum = pbd[:].rearrange("p (k c) h t -> p k (c h t)", k=KD)
        kvcum = ker[:].rearrange("p c a t -> p (c a t)")[:, 0:KD * T].rearrange("p (k t) -> p k t", k=KD)
        yT = kvcum

        names = """s_x s_c s_pool s_dve s_var s_rstd s_xn s_xT s_xTe s_lg s_sh s_ex s_comb s_gw s_wqks s_wvg s_wo s_wos
            s_gfull s_gD s_gA s_e s_eb s_rT s_sc s_mask s_out s_okD s_oA s_st s_stc s_sub s_pv s_th s_sq s_ms s_pw s_on
            s_att s_chosen s_rank s_slot s_xnd s_zero s_scat s_listed s_listf s_lT s_idx s_flag s_flagi
            s_T s_Te s_gus s_sl s_hs s_ys s_ye s_cadd s_w8
            s_qkv s_qkve s_qsq s_qms s_qpw s_thw s_wvv s_t3 s_t3e s_yT s_rqk s_done s_gates s_tick""".split()
        (s_x, s_c, s_pool, s_dve, s_var, s_rstd, s_xn, s_xT, s_xTe, s_lg, s_sh, s_ex, s_comb, s_gw, s_wqks, s_wvg, s_wo,
         s_wos, s_gfull, s_gD, s_gA, s_e, s_eb, s_rT, s_sc, s_mask, s_out, s_okD, s_oA, s_st, s_stc, s_sub, s_pv, s_th,
         s_sq, s_ms, s_pw, s_on, s_att, s_chosen, s_rank, s_slot, s_xnd, s_zero, s_scat, s_listed, s_listf, s_lT, s_idx,
         s_flag, s_flagi, s_T, s_Te, s_gus, s_sl, s_hs, s_ys, s_ye, s_cadd, s_w8,
         s_qkv, s_qkve, s_qsq, s_qms, s_qpw, s_thw, s_wvv, s_t3, s_t3e, s_yT, s_rqk, s_done, s_gates, s_tick) = map(sem, names)
        s_we = [sem(f"s_we{i}") for i in range(RING)]
        s_xg = [sem(f"s_xg{i}") for i in range(RING)]
        s_yst = [sem(f"s_yst{i}") for i in range(2)]
        s_yg = [sem(f"s_yg{i}") for i in range(2)]
        fall, dense = Dense(sem, "fall"), Dense(sem, "dense")

        block = ctx.enter_context(nc.Block())

        def score_bank(pair, m):
            return SC if pair.experts or m % 2 == 0 else XT

        def pair_bodies(eng, body):
            with eng.Fori(0, EXPERT_PAIRS) as j:
                body(Pair(j, 1, experts=True))
            with eng.Fori(0, 2) as j:
                body(Pair(j, 1 + EXPERT_PAIRS, combine=True))
            body(Pair(0, NP - 1))

        @block.sync
        def _(sp):
            sp.dma_start(acc[:], x.rearrange("(c p) d -> p c d", p=P)).then_inc(s_x, 16)
            sp.dma_start(wqks_sb[:], wqks[0]).then_inc(s_wqks, 16)
            sp.dma_start(gate0_sb[:], gate0).then_inc(dense.w[0], 16)
            sp.dma_start(gnw_sb[:], gnw).then_inc(s_gw, 16)
            sp.dma_start(gate1_sb[:], gate1).then_inc(dense.w[1], 16)
            sp.wait_ge(s_c, 9)
            sp.dma_start(listed[0:JUNK, :].rearrange("(a b) o -> a (b o)", a=P), zero_i[:]).then_inc(s_zero, 16)
            sp.dma_start(y_rows[JUNK:JUNK + 1, :], pbd[0:1, 0, :, :].rearrange("p a b -> p (a b)")).then_inc(s_zero, 16)
            sp.wait_ge(s_xn, TT)
            sp.dma_start(xn_rows.rearrange("(c p) d -> p c d", p=P), xn[:]).then_inc(s_xnd, 16)
            for e in range(RING):
                sp.dma_start(wex[:, e, :], w0[e]).then_inc(s_we[e], 16)

            def body(pair):
                if not pair.last:
                    need(sp, s_gfull, pair.at(NG, PRO))
                    sp.wait_ge(s_wqks, pair.at(16, 16))
                    sp.dma_start(wqks_sb[:], wqks[pair.j + (pair.off + 1)]).then_inc(s_wqks, 16)
                if not pair.first:
                    if pair.last:
                        sp.wait_ge(s_gfull, pair.at(NG, PRO))
                    sp.wait_ge(s_wvg, pair.at(16, 0))
                sp.dma_start(wvg_sb[:], wvg[pair.j + pair.off]).then_inc(s_wvg, 16)
                if not pair.first:
                    sp.wait_ge(s_wos, pair.at(1, 0))
                    sp.wait_ge(s_wo, pair.at(16, 0))
                sp.dma_start(wo_raw[:], wo[pair.j + pair.off]).then_inc(s_wo, 16)
                if pair.experts:
                    j = pair.j
                    for s in range(STEPS):
                        sp.wait_ge(s_ye, j * STEPS + (s + 2))
                        rows = y_rows[bass.ds(j * (STEPS * CAP) + s * CAP, CAP), :]
                        sp.dma_start(rows.rearrange("(h p) d -> p h d", h=2), y_sb[0:HC, s % 2, :, :]).then_inc(s_yst[s % 2], 16)
                        sp.wait_ge(s_we[s % RING], j * 64 + (s // RING + 1) * 16)
                        sp.dma_start(wex[:, s % RING, :], w0[j * STEPS + (s + RING)]).then_inc(s_we[s % RING], 16)

            body(Pair(0, 0))
            sp.wait_ge(s_scat, 16 * TT * TOP0)
            sp.dma_start(list_i[:], listed[0:P * HC, :].rearrange("(r p) o -> r (p o)", p=HC)).then_inc(s_listed, 16)
            pair_bodies(sp, body)

            def dense_loads(dn, w, u0, ne, f):
                with sp.Fori(0, ne // 2) as j:
                    for b in range(2):
                        sp.wait_ge(dn.lo, j * 2 + (u0 // 2 + b + 1))
                        sp.wait_ge(dn.w[b], j * 16 + (u0 // 4 + 1) * 16)
                        sp.dma_start(wex[:, b, 0:4 * f + D], w[j * 2 + b]).then_inc(dn.w[b], 16)

            sp.wait_ge(s_ys, 1 + E0)
            for e in range(RING):
                sp.wait_ge(s_we[e], 16 * (EP // RING))
            sp.wait_ge(s_flagi, 1)
            over = sp.value_load(over_i[0:1, 0:1], min_val=0, max_val=1)
            with sp.If(over > 0):
                for b in range(2):
                    sp.dma_start(wex[:, b, :], w0[b]).then_inc(fall.w[b], 16)
                    sp.wait_ge(fall.w[b], 16)
                dense_loads(fall, w0, 0, E0, F0)
                sp.wait_ge(fall.acc, 2 + 2 * E0)
            sp.dma_start(wqkv_sb, wqkv.rearrange("p k n -> p (k n)")).then_inc(s_gw, 16)
            dense_loads(dense, w1, 0, E1 + SH, F1)
            dense_loads(dense, wsw, 2 * (E1 + SH), ESW, P)
            sp.wait_ge(dense.acc, 2 + 2 * (E1 + SH + ESW))
            sp.dma_start(out.rearrange("(c p) d -> p c d", p=P), acc[:]).then_inc(s_done, 16)
            sp.wait_ge(s_done, 16)

        @block.gpsimd
        def _(pool):
            g = nc.gpsimd
            g.memset(ident[:], 0.0).then_inc(s_pool, 1)
            g.memset(causal[:], 1.0).then_inc(s_pool, 1)
            g.memset(before_t[:], 1.0).then_inc(s_pool, 1)
            g.memset(idx[:], 0).then_inc(s_c, 1)
            g.memset(ones[:], 1.0).then_inc(s_c, 1)
            g.memset(neg_half[:], -0.5).then_inc(s_c, 1)
            g.memset(qbd[:], 0.0).then_inc(s_c, 1)
            g.memset(pbd[:], 0.0).then_inc(s_c, 1)
            g.memset(zero_i[:], 0).then_inc(s_c, 1)
            g.iota(token_id[:], pattern=[[P, TT]], base=0, channel_multiplier=1).then_inc(s_c, 1)
            g.iota(junk_of[:], pattern=[[1, TT * 8]], base=JUNK + 1, channel_multiplier=TT * 8,
                   allow_small_or_imprecise_dtypes=True).then_inc(s_c, 1)
            g.iota(slot_of[:], pattern=[[CAP, E0]], base=1, channel_multiplier=0,
                   allow_small_or_imprecise_dtypes=True).then_inc(s_c, 1)
            pool.wait_ge(s_pool, 3)
            g.affine_select(out=ident[:], in_=ident[:], compare_op=ALU.not_equal, fill=1.0, base=0,
                            pattern=[[-1, P]], channel_multiplier=1).then_inc(s_c, 1)
            g.affine_select(out=causal[:], in_=causal[:], compare_op=ALU.is_ge, fill=0.0, base=0,
                            pattern=[[0, 2], [1, P]], channel_multiplier=-1).then_inc(s_c, 1)
            g.affine_select(out=before_t[:], in_=before_t[:], compare_op=ALU.is_gt, fill=0.0, base=0,
                            pattern=[[1, P]], channel_multiplier=-1).then_inc(s_c, 1)
            pool.wait_ge(s_c, 12)

            def ln_power(n):
                pool.wait_ge(s_var, n + 1)
                g.tensor_tensor(rstd[:], veps[:], neg_half[:, 0:TT], ALU.pow).then_inc(s_rstd, 1)

            ln_power(0)
            pool.wait_ge(s_gw, 16)
            g.tensor_scalar(gnw_sb[:], gnw_sb[:], 0.5, None, ALU.mult).then_inc(s_gates, 1)
            pool.wait_ge(s_gates, 1)

            def squares(pair):
                pool.wait_ge(s_oA, pair.at(TT, 0))
                if not (isinstance(pair.j, int) and pair.off == 1):
                    need(pool, s_ms, pair.at(1, -1))
                g.tensor_tensor(o_sq[:], o_sb[:], o_sb[:], ALU.mult).then_inc(s_sq, 1)

            def power(pair):
                pool.wait_ge(s_ms, pair.at(1, 0))
                g.tensor_tensor(pw[:], ss[:], neg_half[:], ALU.pow).then_inc(s_pw, 1)

            def keep_e(pair):
                if not pair.first:
                    pool.wait_ge(s_sc, pair.at(16, 0))
                pool.wait_ge(s_e, pair.at(1, 1))
                pool.sem_inc(s_tick, 1)
                g.tensor_copy(eTb[:], eT[:]).then_inc(s_eb, 1)

            def scale_wo(pair):
                pool.wait_ge(s_gfull, pair.full(pair.use("wo", 3)))
                pool.wait_ge(s_wo, pair.at(16, 16))
                g.tensor_tensor(wo_sb[:], wo_raw[:], gnw_sb[:].unsqueeze(2).broadcast_to([P, 2, D]),
                                ALU.mult).then_inc(s_wos, 1)

            def gather_tokens(slot, col):
                for h in range(2):
                    g.indirect_dma_start(xg[0:HC, slot, h, :], None, xn_rows,
                                         bass.IndirectOffsetOnAxis(ap=stage[0:HC, col + h:col + h + 1], axis=0)
                                         ).then_inc(s_xg[slot], 16)

            def body(pair):
                keep_e(pair)
                if pair.first:
                    pool.wait_ge(s_zero, 32)
                    pool.wait_ge(s_slot, 1)
                    for c in range(TT):
                        for k in range(TOP0):
                            g.indirect_dma_start(listed, bass.IndirectOffsetOnAxis(ap=slot_i[:, c, k:k + 1], axis=0),
                                                 token_id[:, c:c + 1], None).then_inc(s_scat, 16)
                    scale_wo(pair)
                    return
                squares(pair)
                if pair.experts:
                    j = pair.j
                    for slot in range(RING):
                        pool.wait_ge(s_xg[slot], j * 128 + (64 if slot == 0 else 32))
                    pool.sem_inc(s_tick, 1)
                    g.tensor_copy(stage[:], idx[:, bass.ds(j * 32 + 2 * (RING + 1), 32)]).then_inc(s_idx, 1)
                    pool.wait_ge(s_idx, j + 3)
                for s in range(STEPS):
                    if pair.experts:
                        slot = (s + 1) % RING
                        pool.wait_ge(s_T, pair.j * STEPS + (s + 2))
                        pool.sem_inc(s_tick, 1)
                        gather_tokens(slot, 2 * s)
                    if s == TT - 1:
                        power(pair)
                scale_wo(pair)

            def combine_body(pair):
                j = pair.j
                keep_e(pair)
                squares(pair)
                pool.wait_ge(s_cadd, j * 32 + 1)
                pool.sem_inc(s_tick, 1)
                g.tensor_copy(stage[:].rearrange("p (a b) -> p a b", b=8), row_i[:, bass.ds(j * 4, 4), :]).then_inc(s_idx, 1)
                pool.wait_ge(s_idx, j + 3 + EXPERT_PAIRS)
                pool.sem_inc(s_tick, 1)
                for q in range(4):
                    if q >= 2:
                        pool.wait_ge(s_cadd, j * 32 + (8 * (q - 1) + 1))
                        pool.sem_inc(s_tick, 1)
                    for k in range(8):
                        g.indirect_dma_start(yg[:, q % 2, k, :], None, y_rows,
                                             bass.IndirectOffsetOnAxis(ap=stage[:, 8 * q + k:8 * q + k + 1], axis=0)
                                             ).then_inc(s_yg[q % 2], 16)
                    if q == 1:
                        power(pair)
                scale_wo(pair)

            body(Pair(0, 0))
            pool.wait_ge(s_idx, 1)
            g.tensor_copy(stage[:], idx[:, 0:32]).then_inc(s_idx, 1)
            pool.wait_ge(s_idx, 2)
            pool.wait_ge(s_xnd, 16)
            for e in range(RING + 1):
                if e == RING:
                    pool.wait_ge(s_T, 1)
                    pool.wait_ge(s_xg[0], 32)
                gather_tokens(e % RING, 2 * e)
            pool.wait_ge(s_xg[0], 64)
            with pool.Fori(0, EXPERT_PAIRS) as j:
                body(Pair(j, 1, experts=True))
            for slot in range(RING):
                pool.wait_ge(s_xg[slot], 32 * (STEPS + 1 + (slot == 0)))
            pool.wait_ge(s_yst[0], 16 * (E0 // 2 + 1))
            pool.wait_ge(s_yst[1], 16 * (E0 // 2 + 1))
            with pool.Fori(0, 2) as j:
                combine_body(Pair(j, 1 + EXPERT_PAIRS, combine=True))
            body(Pair(0, NP - 1))
            pool.wait_ge(s_oA, NP * TT)
            g.tensor_tensor(o_sq[:], o_sb[:], o_sb[:], ALU.mult).then_inc(s_sq, 1)
            pool.wait_ge(s_ms, NP)
            g.tensor_tensor(pw[:], ss[:], neg_half[:], ALU.pow).then_inc(s_pw, 1)

            def split_tokens(dn):
                for k in range(KD):
                    pool.wait_ge(dn.tok_hi, 1 + k)
                    g.tensor_tensor(x_lo[:, k, :], xnT[:, k, :], x_hi[:, k, :], ALU.subtract).then_inc(dn.tok_lo, 1)

            def split_weights(dn, u0, ne, f):
                with pool.Fori(0, ne // 2) as j:
                    for b in range(2):
                        pool.wait_ge(dn.hi, j * 2 + (u0 // 2 + b + 1))
                        n = 4 * f + D
                        g.tensor_tensor(w_lo[b][:, 0:n], wex[:, b, 0:n], w_hi[b][:, 0:n], ALU.subtract).then_inc(dn.lo, 1)

            pool.sem_inc(fall.lo, 2)
            pool.sem_inc(dense.lo, 2)
            pool.wait_ge(s_att, 1)
            over = pool.value_load(over_i[0:1, 0:1], min_val=0, max_val=1)
            with pool.If(over > 0):
                split_tokens(fall)
                split_weights(fall, 0, E0, F0)
            ln_power(1)
            ln_power(2)
            for half in range(2):
                pool.wait_ge(s_qkve, 4 * half + 4)
                for c in range(4 * half, 4 * half + 4):
                    last = g.tensor_tensor(
                        (o_sb if c < 4 else o_sq)[:].rearrange("p a b -> p (a b)")[:, (c % 4) * 512:(c % 4 + 1) * 512],
                        qkv_qk[:, c, :], qkv_qk[:, c, :], ALU.mult)
                last.then_inc(s_qsq, 1)
            pool.wait_ge(s_qms, 1)
            g.tensor_tensor(pw[:], ss[:], neg_half[:], ALU.pow).then_inc(s_qpw, 1)
            split_tokens(dense)
            split_weights(dense, 0, E1 + SH, F1)
            split_weights(dense, 2 * (E1 + SH), ESW, P)

        @block.tensor
        def _(pe):
            mm = nc.tensor.matmul
            tr = nc.tensor.transpose
            pe.wait_ge(s_c, 12)
            pe.sem_inc(dense.y, 3)
            pe.sem_inc(s_ys, 1)

            def transposed_tokens(n):
                for i in range(4):
                    pe.wait_ge(s_xn, n * TT + 2 * i + 2)
                    for c in range(2):
                        for k in range(KD):
                            o = (c * KD + k) * P
                            last = tr(bank[4 + i][:, o:o + P], xn[:, 2 * i + c, k * P:(k + 1) * P], ident[:])
                    last.then_inc(s_xT, 1)

            def logits(n, gate, ne):
                pe.wait_ge(s_xTe, 4 * n + 4)
                for c in range(TT):
                    for k in range(KD):
                        last = mm(bank[3][:, c * ne:(c + 1) * ne], xnT[:, k, c * P:(c + 1) * P], gate[:, k, :],
                                  start=k == 0, stop=k == KD - 1)
                last.then_inc(s_lg, 1)

            def g_free(pair, n):
                if n >= 2:
                    who, value = pair.taken(n - 2)
                    pe.wait_ge(s_gD if who == "D" else s_gA, value)
                else:
                    pe.wait_ge(s_gD, pair.at(NGD, PRO_D - 1 + n))

            def project_sqk(i, hf, bk):
                for k in range(KD):
                    last = mm(bk[:], wqks_sb[:, i, k, :], xnT[:, k, hf * HALF:(hf + 1) * HALF],
                              start=k == 0, stop=k == KD - 1)
                last.then_inc(s_gfull, 1)

            transposed_tokens(0)
            pe.wait_ge(dense.w[0], 16)
            pe.wait_ge(dense.w[1], 16)
            logits(0, gate0_sb, E0)
            pe.wait_ge(s_wqks, 16)
            for n in range(PRO):
                if n >= 4:
                    pe.wait_ge(s_gA, n - 3)
                elif n >= 2:
                    pe.wait_ge(s_gD, n - 1)
                project_sqk(n // 2, n % 2, G[n % 2])
            pe.wait_ge(s_chosen, 1)
            for c in range(TT):
                for b in range(c + 1):
                    last = mm(bank[7][:, c * E0:(c + 1) * E0], before_t[:] if b == c else ones[:, 0:P],
                              chosen[:, b, :], start=b == 0, stop=b == c)
            last.then_inc(s_rank, 1)
            pe.wait_ge(s_flag, 1)
            mm(bank[6][0:1, 0:1], over_p[:, 0:1], ones[:, 0:1], start=True, stop=True).then_inc(s_flag, 1)
            pe.wait_ge(s_sh, 1)

            def tokens_T(slot, xg_count, par, te):
                pe.wait_ge(s_xg[slot], xg_count)
                if te is not None:
                    pe.wait_ge(s_Te, te)
                for h in range(2):
                    for k in range(KD):
                        o = k * CAP + h * HC
                        last = tr(XT[:, o:o + HC], xg[0:HC, slot, h, k * P:(k + 1) * P], ident[0:HC, 0:HC])
                last.then_inc(s_T, 1)

            def gate_up_s(slot, w_count, par, te, free):
                pe.wait_ge(s_we[slot], w_count)
                pe.wait_ge(s_Te, te)
                if free is not None:
                    pe.wait_ge(s_hs, free)
                for gu in range(2):
                    for k in range(KD):
                        w = (gu * KD + k) * P
                        last = mm(GU[:, gu * CAP:(gu + 1) * CAP], wex[:, slot, w:w + P], xgT[:, par, k, :],
                                  start=k == 0, stop=k == KD - 1)
                last.then_inc(s_gus, 1)

            def output_product(pair, ot, wo_name):
                end = 1 if ot == "oT_end" else 0
                pe.wait_ge(s_on, pair.at(1, end))
                for i in range(4):
                    n = pair.use(ot, i)
                    g_free(pair, n)
                    for c in range(2):
                        for h in range(2):
                            o = (h * 2 + c) * P
                            last = tr(G[n % 2][:, o:o + P], o_n[:, 2 * i + c, h * P:(h + 1) * P], ident[:])
                    last.then_inc(s_gfull, 1)
                pe.wait_ge(s_wos, pair.at(1, end))
                for i in range(4):
                    n = pair.use(wo_name, i)
                    g_free(pair, n)
                    pe.wait_ge(s_gD, pair.taken(pair.use(ot, i))[1])
                    for c in range(2):
                        for h in range(2):
                            t = (2 * i + c) * P
                            last = mm(G[n % 2][:, c * D:(c + 1) * D], oT[:, h, t:t + P], wo_sb[:, h, :],
                                      start=h == 0, stop=h == 1)
                    last.then_inc(s_gfull, 1)

            def body(pair):
                j = pair.j
                pe.wait_ge(s_rT, pair.at(TT, TT))
                pe.wait_ge(s_gA, pair.at(NGA, PRO_A))
                pe.wait_ge(s_gD, pair.at(NGD, PRO_D))
                for c in range(TT):
                    n = pair.use("tr", c)
                    g_free(pair, n)
                    for i, src in enumerate((kT, eT, rT)):
                        last = tr(G[n % 2][:, i * P:(i + 1) * P], src[:, c * P:(c + 1) * P], ident[:])
                    last.then_inc(s_gfull, 1)

                def scores(m, lhs, rhs):
                    before = m if pair.experts else m - 1
                    if not (pair.first and before <= 0):
                        pe.wait_ge(s_mask, pair.at(16, before))
                    if m == 0 and not pair.first and not pair.experts:
                        pe.wait_ge(s_Te, E0 + 2)
                    mm(score_bank(pair, m)[:, 0:2 * P], lhs, rhs, start=True, stop=True).then_inc(s_sc, 1)

                def out_free(m):
                    if m == 0:
                        if not pair.first:
                            pe.wait_ge(s_oA, pair.at(8, 0))
                    elif m <= 8:
                        pe.wait_ge(s_okD, pair.at(8, m))
                    else:
                        pe.wait_ge(s_oA, pair.at(8, m - 8))

                def expert_front(s):
                    tokens_T((s + 2) % RING, j * 128 + ((s + 2) // RING + 1) * 32, s % 2, j * STEPS + (s + 2))

                def expert_back(s):
                    b, par = (s + 1) % RING, s % 2
                    pe.wait_ge(s_hs, j * STEPS + (s + 2))
                    pe.wait_ge(s_ye, j * STEPS + (s + 1))
                    for h in range(2):
                        last = mm(YB[0:HC, h * D:(h + 1) * D], hT_s[:, par, h * HC:(h + 1) * HC],
                                  wex[:, s % RING, 4 * P:4 * P + D], start=True, stop=True)
                    last.then_inc(s_ys, 1)
                    gate_up_s(b, j * 64 + ((s + 1) // RING + 1) * 16, (s + 1) % 2, j * STEPS + (s + 2), j * STEPS + (s + 2))

                def sc_a(c):
                    scores(c, kT[:, c * P:(c + 1) * P], qbd[:, c, :, :])
                sc_a(0)
                for c in range(TT):
                    if pair.experts:
                        expert_front(c)
                    if c < TT - 1:
                        sc_a(c + 1)
                    out_free(c)
                    pe.wait_ge(s_mask, pair.at(16, c + 1))
                    who, value = pair.taken(pair.use("tr", c))
                    pe.wait_ge(s_gA, value)
                    if c:
                        pe.wait_ge(s_stc, pair.at(14, c))
                    for h in range(2):
                        o = OUT[:, h * 64:(h + 1) * 64]
                        last = mm(o, masked[:, c % 2, h * P:(h + 1) * P], ker[:, c, 1, h * 64:(h + 1) * 64],
                                  start=True, stop=c == 0)
                        if c:
                            last = mm(o, qbd[:, c, h, :], sk_sb[:, h * 64:(h + 1) * 64], start=False, stop=True)
                    last.then_inc(s_out, 1)
                    if c < TT - 1:
                        mm(ST[:, 0:P], ker[:, c, 0, :], ker[:, c, 1, :], start=c == 0, stop=True,
                           skip_group_check=True).then_inc(s_st, 1)
                    if pair.experts:
                        expert_back(c)

                pe.wait_ge(s_wvg, pair.at(16, 16))
                for i in range(4):
                    n = pair.use("v", i)
                    g_free(pair, n)
                    for c in range(2):
                        t = (2 * i + c) * P
                        for k in range(KD):
                            last = mm(G[n % 2][:, c * D:(c + 1) * D], xnT[:, k, t:t + P], wvg_sb[:, k, 0, :],
                                      start=k == 0, stop=k == KD - 1)
                    last.then_inc(s_gfull, 1)
                if not pair.last:
                    pe.wait_ge(s_wqks, pair.at(16, 32))
                    for i, name in enumerate(("s", "k", "q")):
                        for hf in range(2):
                            n = pair.use(name, hf)
                            g_free(pair, n)
                            project_sqk(i, hf, G[n % 2])
                pe.wait_ge(s_pv, pair.at(1, 1))
                for i in range(2):
                    n = pair.use("pvT", i)
                    g_free(pair, n)
                    for c in range(4):
                        last = tr(G[n % 2][:, c * P:(c + 1) * P], pv[:, 4 * i + c, :], ident[:])
                    last.then_inc(s_gfull, 1)
                if pair.first:
                    for n in range(pair.use("oT"), pair.use("g")):
                        g_free(pair, n)
                        tr(G[n % 2][:, 0:P], ident[:], ident[:]).then_inc(s_gfull, 1)
                else:
                    output_product(pair, "oT", "wo")
                for i in range(4):
                    n = pair.use("g", i)
                    h, hf = i // 2, i % 2
                    g_free(pair, n)
                    for k in range(KD):
                        last = mm(G[n % 2][:], wvg_sb[:, k, 1, h * P:(h + 1) * P], xnT[:, k, hf * HALF:(hf + 1) * HALF],
                                  start=k == 0, stop=k == KD - 1)
                    last.then_inc(s_gfull, 1)

                pe.wait_ge(s_gD, pair.taken(pair.use("pvT", 1))[1])
                pe.wait_ge(s_eb, pair.at(1, 1))

                def sc_b(c):
                    scores(8 + c, eTb[:, c * P:(c + 1) * P], pbd[:, c, :, :])
                sc_b(0)
                for c in range(TT):
                    if pair.experts:
                        expert_front(8 + c)
                    if c < TT - 1:
                        sc_b(c + 1)
                    out_free(8 + c)
                    pe.wait_ge(s_mask, pair.at(16, c + 9))
                    if c:
                        pe.wait_ge(s_stc, pair.at(14, 7 + c))
                    for h in range(2):
                        o = OUT[:, h * P:(h + 1) * P]
                        last = mm(o, masked[:, c % 2, h * P:(h + 1) * P], v_sb[:, c, h * P:(h + 1) * P],
                                  start=True, stop=c == 0)
                        if c:
                            last = mm(o, pbd[:, c, h, :], sv_sb[:, h * P:(h + 1) * P], start=False, stop=True)
                    last.then_inc(s_out, 1)
                    if c < TT - 1:
                        mm(ST[:, 0:D], ker[:, c, 1, :], v_sb[:, c, :], start=c == 0, stop=True,
                           skip_group_check=True).then_inc(s_st, 1)
                    if pair.experts:
                        expert_back(8 + c)
                if pair.last:
                    output_product(pair, "oT_end", "wo_end")

            body(Pair(0, 0))
            pe.wait_ge(s_listf, 1)
            tr(YB[0:HC, 0:P], list_f[:], ident[:]).then_inc(s_lT, 1)
            tokens_T(0, 32, 0, None)
            gate_up_s(0, 16, 0, 1, None)
            tokens_T(1, 32, 1, 1)
            pe.wait_ge(s_idx, 1)
            pair_bodies(pe, body)

            def dense_pass(dn, tok_hi, tok_lo, u0, ne, f):
                def gate_up(j, u, b, hf):
                    pe.wait_ge(dn.h, j * 4 + (u0 + u + 1))
                    if hf == 0:
                        pe.wait_ge(dn.lo, j * 2 + ((u0 + u) // 2 + 3))
                    q = (u % 2) * 2
                    half = slice(hf * HALF, (hf + 1) * HALF)
                    terms = [(w, t, k) for w, t in ((w_lo[b], tok_hi), (w_hi[b], tok_lo), (w_hi[b], tok_hi))
                             for k in range(KD)]
                    for gu in range(2):
                        for i, (w, t, k) in enumerate(terms):
                            o = (gu * KD + k) * f
                            last = mm(bank[q + gu][0:f, :], w[:, o:o + f], t[:, k, half],
                                      start=i == 0, stop=i == len(terms) - 1)
                    last.then_inc(dn.gu, 1)

                def down(j, u, b):
                    pe.wait_ge(dn.h, j * 4 + (u0 + u + 3))
                    pe.wait_ge(dn.acc, j * 4 + (u0 + u + 1))
                    terms = ((h_lo, w_hi[b]), (h_hi, w_lo[b]), (h_hi, w_hi[b]))
                    for c in range(4):
                        yb = bank[4 + (u % 2) * 2 + c // 2]
                        for i, (h, w) in enumerate(terms):
                            last = mm(yb[:, (c % 2) * D:(c % 2 + 1) * D], h[0:f, u % 2, c * P:(c + 1) * P],
                                      w[0:f, 4 * f:4 * f + D], start=i == 0, stop=i == len(terms) - 1)
                    last.then_inc(dn.y, 1)

                if tok_hi is x_hi:
                    pe.wait_ge(dn.tok_lo, KD)
                gate_up(0, 0, 0, 0)

                def units(j, last):
                    for u in range(4):
                        if u < 3:
                            gate_up(j, u + 1, (u + 1) // 2, (u + 1) % 2)
                        elif not last:
                            gate_up(j, 4, 0, 0)
                        down(j, u, u // 2)
                with pe.Fori(0, ne // 2 - 1) as j:
                    units(j, False)
                units(ne // 2 - 1, True)

            pe.wait_ge(s_att, 1)
            over = pe.value_load(over_i[0:1, 0:1], min_val=0, max_val=1)
            with pe.If(over > 0):
                pe.sem_inc(fall.y, 3)
                dense_pass(fall, x_hi, x_lo, 0, E0, F0)

            transposed_tokens(1)
            logits(1, gate1_sb, E1)
            pe.wait_ge(s_gw, 32)
            for c in range(TT):
                b0, b1 = (0, 1) if c % 2 == 0 else (2, 7)
                if c >= 2:
                    pe.wait_ge(s_qkve, c - 1)
                for k in range(KD):
                    mm(bank[b0][:], xnT[:, k, c * P:(c + 1) * P], wqkv_v[:, k, 0:512], start=k == 0, stop=k == KD - 1)
                for k in range(KD):
                    last = mm(bank[b1][:, 0:D], xnT[:, k, c * P:(c + 1) * P], wqkv_v[:, k, 512:768],
                              start=k == 0, stop=k == KD - 1)
                last.then_inc(s_qkv, 1)
            for i, (src, made) in enumerate(((thq, s_thw), (wk, s_thw), (wv, s_wvv))):
                pe.wait_ge(made, (8, 16, 1)[i])
                if i == 0:
                    pe.wait_ge(s_qkve, TT)
                for q in range(4):
                    n = 4 * i + q
                    if n >= 4:
                        pe.wait_ge(s_t3e, n - 3)
                    for k in range(KD):
                        for c in range(2):
                            o = (k * 2 + c) * P
                            last = tr(bank[n % 4][:, o:o + P], src[:, 2 * q + c, k * P:(k + 1) * P], ident[:])
                    last.then_inc(s_t3, 1)
            pe.wait_ge(s_t3e, 12)
            pe.wait_ge(s_comb, 1)
            dense_pass(dense, x_hi, x_lo, 0, E1 + SH, F1)
            pe.wait_ge(s_yT, 1)
            dense_pass(dense, y_hi, y_lo, 2 * (E1 + SH), ESW, P)

        @block.scalar
        def _(act):
            A = nc.scalar.activation
            copy = nc.scalar.copy

            def transposed_tokens(n):
                for i in range(4):
                    act.wait_ge(s_xT, 4 * n + i + 1)
                    copy(xnT[:, :, 2 * i * P:(2 * i + 2) * P].rearrange("p k (c t) -> p k c t", c=2),
                         bank[4 + i][:].rearrange("p (c k t) -> p k c t", c=2, k=KD)).then_inc(s_xTe, 1)

            transposed_tokens(0)
            act.wait_ge(s_sh, 1)
            A(prob[:], left[:], ACT.Exp).then_inc(s_ex, 1)
            act.wait_ge(s_gD, 2)
            A(eT[:], sclip[:], ACT.Exp).then_inc(s_e, 1)
            for hf in range(2):
                act.wait_ge(s_gfull, 3 + hf)
                copy(kT[:, hf * HALF:(hf + 1) * HALF], G[hf][:]).then_inc(s_gA, 1)

            def tokens_copied(par, t, free):
                act.wait_ge(s_T, t)
                if free is not None:
                    act.wait_ge(s_gus, free)
                copy(xgT[:, par, :, :], XT[:, 0:KD * CAP].rearrange("p (k t) -> p k t", k=KD)).then_inc(s_Te, 1)

            def silu_s(par, gu, free):
                act.wait_ge(s_gus, gu)
                if free is not None:
                    act.wait_ge(s_hs, free)
                A(sil_s[:, par, :], GU[:, 0:CAP], ACT.Tanh, scale=0.5).then_inc(s_sl, 1)

            def body(pair):
                j = pair.j
                for c in range(TT):
                    n = pair.use("tr", c)
                    act.wait_ge(s_gfull, pair.full(n))
                    copy(ker[:, c, :, :], G[n % 2][:, 0:3 * P].rearrange("p (a b) -> p a b", a=3)).then_inc(s_gA, 1)

                def state(m, dst, src):
                    act.wait_ge(s_st, pair.at(14, m + 1))
                    copy(dst, src).then_inc(s_stc, 1)

                def expert_front(s):
                    tokens_copied(s % 2, j * STEPS + (s + 3), j * STEPS + (s + 1))

                def expert_back(s):
                    silu_s((s + 1) % 2, j * STEPS + (s + 2), j * STEPS + (s + 1))

                for c in range(TT):
                    if pair.experts:
                        expert_front(c)
                    if c < TT - 1:
                        state(c, sk_sb[:], ST[:, 0:P])
                    if pair.experts:
                        expert_back(c)
                for i in range(4):
                    n = pair.use("v", i)
                    act.wait_ge(s_gfull, pair.full(n))
                    if i == 0 and not pair.first:
                        act.wait_ge(s_ms, pair.at(1, 0))
                    copy(v_sb[:, 2 * i:2 * i + 2, :], G[n % 2][:].rearrange("p (a b) -> p a b", a=2)).then_inc(s_gA, 1)
                act.wait_ge(s_sub, pair.at(1, 1))
                A(pv[:], ok[:], ACT.Exp).then_inc(s_pv, 1)
                if not pair.last:
                    for hf in range(2):
                        n = pair.use("k", hf)
                        act.wait_ge(s_gfull, pair.full(n))
                        copy(kT[:, hf * HALF:(hf + 1) * HALF], G[n % 2][:]).then_inc(s_gA, 1)
                    act.wait_ge(s_gD, pair.taken(pair.use("s", 1))[1])
                    act.wait_ge(s_eb, pair.at(1, 1))
                    A(eT[:], sclip[:], ACT.Exp).then_inc(s_e, 1)
                for i in range(4):
                    n = pair.use("g", i)
                    act.wait_ge(s_gfull, pair.full(n))
                    if i >= 2:
                        act.wait_ge(s_gD, pair.taken(n - 2)[1])
                    A(th[:, i % 2, :], G[n % 2][:], ACT.Tanh, scale=0.5).then_inc(s_th, 1)
                for c in range(TT):
                    if pair.experts:
                        expert_front(8 + c)
                    act.wait_ge(s_out, pair.at(16, 9 + c))
                    if c == 0 and not pair.first:
                        act.wait_ge(s_on, pair.at(1, 0))
                    copy(o_sb[:, c, :], OUT[:, 0:D]).then_inc(s_oA, 1)
                    if c < TT - 1:
                        state(7 + c, sv_sb[:], ST[:, 0:D])
                    if pair.experts:
                        expert_back(8 + c)

            body(Pair(0, 0))
            tokens_copied(0, 1, None)
            silu_s(0, 1, None)
            tokens_copied(1, 2, None)
            pair_bodies(act, body)

            def split_tokens(dn):
                for k in range(KD):
                    copy(x_hi[:, k, :], xnT[:, k, :]).then_inc(dn.tok_hi, 1)

            def dense_pass(dn, u0, ne, f):
                def weights_hi(j, e):
                    act.wait_ge(dn.w[e % 2], j * 16 + (u0 // 4 + e // 2 + 2) * 16)
                    act.wait_ge(dn.y, j * 4 + (u0 + 2 * e + 1))
                    n = 4 * f + D
                    copy(w_hi[e % 2][:, 0:n], wex[:, e % 2, 0:n]).then_inc(dn.hi, 1)

                def units(j, last):
                    for u in range(4):
                        act.wait_ge(dn.gu, j * 4 + (u0 + u + 1))
                        act.wait_ge(dn.h, j * 4 + (u0 + u + 1))
                        A(sil[0:f, u % 2, :], bank[(u % 2) * 2][0:f, :], ACT.Silu).then_inc(dn.sil, 1)
                        if u == 0 or (u == 2 and not last):
                            weights_hi(j, u // 2 + 1)

                weights_hi(0, 0)
                with act.Fori(0, ne // 2 - 1) as j:
                    units(j, False)
                units(ne // 2 - 1, True)

            act.wait_ge(s_att, 1)
            over = act.value_load(over_i[0:1, 0:1], min_val=0, max_val=1)
            with act.If(over > 0):
                split_tokens(fall)
                dense_pass(fall, 0, E0, F0)
            transposed_tokens(1)
            act.wait_ge(s_lg, 2)
            A(prob[:, :, 0:E1], bank[3][:, 0:TT * E1].rearrange("p (c e) -> p c e", c=TT), ACT.Sigmoid).then_inc(s_ex, 1)
            for c in range(TT):
                b0, b1 = (0, 1) if c % 2 == 0 else (2, 7)
                act.wait_ge(s_qkv, c + 1)
                if c == 0:
                    act.wait_ge(s_rstd, 3)
                A(qkv_qk[:, c, :], bank[b0][:], ACT.Copy, scale=rstd[:, c:c + 1])
                A(qkv_v[:, c, :], bank[b1][:, 0:D], ACT.Copy, scale=rstd[:, c:c + 1]).then_inc(s_qkve, 1)
            act.wait_ge(s_rqk, 1)
            for c in range(TT):
                A(thq[:, c, :], qkv_qk[:, c, 0:D], ACT.Tanh, scale=rs[:, c:c + 1]).then_inc(s_thw, 1)
            for c in range(TT):
                A(wk[:, c, :], qkv_qk[:, c, D:2 * D], ACT.Exp, scale=rs[:, TT + c:TT + c + 1]).then_inc(s_thw, 1)
            for i, dst in enumerate((thT, wcT, kvT)):
                for q in range(4):
                    n = 4 * i + q
                    act.wait_ge(s_t3, n + 1)
                    copy(dst[:, :, 2 * q * P:(2 * q + 2) * P],
                         bank[n % 4][:].rearrange("p (k t) -> p k t", k=KD)).then_inc(s_t3e, 1)
            split_tokens(dense)
            dense_pass(dense, 0, E1 + SH, F1)
            dense_pass(dense, 2 * (E1 + SH), ESW, P)

        @block.vector
        def _(dve):
            V = nc.vector
            links = {"base": 0, "n": 0}

            def link(ins):
                links["n"] += 1
                ins.then_inc(s_dve, 1)
                dve.wait_ge(s_dve, links["base"] + links["n"])

            def wide(col, n):
                return col.unsqueeze(2).broadcast_to([P, col.shape[1], n])

            dve.sem_inc(s_hs, 1)
            dve.sem_inc(s_ye, 1)
            dve.sem_inc(s_cadd, 1)
            dve.sem_inc(s_yst[0], 16)
            dve.sem_inc(s_yst[1], 16)

            def layernorm(n):
                for c in range(TT):
                    last = V.bn_stats(stats[:, c, :], acc[:, c, :])
                link(last)
                for c in range(TT):
                    last = V.bn_aggr(mv[:, c, :], stats[:, c, :])
                link(last)
                V.tensor_scalar(veps[:], mv[:, :, 1], EPS_LN, None, ALU.add).then_inc(s_var, 1)
                dve.wait_ge(s_rstd, n + 1)
                for c in range(TT):
                    V.tensor_scalar(xn[:, c, :], acc[:, c, :], mv[:, c, 0:1], rstd[:, c:c + 1],
                                    ALU.subtract, ALU.mult).then_inc(s_xn, 1)

            dve.wait_ge(s_x, 16)
            layernorm(0)

            dve.wait_ge(s_lg, 1)
            lg = bank[3][:].rearrange("p (c e) -> p c e", c=TT)
            link(V.tensor_reduce(rmax[:], lg, AX, ALU.max))
            V.tensor_tensor(left[:], lg, wide(rmax[:], E0), ALU.subtract).then_inc(s_sh, 1)

            def clip_s(wait, bk, hf):
                dve.wait_ge(s_gfull, wait)
                V.tensor_scalar(sclip[:, hf * HALF:(hf + 1) * HALF], bk[:], 32.0, -32.0,
                                ALU.min, ALU.max).then_inc(s_gD, 1)

            def place_q(wait, bk, hf):
                dve.wait_ge(s_gfull, wait)
                for h in range(2):
                    r = slice(64 * h, 64 * h + 64)
                    last = V.tensor_scalar(qbd[r, 4 * hf:4 * hf + 4, h, :],
                                           bk[r, :].rearrange("p (c t) -> p c t", c=4), 0.125, None, ALU.mult)
                last.then_inc(s_gD, 1)

            def running_sum():
                link(V.tensor_tensor_scan(zT[:], ones[:], eT[:], 0.0, ALU.mult, ALU.add))

            def reciprocal_z(c):
                V.reciprocal(rT[:, c * P:(c + 1) * P], zT[:, c * P:(c + 1) * P]).then_inc(s_rT, 1)

            dve.wait_ge(s_c, 12)
            for hf in range(2):
                clip_s(1 + hf, G[hf], hf)
            for hf in range(2):
                place_q(5 + hf, G[hf], hf)
            dve.wait_ge(s_ex, 1)
            link(V.tensor_reduce(rsum[:], prob[:], AX, ALU.add))
            link(V.reciprocal(rsum[:], rsum[:]))
            link(V.tensor_tensor(prob[:], prob[:], wide(rsum[:], E0), ALU.mult))
            for c in range(TT):
                last = V.max(top[:, c, :], prob[:, c, :])
            link(last)
            for c in range(TT):
                last = V.match_replace(left[:, c, :], top[:, c, :], prob[:, c, :], -1.0)
            link(last)
            V.tensor_scalar(chosen[:], left[:], 0.0, None, ALU.is_lt).then_inc(s_chosen, 1)
            dve.wait_ge(s_chosen, 1)
            link(V.tensor_tensor(comb0[:], prob[:], chosen[:], ALU.mult))
            dve.wait_ge(s_rank, 1)
            rank = bank[7][:].rearrange("p (c e) -> p c e", c=TT)
            link(V.tensor_scalar(fits[:], rank, float(CAP), None, ALU.is_lt))
            link(V.tensor_tensor(prob[:], comb0[:], fits[:], ALU.mult))
            link(V.tensor_tensor(over0[:], comb0[:], prob[:], ALU.subtract))
            link(V.tensor_tensor(left[:], rank, slot_of[:].unsqueeze(1).broadcast_to([P, TT, E0]), ALU.add))
            link(V.tensor_tensor(left[:], left[:], chosen[:], ALU.mult))
            link(V.tensor_tensor(comb0[:], chosen[:], fits[:], ALU.mult))
            link(V.tensor_tensor(left[:], left[:], comb0[:], ALU.mult))
            link(V.tensor_tensor(comb0[:], chosen[:], comb0[:], ALU.subtract))
            V.tensor_reduce(over_p[:], comb0[:].rearrange("p c e -> p (c e)"), AX, ALU.max).then_inc(s_flag, 1)
            for c in range(TT):
                last = V.max(top[:, c, :], left[:, c, :])
            link(last)
            link(V.scalar_tensor_tensor(w8[:], top[:], 0.0, junk_of[:], ALU.is_equal, ALU.mult))
            link(V.scalar_tensor_tensor(w8[:], top[:], -1.0, w8[:], ALU.add, ALU.add))
            V.tensor_scalar(row_i[:], w8[:], float(JUNK), None, ALU.min)
            V.tensor_copy(slot_i[:], w8[:]).then_inc(s_slot, 1)
            dve.wait_ge(s_e, 1)
            running_sum()
            for c in range(TT):
                reciprocal_z(c)
            dve.wait_ge(s_slot, 1)
            dve.wait_ge(s_zero, 32)
            dve.wait_ge(s_flag, 2)
            V.tensor_scalar(over_i[0:1, 0:1], bank[6][0:1, 0:1], 0.5, None, ALU.is_gt).then_inc(s_flagi, 1)
            link(V.tensor_copy(fits[:], prob[:]))

            def h_s(par, sl, free):
                dve.wait_ge(s_sl, sl)
                if free is not None:
                    dve.wait_ge(s_ys, free)
                V.scalar_tensor_tensor(sil_s[:, par, :], sil_s[:, par, :], 1.0, GU[:, 0:CAP], ALU.add, ALU.mult
                                       ).then_inc(s_w8, 1)

            def expert_h(par, sl, free, seen):
                h_s(par, sl, free)
                dve.wait_ge(s_w8, seen)
                V.tensor_tensor(hT_s[:, par, :], sil_s[:, par, :], GU[:, CAP:2 * CAP], ALU.mult).then_inc(s_hs, 1)

            def gate_and_add(pair, ot, wo_name):
                for i in range(4):
                    n = pair.use(ot, i)
                    dve.wait_ge(s_gfull, pair.full(n))
                    t = 2 * i * P
                    V.tensor_tensor(oT[:, :, t:t + 2 * P], G[n % 2][:].rearrange("p (h t) -> p h t", h=2),
                                    gT[:, :, t:t + 2 * P], ALU.mult).then_inc(s_gD, 1)
                for i in range(4):
                    n = pair.use(wo_name, i)
                    dve.wait_ge(s_gfull, pair.full(n))
                    a = acc[:, 2 * i:2 * i + 2, :]
                    V.tensor_tensor(a, a, G[n % 2][:].rearrange("p (c d) -> p c d", c=2), ALU.add).then_inc(s_gD, 1)

            def root_mean_square(pair, k):
                dve.wait_ge(s_sq, pair.at(1, k))
                link(V.tensor_reduce(ss[:], o_sq[:].rearrange("p c (h v) -> p (c h) v", h=2), AX, ALU.add))
                link(V.tensor_tensor(ss[:], ss[:], rs[:], ALU.mult))
                link(V.tensor_tensor(ss[:], ss[:], rs[:], ALU.mult))
                V.tensor_scalar(ss[:], ss[:], 1.0 / 128, EPS_O, ALU.mult, ALU.add).then_inc(s_ms, 1)

            def normalise(pair, k):
                dve.wait_ge(s_pw, pair.at(1, k))
                link(V.tensor_tensor(sc16[:], pw[:], rs[:], ALU.mult))
                V.tensor_tensor(o_n[:].rearrange("p c (h v) -> p (c h) v", h=2),
                                o_sb[:].rearrange("p c (h v) -> p (c h) v", h=2),
                                wide(sc16[:], P), ALU.mult).then_inc(s_on, 1)

            def slot_weights(first, n):
                for k in range(first, first + n):
                    link(V.tensor_tensor(prob[:], left[:], wide(top[:, :, k], E0), ALU.is_equal))
                    link(V.tensor_tensor(prob[:], prob[:], fits[:], ALU.mult))
                    link(V.tensor_reduce(w8[:, :, k], prob[:], AX, ALU.add))
                if first + n == TOP0:
                    link(V.tensor_scalar(w8[:], w8[:], 0.5, None, ALU.mult))

            def body(pair):
                j = pair.j

                def mask(m):
                    dve.wait_ge(s_sc, pair.at(16, m + 1))
                    if m >= 2:
                        dve.wait_ge(s_out, pair.at(16, m - 1))
                    V.tensor_tensor(masked[:, m % 2, :], score_bank(pair, m)[:, 0:2 * P],
                                    causal[:].rearrange("p a b -> p (a b)"), ALU.mult).then_inc(s_mask, 1)

                def expert_back(s):
                    dve.wait_ge(s_ys, j * STEPS + (s + 2))
                    dve.wait_ge(s_yst[s % 2], j * (8 * 16) + (s // 2 + 1) * 16)
                    V.tensor_copy(y_sb[0:HC, s % 2, :, :], YB[0:HC, :].rearrange("p (h d) -> p h d", h=2)).then_inc(s_ye, 1)
                    expert_h((s + 1) % 2, j * STEPS + (s + 2), j * STEPS + (s + 1), j * STEPS + (s + 2))

                def add_results(first, n):
                    for i in range(first, first + n):
                        q, k, t = i // TOP0, i % TOP0, j * 4 + i // TOP0
                        if k == 0:
                            dve.wait_ge(s_yg[q % 2], j * 256 + (q // 2 + 1) * 128)
                        dve.wait_ge(s_cadd, j * 32 + (i + 1))
                        a = acc[:, bass.ds(t, 1), :]
                        V.scalar_tensor_tensor(a, yg[:, q % 2, k:k + 1, :], w8[:, bass.ds(t, 1), k], a,
                                               ALU.mult, ALU.add).then_inc(s_cadd, 1)

                mask(0)
                for c in range(TT):
                    if c < TT - 1:
                        mask(c + 1)
                    dve.wait_ge(s_out, pair.at(16, c + 1))
                    V.tensor_tensor(ok[:, c, :], OUT[:, 0:P], ker[:, c, 2, :], ALU.mult).then_inc(s_okD, 1)
                    if pair.experts:
                        expert_back(c)
                    if pair.combine and c >= 4:
                        add_results(2 * (c - 4), 2)
                    if c == 5 and not pair.first:
                        root_mean_square(pair, 0)
                dve.wait_ge(s_okD, pair.at(8, 8))
                slots = ok[:].rearrange("p c (h m) -> p (c h) m", h=2)
                link(V.tensor_reduce(mx[:], slots, AX, ALU.max))
                V.tensor_tensor(slots, slots, wide(mx[:], 64), ALU.subtract).then_inc(s_sub, 1)
                if not pair.last:
                    for hf in range(2):
                        n = pair.use("s", hf)
                        clip_s(pair.full(n), G[n % 2], hf)
                if pair.first:
                    slot_weights(0, 4)
                else:
                    normalise(pair, 0)
                dve.wait_ge(s_pv, pair.at(1, 1))
                link(V.tensor_reduce(sm[:], pv[:].rearrange("p c (h m) -> p (c h) m", h=2), AX, ALU.add))
                link(V.reciprocal(rs[:], sm[:]))
                if not pair.last:
                    for hf in range(2):
                        n = pair.use("q", hf)
                        place_q(pair.full(n), G[n % 2], hf)
                for i in range(2):
                    n = pair.use("pvT", i)
                    dve.wait_ge(s_gfull, pair.full(n))
                    for h in range(2):
                        r = slice(64 * h, 64 * h + 64)
                        last = V.tensor_tensor(pbd[r, 4 * i:4 * i + 4, h, :],
                                               G[n % 2][r, :].rearrange("p (c t) -> p c t", c=4),
                                               rT[r, i * HALF:(i + 1) * HALF].rearrange("p (c t) -> p c t", c=4), ALU.mult)
                    last.then_inc(s_gD, 1)
                if pair.first:
                    for n in range(pair.use("oT"), pair.use("g")):
                        dve.wait_ge(s_gfull, pair.full(n))
                        V.tensor_copy(mv[:, n - pair.use("oT"), 0:1], G[n % 2][:, 0:1]).then_inc(s_gD, 1)
                    slot_weights(4, 4)
                else:
                    gate_and_add(pair, "oT", "wo")
                if not pair.last:
                    dve.wait_ge(s_e, pair.at(1, 2))
                    running_sum()
                for i in range(4):
                    n = pair.use("g", i)
                    h, hf = i // 2, i % 2
                    dve.wait_ge(s_th, pair.at(4, i + 1))
                    V.scalar_tensor_tensor(gT[:, h, hf * HALF:(hf + 1) * HALF], th[:, i % 2, :], 1.0,
                                           G[n % 2][:], ALU.add, ALU.mult).then_inc(s_gD, 1)
                mask(8)
                for c in range(TT):
                    if c < TT - 1:
                        mask(9 + c)
                    if not pair.last:
                        reciprocal_z(c)
                    if pair.combine:
                        add_results(8 + 3 * c, 3)
                    if pair.experts:
                        expert_back(8 + c)
                if pair.last:
                    root_mean_square(pair, 1)
                    normalise(pair, 1)
                    gate_and_add(pair, "oT_end", "wo_end")
                    dve.wait_ge(s_gD, pair.taken(pair.use("wo_end", 3))[1])

            def looped(rounds, make):
                start = links["base"] + links["n"]
                probe = LINKS[make(0)]
                with dve.Fori(0, rounds) as j:
                    links["base"], links["n"] = j * probe + start, 0
                    body(make(j, True))
                    assert links["n"] == probe, links["n"]
                links["base"], links["n"] = 0, start + rounds * probe

            def make_experts(j, pair=False):
                return Pair(j, 1, experts=True) if pair else "experts"

            def make_combine(j, pair=False):
                return Pair(j, 1 + EXPERT_PAIRS, combine=True) if pair else "combine"

            LINKS = {"experts": 8, "combine": 8}

            body(Pair(0, 0))
            dve.wait_ge(s_listed, 16)
            V.tensor_copy(list_f[:], list_i[:]).then_inc(s_listf, 1)
            dve.wait_ge(s_lT, 1)
            V.tensor_copy(idx[0:HC, 0:P], YB[0:HC, 0:P]).then_inc(s_idx, 1)
            expert_h(0, 1, None, 1)
            looped(EXPERT_PAIRS, make_experts)
            looped(2, make_combine)
            body(Pair(0, NP - 1))
            for dn in (fall, dense):
                dve.sem_inc(dn.h, 2)
                dve.sem_inc(dn.acc, 2)
            dve.sem_inc(s_att, 1)

            def dense_pass(dn, comb, u0, ne, f):
                def make_h(j, u):
                    dve.wait_ge(dn.sil, j * 4 + (u0 + u + 1))
                    dve.wait_ge(dn.y, j * 4 + (u0 + u + 2))
                    V.tensor_tensor(h_f32[0:f, u % 2, :], sil[0:f, u % 2, :], bank[(u % 2) * 2 + 1][0:f, :],
                                    ALU.mult).then_inc(dn.made, 1)
                    dve.wait_ge(dn.made, j * 8 + (2 * (u0 + u) + 1))
                    V.tensor_copy(h_hi[0:f, u % 2, :], h_f32[0:f, u % 2, :]).then_inc(dn.made, 1)
                    dve.wait_ge(dn.made, j * 8 + (2 * (u0 + u) + 2))
                    V.tensor_tensor(h_lo[0:f, u % 2, :], h_f32[0:f, u % 2, :], h_hi[0:f, u % 2, :],
                                    ALU.subtract).then_inc(dn.h, 1)

                def add(j, u):
                    dve.wait_ge(dn.y, j * 4 + (u0 + u + 4))
                    dve.wait_ge(dn.acc, j * 4 + (u0 + u + 1))
                    for c in range(4):
                        yb = bank[4 + (u % 2) * 2 + c // 2][:, (c % 2) * D:(c % 2 + 1) * D]
                        t = (u % 2) * 4 + c
                        if comb is not None:
                            last = V.scalar_tensor_tensor(acc[:, t, :], yb, comb[:, t, bass.ds(j * 2 + u // 2, 1)],
                                                          acc[:, t, :], ALU.mult, ALU.add)
                        else:
                            last = V.tensor_tensor(acc[:, t, :], acc[:, t, :], yb, ALU.add)
                    last.then_inc(dn.acc, 1)

                def units(j, last):
                    for u in range(4):
                        if u < 3 or not last:
                            make_h(j, u + 1)
                        add(j, u)

                make_h(0, 0)
                with dve.Fori(0, ne // 2 - 1) as j:
                    units(j, False)
                units(ne // 2 - 1, True)

            over = dve.value_load(over_i[0:1, 0:1], min_val=0, max_val=1)
            with dve.If(over > 0):
                dense_pass(fall, over0, 0, E0, F0)
                dve.wait_ge(fall.acc, 2 + 2 * E0)
            layernorm(1)
            dve.wait_ge(s_xn, 2 * TT)
            for c in range(TT):
                last = V.tensor_tensor_reduce(out=o_sq[:, c, :], in0=xn[:, c, :], in1=xn[:, c, :], scale=1.0, scalar=0.0,
                                              op0=ALU.mult, op1=ALU.add, accum_out=ss[:, c:c + 1])
            link(last)
            V.tensor_scalar(veps[:], ss[:, 0:TT], 1.0 / D, EPS_RMS, ALU.mult, ALU.add).then_inc(s_var, 1)
            link(V.tensor_tensor(acc[:], acc[:], xn[:], ALU.add))

            dve.wait_ge(s_ex, 2)
            V.memset(prob[:, :, E1:E1 + 2], -1.0)
            for c in range(TT):
                last = V.max(top[:, c, :], prob[:, c, 0:E1])
            link(last)
            link(V.memset(top[:, :, TOP1:8], -1.0))
            for c in range(TT):
                last = V.match_replace(left[:, c, 0:E1 + 2], top[:, c, :], prob[:, c, 0:E1 + 2], 0.0)
            link(last)
            link(V.tensor_tensor(comb1, prob[:, :, 0:E1 + 2], left[:, :, 0:E1 + 2], ALU.subtract))
            link(V.tensor_reduce(rsum[:], comb1[:, :, 0:E1], AX, ALU.add))
            link(V.tensor_scalar(rsum[:], rsum[:], 1e-20, None, ALU.add))
            link(V.reciprocal(rsum[:], rsum[:]))
            link(V.tensor_tensor(comb1[:, :, 0:E1], comb1[:, :, 0:E1],
                                 rsum[:].unsqueeze(2).broadcast_to([P, TT, E1]), ALU.mult))
            V.memset(comb1[:, :, E1:E1 + SH], 1.0).then_inc(s_comb, 1)

            dve.wait_ge(s_qsq, 2)
            for i, src in enumerate((o_sb, o_sq)):
                last = V.tensor_reduce(ss[:, 8 * i:8 * i + 8],
                                       src[:].rearrange("p a d -> p (a d)").rearrange("p (n d) -> p n d", d=D), AX, ALU.add)
            link(last)
            V.tensor_scalar(ss[:], ss[:], 1.0 / D, EPS_RMS, ALU.mult, ALU.add).then_inc(s_qms, 1)
            dve.wait_ge(s_qpw, 1)
            pqk = pw[:].rearrange("p (c a) -> p a c", a=2)
            V.tensor_scalar(rs[:, 0:TT], pqk[:, 0, :], 0.5, None, ALU.mult)
            V.tensor_copy(rs[:, TT:2 * TT], pqk[:, 1, :]).then_inc(s_rqk, 1)
            dve.wait_ge(s_thw, 2 * TT)
            V.tensor_tensor(wv[:], wk[:], qkv_v, ALU.mult).then_inc(s_wvv, 1)
            for k in range(KD):
                dve.wait_ge(s_t3e, 8)
                V.tensor_tensor_scan(wcum[:, k, :], ones[:], wcT[:, k, :], 0.0, ALU.mult, ALU.add)
            for k in range(KD):
                dve.wait_ge(s_t3e, 12)
                last = V.tensor_tensor_scan(kvcum[:, k, :], ones[:], kvT[:, k, :], 0.0, ALU.mult, ALU.add)
            link(last)
            link(V.tensor_scalar(wcum, wcum, 1e-6, 2.0, ALU.add, ALU.mult))
            link(V.reciprocal(wcum, wcum))
            link(V.tensor_tensor(kvcum, kvcum, wcum, ALU.mult))
            link(V.scalar_tensor_tensor(yT, thT[:], 1.0, kvcum, ALU.add, ALU.mult))
            link(V.tensor_copy(y_hi, yT))
            V.tensor_tensor(y_lo, yT, y_hi, ALU.subtract).then_inc(s_yT, 1)
            dense_pass(dense, comb1, 0, E1 + SH, F1)
            dense_pass(dense, None, 2 * (E1 + SH), ESW, P)


def kernel(**inputs):
    import numpy as np
    import concourse.bacc as bacc
    from concourse.bass_utils import run_bass_kernel_spmd

    a = {k: np.asarray(v) for k, v in inputs.items()}

    def by_k(w):
        return w.reshape(KD, P, -1).transpose(1, 0, 2)

    def by_pair(w):
        return w.reshape(KD, P, NP, -1).transpose(2, 1, 0, 3)

    def by_expert(gate, up, down, pad=0):
        gate, up, down = (np.concatenate([w, np.zeros((pad, *w.shape[1:]), w.dtype)]) for w in (gate, up, down))
        e, _, f = gate.shape
        row = [w.reshape(e, KD, P, f).transpose(0, 2, 1, 3).reshape(e, P, KD * f) for w in (gate, up)]
        low = np.zeros((e, P, D), down.dtype)
        low[:, :f] = down
        return np.concatenate([*row, low], axis=2)

    w13 = a["L0_ffn_w13"]
    swi = a["L1_attn_w_swiglu"]
    ff = swi.shape[0] // 2
    sg, su, sd = (a[f"L1_ffn_{n}"] for n in ("sg", "su", "sd"))
    shared = [w.reshape(D, SH, F1).transpose(1, 0, 2) for w in (sg, su)]
    arrays = {
        "x": a["L0_attn_hidden_states"].reshape(T, D),
        "wqks": np.stack([by_pair(a[f"L0_attn_{n}"]) for n in ("Ws", "Wk", "Wq")], axis=2),
        "wvg": np.stack([by_pair(a["L0_attn_Wv"]), by_pair(a["L0_attn_Wg"])], axis=3),
        "wo": a["L0_attn_Wo"].reshape(NP, 2, P, D).transpose(0, 2, 1, 3),
        "gnw": a["L0_attn_g_norm_weight"].reshape(P, 1),
        "gate0": by_k(a["L0_ffn_gate_w"].T),
        "w0": by_expert(w13[:, :F0].transpose(0, 2, 1), w13[:, F0:].transpose(0, 2, 1), a["L0_ffn_w2"].transpose(0, 2, 1),
                        EP - E0),
        "wqkv": by_k(a["L1_attn_w_qkv"].T),
        "wsw": by_expert(swi[ff:].reshape(ESW, P, D).transpose(0, 2, 1), swi[:ff].reshape(ESW, P, D).transpose(0, 2, 1),
                         a["L1_attn_w_out"].T.reshape(ESW, P, D)),
        "gate1": by_k(a["L1_ffn_gate_w"]),
        "w1": by_expert(*(np.concatenate([w, s]) for w, s in (
            (a["L1_ffn_wg"], shared[0]), (a["L1_ffn_wu"], shared[1]), (a["L1_ffn_wd"], sd.reshape(SH, F1, D))))),
    }
    nc = bacc.Bacc("TRN2", target_bir_lowering=False, num_devices=1)
    args, given = [], {}
    for name, array in arrays.items():
        given[f"in_{name}"] = np.ascontiguousarray(array)
        args.append(nc.dram_tensor(f"in_{name}", array.shape, mybir.dt.from_np(array.dtype), kind="ExternalInput").ap())
    args.append(nc.dram_tensor("result", (T, D), F32, kind="ExternalOutput").ap())
    build(nc, *args)
    r = run_bass_kernel_spmd(nc, [given], core_ids=[0])
    return r.results[0]["result"].reshape(1, T, D)
```

```python
from contextlib import ExitStack

import concourse.bass as bass
from concourse import mybir

F32, F32R, I32 = mybir.dt.float32, mybir.dt.float32r, mybir.dt.int32
ALU = mybir.AluOpType
ACT = mybir.ActivationFunctionType
AX = mybir.AxisListType.X

P = 128
T, D = 1024, 256
TT = T // P
KD = D // P
NP = 8
HALF = T // 2
EPS_LN, EPS_O, EPS_RMS = 1e-5, 1e-5, 1.1920929e-07
E0, TOP0, F0 = 64, 8, 128
E1, TOP1, F1, SH = 32, 6, 96, 2
ESW = 8
WROW = 4 * P + D

CAP, HC = 192, 96
JUNK = E0 * CAP
LISTED = JUNK + T * TOP0
STEPS = 16
EXPERT_PAIRS = E0 // STEPS
EP = E0 + 4
IDX = 2 * (E0 + 6)
RING = 4

USES = [("tr", 8, "A"), ("v", 4, "A"), ("s", 2, "D"), ("k", 2, "A"), ("q", 2, "D"), ("pvT", 2, "D"),
        ("oT", 4, "D"), ("wo", 4, "D"), ("g", 4, "D")]
LAST_USES = [("tr", 8, "A"), ("v", 4, "A"), ("pvT", 2, "D"), ("oT", 4, "D"), ("wo", 4, "D"), ("g", 4, "D"),
             ("oT_end", 4, "D"), ("wo_end", 4, "D")]


def laid_out(uses):
    first, taken_by = {}, []
    for name, n, who in uses:
        first[name] = len(taken_by)
        taken_by += [who] * n
    return first, taken_by


FIRST_USE, TAKEN_BY = laid_out(USES)
LAST_FIRST, LAST_TAKEN_BY = laid_out(LAST_USES)
NG, NGD, NGA = len(TAKEN_BY), TAKEN_BY.count("D"), TAKEN_BY.count("A")
PRO, PRO_D, PRO_A = 6, 4, 2
PASSES = ((1, 0), (0, 1), (0, 0))


class Pair:

    def __init__(self, j, off, experts=False, combine=False):
        self.j, self.off, self.experts, self.combine = j, off, experts, combine
        self.first = isinstance(j, int) and off == 0
        self.last = isinstance(j, int) and off == NP - 1

    def at(self, per, k):
        v = self.off * per + k
        return v if isinstance(self.j, int) else self.j * per + v

    def use(self, name, i=0):
        return (LAST_FIRST if self.last else FIRST_USE)[name] + i

    def full(self, n):
        return self.at(NG, PRO + n + 1)

    def taken(self, n):
        taken_by = LAST_TAKEN_BY if self.last else TAKEN_BY
        who = taken_by[n]
        k = taken_by[:n + 1].count(who)
        return (who, self.at(NGD, PRO_D + k)) if who == "D" else (who, self.at(NGA, PRO_A + k))


class Dense:

    def __init__(self, sem, name):
        self.w = [sem(f"{name}_w0"), sem(f"{name}_w1")]
        self.gu, self.sil, self.h, self.y, self.acc, self.hi, self.lo, self.made = (
            sem(f"{name}_{n}") for n in ("gu", "sil", "h", "y", "acc", "hi", "lo", "made"))


def build(nc, x, wqks, wvg, wo, gnw, gate0, w0, wqkv, wsw, gate1, w1, out):
    listed = nc.dram_tensor("listed", (LISTED, 1), I32, kind="Internal").ap()
    xn_rows = nc.dram_tensor("xn_rows", (T, D), F32, kind="Internal").ap()
    y_rows = nc.dram_tensor("y_rows", (JUNK + 1, D), F32, kind="Internal").ap()
    ctx = ExitStack()
    with ctx:
        def sb(name, *shape, dt=F32, stack=ctx):
            return stack.enter_context(nc.sbuf_tensor(name, [P, *shape], dt))

        def sem(name):
            return ctx.enter_context(nc.semaphore(name))

        bank = [ctx.enter_context(nc.psum_tensor(f"bank{i}", [P, 512], F32)) for i in range(8)]
        G = bank[0:2]
        SC, OUT, ST = bank[2], bank[3], bank[4]
        XT, GU, YB = bank[5], bank[6], bank[7]

        ident = sb("ident", P)
        causal = sb("causal", 2, P)
        before_t = sb("before_t", P)
        ones = sb("ones", T)
        neg_half = sb("neg_half", 16)
        slot_of = sb("slot_of", E0)
        token_id = sb("token_id", TT, dt=I32)
        junk_of = sb("junk_of", TT, 8)
        zero_i = sb("zero_i", JUNK // P, dt=I32)
        acc = sb("acc", TT, D)
        xT_hi, xT_lo = (sb(f"xT_{part}", KD, T, dt=F32R) for part in ("hi", "lo"))
        stats = sb("stats", TT, 6)
        mv = sb("mv", TT, 2)
        veps = sb("veps", TT)
        rstd = sb("rstd", TT)
        gate0_sb = sb("gate0_sb", KD, E0)
        gate1_sb = sb("gate1_sb", KD, E1)
        comb0 = sb("comb0", TT, E0)
        over0 = sb("over0", TT, E0)
        prob = sb("prob", TT, E0)
        left = sb("left", TT, E0)
        chosen = sb("chosen", TT, E0)
        fits = sb("fits", TT, E0)
        top = sb("top", TT, 8)
        w8 = sb("w8", TT, 8)
        slot_i = sb("slot_i", TT, 8, dt=I32)
        row_i = sb("row_i", TT, 8, dt=I32)
        rmax = sb("rmax", TT)
        rsum = sb("rsum", TT)
        over_p = sb("over_p", 1)
        over_i = sb("over_i", 1, dt=I32)
        list_i = sb("list_i", HC, dt=I32)
        list_f = sb("list_f", HC)
        idx = sb("idx", IDX, dt=I32)
        stage = sb("stage", 32, dt=I32)
        wqks_sb = sb("wqks_sb", 3, KD, P)
        wvg_sb = sb("wvg_sb", KD, 2, D)
        wqks_hi, wqks_lo = (sb(f"wqks_{part}", 3, KD, P, dt=F32R) for part in ("hi", "lo"))
        wvg_hi, wvg_lo = (sb(f"wvg_{part}", KD, 2, D, dt=F32R) for part in ("hi", "lo"))
        wo_raw = sb("wo_raw", 2, D)
        wo_sb = sb("wo_sb", 2, D)
        gnw_sb = sb("gnw_sb", 1)
        kT = sb("kT", T)
        qbd = sb("qbd", TT, 2, P)
        pbd = sb("pbd", TT, 2, P)
        ker = sb("ker", TT, 3, P)
        th = sb("th", 2, HALF)
        masked = sb("masked", 2, 2 * P)
        sk_sb = sb("sk_sb", P)
        sv_sb = sb("sv_sb", D)
        mx = sb("mx", 16)
        sm = sb("sm", 16)
        rs = sb("rs", 16)
        ss = sb("ss", 16)
        pw = sb("pw", 16)
        sc16 = sb("sc16", 16)
        o_n = sb("o_n", TT, D)
        room = sb("room", RING * (WROW + 2 * D))
        wex = room[:, 0:RING * WROW].rearrange("p (r n) -> p r n", r=RING)
        xg = room[:, RING * WROW:RING * (WROW + 2 * D)].rearrange("p (r h d) -> p r h d", r=RING, h=2)
        xgT = sb("xgT", 2, KD, CAP)
        sil_s = sb("sil_s", 2, CAP)
        hT_s = sb("hT_s", 2, CAP)
        yg = room[:, 0:2 * TOP0 * D].rearrange("p (a b d) -> p a b d", a=2, b=TOP0)
        first_use = ExitStack()
        eT = sb("eT", T, stack=first_use)
        eTb = sb("eTb", T, stack=first_use)
        zT = sb("zT", T, stack=first_use)
        rT = sb("rT", T, stack=first_use)
        v_sb = sb("v_sb", TT, D, stack=first_use)
        o_sb = sb("o_sb", TT, D, stack=first_use)
        y_sb = sb("y_sb", 2, 2, D, stack=first_use)
        ok = sb("ok", TT, P, stack=first_use)
        goT = sb("goT", 4, T, stack=first_use)
        gT, oT = goT[:, 0:2, :], goT[:, 2:4, :]
        first_use.close()
        w_hi, w_lo = ([sb(f"w_{part}{b}", T, dt=F32R)[:] for b in range(2)] for part in ("hi", "lo"))
        h_hi, h_lo = (sb(f"h_{part}", 2, HALF, dt=F32R)[:] for part in ("hi", "lo"))
        y_hi, y_lo = (sb(f"y_{part}", KD, T, dt=F32R)[:] for part in ("hi", "lo"))
        pv = ok
        comb1 = chosen[:, :, 0:E1 + SH]
        sil = th
        th_rows = th[:].rearrange("p a t -> p (a t)").rearrange("p (c t) -> p c t", c=TT)
        xn, sclip = o_n, zT
        xnT = v_sb[:].rearrange("p c d -> p (c d)").rearrange("p (k t) -> p k t", k=KD)
        qkv_qk = goT.rearrange("p a t -> p (a t)").rearrange("p (c n) -> p c n", c=TT)
        qkv_v = xg.rearrange("p a b d -> p (a b) d")
        junk_q = o_sb[:]
        junk_k = ker[:].rearrange("p c a t -> p (c a t)")[:, 0:TT * D].rearrange("p (c d) -> p c d", c=TT)
        wqkv_sb = wex[:, 2:4, :].rearrange("p a n -> p (a n)")
        wqkv_v = wqkv_sb.rearrange("p (k n) -> p k n", k=KD)
        thq, thT, wcT = v_sb, gT, oT
        h_f32 = kT[:].rearrange("p (a t) -> p a t", a=2)
        wk, wv = o_sb, o_n
        kvT = qbd[:].rearrange("p (k c) h t -> p k (c h t)", k=KD)
        wcum = pbd[:].rearrange("p (k c) h t -> p k (c h t)", k=KD)
        kvcum = ker[:].rearrange("p c a t -> p (c a t)")[:, 0:KD * T].rearrange("p (k t) -> p k t", k=KD)

        names = """s_x s_c s_pool s_dve s_var s_rstd s_xn s_xT s_xTe s_lg s_sh s_ex s_comb s_gw s_wqks s_wvg s_wo s_wos
            s_gfull s_gD s_gA s_e s_eb s_rT s_sc s_mask s_out s_okD s_oA s_st s_stc s_sub s_pv s_th s_ms s_pw s_on
            s_att s_chosen s_rank s_slot s_xnd s_zero s_scat s_listed s_listf s_lT s_idx s_flag s_flagi
            s_T s_Te s_gus s_sl s_hs s_ys s_ye s_cadd s_w8
            s_qkv s_qkve s_qms s_qpw s_thw s_wvv s_t3 s_t3e s_rqk s_done s_gates s_tick s_wh s_wl s_xh s_xl
            s_yc""".split()
        (s_x, s_c, s_pool, s_dve, s_var, s_rstd, s_xn, s_xT, s_xTe, s_lg, s_sh, s_ex, s_comb, s_gw, s_wqks, s_wvg, s_wo,
         s_wos, s_gfull, s_gD, s_gA, s_e, s_eb, s_rT, s_sc, s_mask, s_out, s_okD, s_oA, s_st, s_stc, s_sub, s_pv, s_th,
         s_ms, s_pw, s_on, s_att, s_chosen, s_rank, s_slot, s_xnd, s_zero, s_scat, s_listed, s_listf, s_lT, s_idx,
         s_flag, s_flagi, s_T, s_Te, s_gus, s_sl, s_hs, s_ys, s_ye, s_cadd, s_w8,
         s_qkv, s_qkve, s_qms, s_qpw, s_thw, s_wvv, s_t3, s_t3e, s_rqk, s_done, s_gates, s_tick, s_wh, s_wl, s_xh, s_xl,
         s_yc) = map(sem, names)
        s_we = [sem(f"s_we{i}") for i in range(RING)]
        s_xg = [sem(f"s_xg{i}") for i in range(RING)]
        s_yst = [sem(f"s_yst{i}") for i in range(2)]
        s_yg = [sem(f"s_yg{i}") for i in range(4)]
        fall, dense = Dense(sem, "fall"), Dense(sem, "dense")

        block = ctx.enter_context(nc.Block())

        def score_bank(pair, m):
            return SC if pair.experts or m % 2 == 0 else XT

        def pair_bodies(eng, body):
            with eng.Fori(0, EXPERT_PAIRS) as j:
                body(Pair(j, 1, experts=True))
            with eng.Fori(0, 2) as j:
                body(Pair(j, 1 + EXPERT_PAIRS, combine=True))
            body(Pair(0, NP - 1))

        @block.sync
        def _(sp):
            sp.dma_start(acc[:], x.rearrange("(c p) d -> p c d", p=P)).then_inc(s_x, 16)
            sp.dma_start(wqks_sb[:], wqks[0]).then_inc(s_wqks, 16)
            sp.dma_start(gate0_sb[:], gate0).then_inc(dense.w[0], 16)
            sp.dma_start(gnw_sb[:], gnw).then_inc(s_gw, 16)
            sp.dma_start(gate1_sb[:], gate1).then_inc(dense.w[1], 16)
            sp.wait_ge(s_c, 9)
            sp.dma_start(listed[0:JUNK, :].rearrange("(a b) o -> a (b o)", a=P), zero_i[:]).then_inc(s_zero, 16)
            sp.dma_start(y_rows[JUNK:JUNK + 1, :], pbd[0:1, 0, :, :].rearrange("p a b -> p (a b)")).then_inc(s_zero, 16)
            sp.wait_ge(s_xn, TT)
            sp.dma_start(xn_rows.rearrange("(c p) d -> p c d", p=P), xn[:]).then_inc(s_xnd, 16)
            for e in range(RING):
                sp.dma_start(wex[:, e, :], w0[e]).then_inc(s_we[e], 16)

            def body(pair):
                if not pair.last:
                    sp.wait_ge(s_wl, pair.at(2, 1))
                    sp.wait_ge(s_wqks, pair.at(16, 16))
                    sp.dma_start(wqks_sb[:], wqks[pair.j + (pair.off + 1)]).then_inc(s_wqks, 16)
                if not pair.first:
                    if pair.last:
                        sp.wait_ge(s_wl, pair.at(2, 0))
                    sp.wait_ge(s_wvg, pair.at(16, 0))
                sp.dma_start(wvg_sb[:], wvg[pair.j + pair.off]).then_inc(s_wvg, 16)
                if not pair.first:
                    sp.wait_ge(s_wos, pair.at(1, 0))
                    sp.wait_ge(s_wo, pair.at(16, 0))
                sp.dma_start(wo_raw[:], wo[pair.j + pair.off]).then_inc(s_wo, 16)
                if pair.experts:
                    j = pair.j
                    for s in range(STEPS):
                        sp.wait_ge(s_ye, j * STEPS + (s + 2))
                        rows = y_rows[bass.ds(j * (STEPS * CAP) + s * CAP, CAP), :]
                        sp.dma_start(rows.rearrange("(h p) d -> p h d", h=2), y_sb[0:HC, s % 2, :, :]).then_inc(s_yst[s % 2], 16)
                        sp.wait_ge(s_we[s % RING], j * 64 + (s // RING + 1) * 16)
                        sp.dma_start(wex[:, s % RING, :], w0[j * STEPS + (s + RING)]).then_inc(s_we[s % RING], 16)

            body(Pair(0, 0))
            sp.wait_ge(s_scat, 16 * TT * TOP0)
            sp.dma_start(list_i[:], listed[0:P * HC, :].rearrange("(r p) o -> r (p o)", p=HC)).then_inc(s_listed, 16)
            pair_bodies(sp, body)

            def dense_loads(dn, w, u0, ne, f):
                with sp.Fori(0, ne // 2) as j:
                    for b in range(2):
                        sp.wait_ge(dn.lo, j * 2 + (u0 // 2 + b + 1))
                        sp.wait_ge(dn.w[b], j * 16 + (u0 // 4 + 1) * 16)
                        sp.dma_start(wex[:, b, 0:4 * f + D], w[j * 2 + b]).then_inc(dn.w[b], 16)

            for e in range(RING):
                sp.wait_ge(s_we[e], 16 * (EP // RING))
            for i in range(4):
                sp.wait_ge(s_yg[i], 16 * TOP0 * TT // 4)
            sp.wait_ge(s_cadd, 1 + TT * TOP0)
            sp.wait_ge(s_flagi, 1)
            over = sp.value_load(over_i[0:1, 0:1], min_val=0, max_val=1)
            with sp.If(over > 0):
                for b in range(2):
                    sp.dma_start(wex[:, b, :], w0[b]).then_inc(fall.w[b], 16)
                    sp.wait_ge(fall.w[b], 16)
                dense_loads(fall, w0, 0, E0, F0)
                sp.wait_ge(fall.acc, 2 + 2 * E0)
            sp.dma_start(wqkv_sb, wqkv.rearrange("p k n -> p (k n)")).then_inc(s_gw, 16)
            dense_loads(dense, w1, 0, E1 + SH, F1)
            dense_loads(dense, wsw, 2 * (E1 + SH), ESW, P)
            sp.wait_ge(dense.acc, 2 + 2 * (E1 + SH + ESW))
            sp.dma_start(out.rearrange("(c p) d -> p c d", p=P), acc[:]).then_inc(s_done, 16)
            sp.wait_ge(s_done, 16)

        @block.gpsimd
        def _(pool):
            g = nc.gpsimd
            g.memset(ident[:], 0.0).then_inc(s_pool, 1)
            g.memset(causal[:], 1.0).then_inc(s_pool, 1)
            g.memset(before_t[:], 1.0).then_inc(s_pool, 1)
            g.memset(idx[:], 0).then_inc(s_c, 1)
            g.memset(ones[:], 1.0).then_inc(s_c, 1)
            g.memset(neg_half[:], -0.5).then_inc(s_c, 1)
            g.memset(qbd[:], 0.0).then_inc(s_c, 1)
            g.memset(pbd[:], 0.0).then_inc(s_c, 1)
            g.memset(zero_i[:], 0).then_inc(s_c, 1)
            g.iota(token_id[:], pattern=[[P, TT]], base=0, channel_multiplier=1).then_inc(s_c, 1)
            g.iota(junk_of[:], pattern=[[1, TT * 8]], base=JUNK + 1, channel_multiplier=TT * 8,
                   allow_small_or_imprecise_dtypes=True).then_inc(s_c, 1)
            g.iota(slot_of[:], pattern=[[CAP, E0]], base=1, channel_multiplier=0,
                   allow_small_or_imprecise_dtypes=True).then_inc(s_c, 1)
            pool.wait_ge(s_pool, 3)
            g.affine_select(out=ident[:], in_=ident[:], compare_op=ALU.not_equal, fill=1.0, base=0,
                            pattern=[[-1, P]], channel_multiplier=1).then_inc(s_c, 1)
            g.affine_select(out=causal[:], in_=causal[:], compare_op=ALU.is_ge, fill=0.0, base=0,
                            pattern=[[0, 2], [1, P]], channel_multiplier=-1).then_inc(s_c, 1)
            g.affine_select(out=before_t[:], in_=before_t[:], compare_op=ALU.is_gt, fill=0.0, base=0,
                            pattern=[[1, P]], channel_multiplier=-1).then_inc(s_c, 1)
            pool.wait_ge(s_c, 12)

            def ln_power(n):
                pool.wait_ge(s_var, n + 1)
                g.tensor_tensor(rstd[:], veps[:], neg_half[:, 0:TT], ALU.pow).then_inc(s_rstd, 1)

            ln_power(0)
            pool.wait_ge(s_gw, 16)
            g.tensor_scalar(gnw_sb[:], gnw_sb[:], 0.5, None, ALU.mult).then_inc(s_gates, 1)
            pool.wait_ge(s_gates, 1)

            def split_lo(raw, hi, lo, made):
                pool.wait_ge(s_wh, made)
                g.tensor_tensor(lo[:], raw[:], hi[:], ALU.subtract).then_inc(s_wl, 1)

            def power(pair):
                pool.wait_ge(s_ms, pair.at(1, 0))
                g.tensor_tensor(pw[:], ss[:], neg_half[:], ALU.pow).then_inc(s_pw, 1)

            def keep_e(pair):
                if not pair.first:
                    pool.wait_ge(s_sc, pair.at(16, 0))
                pool.wait_ge(s_e, pair.at(1, 1))
                pool.sem_inc(s_tick, 1)
                g.tensor_copy(eTb[:], eT[:]).then_inc(s_eb, 1)

            def scale_wo(pair):
                pool.wait_ge(s_gfull, pair.full(pair.use("wo", 3)))
                pool.wait_ge(s_wo, pair.at(16, 16))
                g.tensor_tensor(wo_sb[:], wo_raw[:], gnw_sb[:].unsqueeze(2).broadcast_to([P, 2, D]),
                                ALU.mult).then_inc(s_wos, 1)

            def gather_tokens(slot, col):
                for h in range(2):
                    g.indirect_dma_start(xg[0:HC, slot, h, :], None, xn_rows,
                                         bass.IndirectOffsetOnAxis(ap=stage[0:HC, col + h:col + h + 1], axis=0)
                                         ).then_inc(s_xg[slot], 16)

            def body(pair):
                if pair.first:
                    split_lo(wqks_sb, wqks_hi, wqks_lo, 1)
                    split_lo(wvg_sb, wvg_hi, wvg_lo, 2)
                    split_lo(wqks_sb, wqks_hi, wqks_lo, 3)
                keep_e(pair)
                if pair.first:
                    pool.wait_ge(s_zero, 32)
                    pool.wait_ge(s_slot, 1)
                    for c in range(TT):
                        for k in range(TOP0):
                            g.indirect_dma_start(listed, bass.IndirectOffsetOnAxis(ap=slot_i[:, c, k:k + 1], axis=0),
                                                 token_id[:, c:c + 1], None).then_inc(s_scat, 16)
                    scale_wo(pair)
                    return
                if pair.experts:
                    j = pair.j
                    for slot in range(RING):
                        pool.wait_ge(s_xg[slot], j * 128 + (64 if slot == 0 else 32))
                    pool.sem_inc(s_tick, 1)
                    g.tensor_copy(stage[:], idx[:, bass.ds(j * 32 + 2 * (RING + 1), 32)]).then_inc(s_idx, 1)
                    pool.wait_ge(s_idx, j + 3)
                for s in range(STEPS):
                    if pair.experts:
                        slot = (s + 1) % RING
                        pool.wait_ge(s_T, pair.j * STEPS + (s + 2))
                        pool.sem_inc(s_tick, 1)
                        gather_tokens(slot, 2 * s)
                    if s == 3:
                        split_lo(wvg_sb, wvg_hi, wvg_lo, pair.at(2, 2))
                    if s == 5 and not pair.last:
                        split_lo(wqks_sb, wqks_hi, wqks_lo, pair.at(2, 3))
                    if s == TT - 1:
                        power(pair)
                scale_wo(pair)

            def combine_body(pair):
                j = pair.j
                keep_e(pair)
                pool.wait_ge(s_cadd, j * 32 + 1)
                pool.sem_inc(s_tick, 1)
                g.tensor_copy(stage[:].rearrange("p (a b) -> p a b", b=8), row_i[:, bass.ds(j * 4, 4), :]).then_inc(s_idx, 1)
                pool.wait_ge(s_idx, j + 3 + EXPERT_PAIRS)
                pool.sem_inc(s_tick, 1)
                for q in range(4):
                    for k in range(TOP0):
                        if q >= 2 and k % 4 == 0:
                            pool.wait_ge(s_cadd, j * 32 + (TOP0 * (q - 2) + k + 5))
                            pool.sem_inc(s_tick, 1)
                        g.indirect_dma_start(yg[:, q % 2, k, :], None, y_rows,
                                             bass.IndirectOffsetOnAxis(ap=stage[:, 8 * q + k:8 * q + k + 1], axis=0)
                                             ).then_inc(s_yg[2 * (q % 2) + k // 4], 16)
                    if q == 0:
                        split_lo(wvg_sb, wvg_hi, wvg_lo, pair.at(2, 2))
                        split_lo(wqks_sb, wqks_hi, wqks_lo, pair.at(2, 3))
                        power(pair)
                scale_wo(pair)

            body(Pair(0, 0))
            pool.wait_ge(s_idx, 1)
            g.tensor_copy(stage[:], idx[:, 0:32]).then_inc(s_idx, 1)
            pool.wait_ge(s_idx, 2)
            pool.wait_ge(s_xnd, 16)
            for e in range(RING + 1):
                if e == RING:
                    pool.wait_ge(s_T, 1)
                    pool.wait_ge(s_xg[0], 32)
                gather_tokens(e % RING, 2 * e)
            pool.wait_ge(s_xg[0], 64)
            with pool.Fori(0, EXPERT_PAIRS) as j:
                body(Pair(j, 1, experts=True))
            for slot in range(RING):
                pool.wait_ge(s_xg[slot], 32 * (STEPS + 1 + (slot == 0)))
            pool.wait_ge(s_ye, 1 + E0)
            pool.wait_ge(s_gus, 1 + E0)
            pool.wait_ge(s_T, 2 + E0)
            for e in range(RING):
                pool.wait_ge(s_we[e], 16 * (EP // RING))
            pool.wait_ge(s_yst[0], 16 * (E0 // 2 + 1))
            pool.wait_ge(s_yst[1], 16 * (E0 // 2 + 1))
            with pool.Fori(0, 2) as j:
                combine_body(Pair(j, 1 + EXPERT_PAIRS, combine=True))
            body(Pair(0, NP - 1))
            pool.wait_ge(s_ms, NP)
            g.tensor_tensor(pw[:], ss[:], neg_half[:], ALU.pow).then_inc(s_pw, 1)

            def split_weights(dn, u0, ne, f):
                with pool.Fori(0, ne // 2) as j:
                    for b in range(2):
                        pool.wait_ge(dn.hi, j * 2 + (u0 // 2 + b + 1))
                        n = 4 * f + D
                        g.tensor_tensor(w_lo[b][:, 0:n], wex[:, b, 0:n], w_hi[b][:, 0:n], ALU.subtract).then_inc(dn.lo, 1)

            pool.sem_inc(fall.lo, 2)
            pool.sem_inc(dense.lo, 2)
            pool.wait_ge(s_att, 1)
            over = pool.value_load(over_i[0:1, 0:1], min_val=0, max_val=1)
            with pool.If(over > 0):
                split_weights(fall, 0, E0, F0)
            for k in range(KD):
                pool.wait_ge(s_wh, 2 * NP + k + 1)
                g.tensor_tensor(w_lo[k][:, 0:3 * D], wqkv_v[:, k, :], w_hi[k][:, 0:3 * D], ALU.subtract).then_inc(s_wl, 1)
            ln_power(1)
            ln_power(2)
            pool.wait_ge(s_qms, 1)
            g.tensor_tensor(pw[:], ss[:], neg_half[:], ALU.pow).then_inc(s_qpw, 1)
            split_weights(dense, 0, E1 + SH, F1)
            split_weights(dense, 2 * (E1 + SH), ESW, P)

        @block.tensor
        def _(pe):
            mm = nc.tensor.matmul
            tr = nc.tensor.transpose
            pe.wait_ge(s_c, 12)
            pe.sem_inc(dense.y, 3)
            pe.sem_inc(s_ys, 1)

            def transposed_tokens(n):
                for i in range(4):
                    pe.wait_ge(s_xn, n * TT + 2 * i + 2)
                    for c in range(2):
                        for k in range(KD):
                            o = (c * KD + k) * P
                            last = tr(bank[4 + i][:, o:o + P], xn[:, 2 * i + c, k * P:(k + 1) * P], ident[:])
                    last.then_inc(s_xT, 1)

            def logits(n, gate, ne):
                pe.wait_ge(s_xTe, 4 * n + 4)
                for c in range(TT):
                    for k in range(KD):
                        last = mm(bank[3][:, c * ne:(c + 1) * ne], xnT[:, k, c * P:(c + 1) * P], gate[:, k, :],
                                  start=k == 0, stop=k == KD - 1)
                last.then_inc(s_lg, 1)
                pe.wait_ge(s_xh, 4 * n + 4)

            def g_free(pair, n):
                if n >= 2:
                    who, value = pair.taken(n - 2)
                    pe.wait_ge(s_gD if who == "D" else s_gA, value)
                else:
                    pe.wait_ge(s_gD, pair.at(NGD, PRO_D - 1 + n))

            def split_product(o, terms):
                for i, (lhs, rhs) in enumerate(terms):
                    last = mm(o, lhs, rhs, start=i == 0, stop=i == len(terms) - 1)
                return last

            def project_sqk(i, hf, bk):
                half = slice(hf * HALF, (hf + 1) * HALF)
                last = split_product(bk[:], [((wqks_hi, wqks_lo)[a][:, i, k, :], (xT_hi, xT_lo)[b][:, k, half])
                                             for a, b in PASSES for k in range(KD)])
                last.then_inc(s_gfull, 1)

            transposed_tokens(0)
            pe.wait_ge(dense.w[0], 16)
            pe.wait_ge(dense.w[1], 16)
            logits(0, gate0_sb, E0)
            pe.wait_ge(s_wl, 1)
            pe.wait_ge(s_xl, 4)
            for n in range(PRO):
                if n >= 4:
                    pe.wait_ge(s_gA, n - 3)
                elif n >= 2:
                    pe.wait_ge(s_gD, n - 1)
                project_sqk(n // 2, n % 2, G[n % 2])
            pe.wait_ge(s_chosen, 1)
            for c in range(TT):
                for b in range(c + 1):
                    last = mm(bank[7][:, c * E0:(c + 1) * E0], before_t[:] if b == c else ones[:, 0:P],
                              chosen[:, b, :], start=b == 0, stop=b == c)
            last.then_inc(s_rank, 1)
            pe.wait_ge(s_flag, 1)
            mm(bank[6][0:1, 0:1], over_p[:, 0:1], ones[:, 0:1], start=True, stop=True).then_inc(s_flag, 1)
            pe.wait_ge(s_sh, 1)

            def tokens_T(slot, xg_count, par, te):
                pe.wait_ge(s_xg[slot], xg_count)
                if te is not None:
                    pe.wait_ge(s_Te, te)
                for h in range(2):
                    for k in range(KD):
                        o = k * CAP + h * HC
                        last = tr(XT[:, o:o + HC], xg[0:HC, slot, h, k * P:(k + 1) * P], ident[0:HC, 0:HC])
                last.then_inc(s_T, 1)

            def gate_up_s(slot, w_count, par, te, free):
                pe.wait_ge(s_we[slot], w_count)
                pe.wait_ge(s_Te, te)
                if free is not None:
                    pe.wait_ge(s_hs, free)
                for gu in range(2):
                    for k in range(KD):
                        w = (gu * KD + k) * P
                        last = mm(GU[:, gu * CAP:(gu + 1) * CAP], wex[:, slot, w:w + P], xgT[:, par, k, :],
                                  start=k == 0, stop=k == KD - 1)
                last.then_inc(s_gus, 1)

            def output_product(pair, ot, wo_name):
                end = 1 if ot == "oT_end" else 0
                pe.wait_ge(s_on, pair.at(1, end))
                for i in range(4):
                    n = pair.use(ot, i)
                    g_free(pair, n)
                    for c in range(2):
                        for h in range(2):
                            o = (h * 2 + c) * P
                            last = tr(G[n % 2][:, o:o + P], o_n[:, 2 * i + c, h * P:(h + 1) * P], ident[:])
                    last.then_inc(s_gfull, 1)
                pe.wait_ge(s_wos, pair.at(1, end))
                for i in range(4):
                    n = pair.use(wo_name, i)
                    g_free(pair, n)
                    pe.wait_ge(s_gD, pair.taken(pair.use(ot, i))[1])
                    for c in range(2):
                        for h in range(2):
                            t = (2 * i + c) * P
                            last = mm(G[n % 2][:, c * D:(c + 1) * D], oT[:, h, t:t + P], wo_sb[:, h, :],
                                      start=h == 0, stop=h == 1)
                    last.then_inc(s_gfull, 1)

            def body(pair):
                j = pair.j
                pe.wait_ge(s_gA, pair.at(NGA, PRO_A))
                pe.wait_ge(s_gD, pair.at(NGD, PRO_D))
                for c in range(TT):
                    n = pair.use("tr", c)
                    pe.wait_ge(s_rT, pair.at(TT, c + 1))
                    g_free(pair, n)
                    for i, src in enumerate((kT, eT, rT)):
                        last = tr(G[n % 2][:, i * P:(i + 1) * P], src[:, c * P:(c + 1) * P], ident[:])
                    last.then_inc(s_gfull, 1)

                def scores(m, lhs, rhs):
                    before = m if pair.experts else m - 1
                    if not (pair.first and before <= 0):
                        pe.wait_ge(s_mask, pair.at(16, before))
                    if m == 0 and not pair.first and not pair.experts:
                        pe.wait_ge(s_Te, E0 + 2)
                    mm(score_bank(pair, m)[:, 0:2 * P], lhs, rhs, start=True, stop=True).then_inc(s_sc, 1)

                def out_free(m):
                    if m == 0:
                        if not pair.first:
                            pe.wait_ge(s_oA, pair.at(8, 0))
                    elif m <= 8:
                        pe.wait_ge(s_okD, pair.at(8, m))
                    else:
                        pe.wait_ge(s_oA, pair.at(8, m - 8))

                def expert_front(s):
                    tokens_T((s + 2) % RING, j * 128 + ((s + 2) // RING + 1) * 32, s % 2, j * STEPS + (s + 2))

                def expert_back(s):
                    b, par = (s + 1) % RING, s % 2
                    pe.wait_ge(s_hs, j * STEPS + (s + 2))
                    pe.wait_ge(s_ye, j * STEPS + (s + 1))
                    for h in range(2):
                        last = mm(YB[0:HC, h * D:(h + 1) * D], hT_s[:, par, h * HC:(h + 1) * HC],
                                  wex[:, s % RING, 4 * P:4 * P + D], start=True, stop=True)
                    last.then_inc(s_ys, 1)
                    gate_up_s(b, j * 64 + ((s + 1) // RING + 1) * 16, (s + 1) % 2, j * STEPS + (s + 2), j * STEPS + (s + 2))

                def sc_a(c):
                    scores(c, kT[:, c * P:(c + 1) * P], qbd[:, c, :, :])
                sc_a(0)
                for c in range(TT):
                    if pair.experts:
                        expert_front(c)
                    if c < TT - 1:
                        sc_a(c + 1)
                    out_free(c)
                    pe.wait_ge(s_mask, pair.at(16, c + 1))
                    who, value = pair.taken(pair.use("tr", c))
                    pe.wait_ge(s_gA, value)
                    if c:
                        pe.wait_ge(s_stc, pair.at(14, c))
                    for h in range(2):
                        o = OUT[:, h * 64:(h + 1) * 64]
                        last = mm(o, masked[:, c % 2, h * P:(h + 1) * P], ker[:, c, 1, h * 64:(h + 1) * 64],
                                  start=True, stop=c == 0)
                        if c:
                            last = mm(o, qbd[:, c, h, :], sk_sb[:, h * 64:(h + 1) * 64], start=False, stop=True)
                    last.then_inc(s_out, 1)
                    if c < TT - 1:
                        mm(ST[:, 0:P], ker[:, c, 0, :], ker[:, c, 1, :], start=c == 0, stop=True,
                           skip_group_check=True).then_inc(s_st, 1)
                    if pair.experts:
                        expert_back(c)

                pe.wait_ge(s_wl, pair.at(2, 2))
                for i in range(4):
                    n = pair.use("v", i)
                    g_free(pair, n)
                    for c in range(2):
                        t = (2 * i + c) * P
                        last = split_product(G[n % 2][:, c * D:(c + 1) * D],
                                             [((xT_hi, xT_lo)[a][:, k, t:t + P], (wvg_hi, wvg_lo)[b][:, k, 0, :])
                                              for a, b in PASSES for k in range(KD)])
                    last.then_inc(s_gfull, 1)
                if not pair.last:
                    pe.wait_ge(s_wl, pair.at(2, 3))
                    for i, name in enumerate(("s", "k", "q")):
                        for hf in range(2):
                            n = pair.use(name, hf)
                            g_free(pair, n)
                            project_sqk(i, hf, G[n % 2])
                pe.wait_ge(s_pv, pair.at(1, 1))
                for i in range(2):
                    n = pair.use("pvT", i)
                    g_free(pair, n)
                    for c in range(4):
                        last = tr(G[n % 2][:, c * P:(c + 1) * P], pv[:, 4 * i + c, :], ident[:])
                    last.then_inc(s_gfull, 1)
                if pair.first:
                    for n in range(pair.use("oT"), pair.use("g")):
                        g_free(pair, n)
                        tr(G[n % 2][:, 0:P], ident[:], ident[:]).then_inc(s_gfull, 1)
                else:
                    output_product(pair, "oT", "wo")
                for i in range(4):
                    n = pair.use("g", i)
                    h, hf = i // 2, i % 2
                    g_free(pair, n)
                    half = slice(hf * HALF, (hf + 1) * HALF)
                    last = split_product(G[n % 2][:], [((wvg_hi, wvg_lo)[a][:, k, 1, h * P:(h + 1) * P],
                                                        (xT_hi, xT_lo)[b][:, k, half])
                                                       for a, b in PASSES for k in range(KD)])
                    last.then_inc(s_gfull, 1)

                pe.wait_ge(s_gD, pair.taken(pair.use("pvT", 1))[1])
                pe.wait_ge(s_eb, pair.at(1, 1))

                def sc_b(c):
                    scores(8 + c, eTb[:, c * P:(c + 1) * P], pbd[:, c, :, :])
                sc_b(0)
                for c in range(TT):
                    if pair.experts:
                        expert_front(8 + c)
                    if c < TT - 1:
                        sc_b(c + 1)
                    out_free(8 + c)
                    pe.wait_ge(s_mask, pair.at(16, c + 9))
                    if c:
                        pe.wait_ge(s_stc, pair.at(14, 7 + c))
                    for h in range(2):
                        o = OUT[:, h * P:(h + 1) * P]
                        last = mm(o, masked[:, c % 2, h * P:(h + 1) * P], v_sb[:, c, h * P:(h + 1) * P],
                                  start=True, stop=c == 0)
                        if c:
                            last = mm(o, pbd[:, c, h, :], sv_sb[:, h * P:(h + 1) * P], start=False, stop=True)
                    last.then_inc(s_out, 1)
                    if c < TT - 1:
                        mm(ST[:, 0:D], ker[:, c, 1, :], v_sb[:, c, :], start=c == 0, stop=True,
                           skip_group_check=True).then_inc(s_st, 1)
                    if pair.experts:
                        expert_back(8 + c)
                if pair.last:
                    output_product(pair, "oT_end", "wo_end")

            body(Pair(0, 0))
            pe.wait_ge(s_listf, 1)
            tr(YB[0:HC, 0:P], list_f[:], ident[:]).then_inc(s_lT, 1)
            tokens_T(0, 32, 0, None)
            gate_up_s(0, 16, 0, 1, None)
            tokens_T(1, 32, 1, 1)
            pe.wait_ge(s_idx, 1)
            pair_bodies(pe, body)

            def dense_pass(dn, tok_hi, tok_lo, u0, ne, f):
                def gate_up(j, u, b, hf):
                    pe.wait_ge(dn.h, j * 4 + (u0 + u + 1))
                    if hf == 0:
                        pe.wait_ge(dn.lo, j * 2 + ((u0 + u) // 2 + 3))
                    q = (u % 2) * 2
                    half = slice(hf * HALF, (hf + 1) * HALF)
                    terms = [(w, t, k) for w, t in ((w_lo[b], tok_hi), (w_hi[b], tok_lo), (w_hi[b], tok_hi))
                             for k in range(KD)]
                    for gu in range(2):
                        for i, (w, t, k) in enumerate(terms):
                            o = (gu * KD + k) * f
                            last = mm(bank[q + gu][0:f, :], w[:, o:o + f], t[:, k, half],
                                      start=i == 0, stop=i == len(terms) - 1)
                    last.then_inc(dn.gu, 1)

                def down(j, u, b):
                    pe.wait_ge(dn.h, j * 4 + (u0 + u + 3))
                    pe.wait_ge(dn.acc, j * 4 + (u0 + u + 1))
                    terms = ((h_lo, w_hi[b]), (h_hi, w_lo[b]), (h_hi, w_hi[b]))
                    for c in range(4):
                        yb = bank[4 + (u % 2) * 2 + c // 2]
                        for i, (h, w) in enumerate(terms):
                            last = mm(yb[:, (c % 2) * D:(c % 2 + 1) * D], h[0:f, u % 2, c * P:(c + 1) * P],
                                      w[0:f, 4 * f:4 * f + D], start=i == 0, stop=i == len(terms) - 1)
                    last.then_inc(dn.y, 1)

                gate_up(0, 0, 0, 0)

                def units(j, last):
                    for u in range(4):
                        if u < 3:
                            gate_up(j, u + 1, (u + 1) // 2, (u + 1) % 2)
                        elif not last:
                            gate_up(j, 4, 0, 0)
                        down(j, u, u // 2)
                with pe.Fori(0, ne // 2 - 1) as j:
                    units(j, False)
                units(ne // 2 - 1, True)

            pe.wait_ge(s_att, 1)
            over = pe.value_load(over_i[0:1, 0:1], min_val=0, max_val=1)
            with pe.If(over > 0):
                pe.sem_inc(fall.y, 3)
                dense_pass(fall, xT_hi, xT_lo, 0, E0, F0)

            transposed_tokens(1)
            logits(1, gate1_sb, E1)
            pe.wait_ge(s_wl, 2 * NP + KD)
            pe.wait_ge(s_xl, 8)
            for c in range(TT):
                b0, b1 = (0, 1) if c % 2 == 0 else (2, 7)
                if c >= 2:
                    pe.wait_ge(s_qkve, c - 1)
                for o, cols in ((bank[b0][:], slice(0, 2 * D)), (bank[b1][:, 0:D], slice(2 * D, 3 * D))):
                    last = split_product(o, [((xT_hi, xT_lo)[a][:, k, c * P:(c + 1) * P], (w_hi, w_lo)[b][k][:, cols])
                                             for a, b in PASSES for k in range(KD)])
                last.then_inc(s_qkv, 1)
            for i, (src, made) in enumerate(((thq, s_thw), (wk, s_thw), (wv, s_wvv))):
                if i == 0:
                    pe.wait_ge(s_qkve, TT)
                for q in range(4):
                    pe.wait_ge(made, (2 * q + 2, 2 * q + 10, q + 1)[i])
                    n = 4 * i + q
                    if n >= 4:
                        pe.wait_ge(s_t3e, n - 3)
                    for k in range(KD):
                        for c in range(2):
                            o = (k * 2 + c) * P
                            last = tr(bank[n % 4][:, o:o + P], src[:, 2 * q + c, k * P:(k + 1) * P], ident[:])
                    last.then_inc(s_t3, 1)
            pe.wait_ge(s_t3e, 12)
            pe.wait_ge(s_comb, 1)
            dense_pass(dense, xT_hi, xT_lo, 0, E1 + SH, F1)
            pe.wait_ge(s_yc, 1 + 5 * ((E1 + SH) // 2 - 1))
            dense_pass(dense, y_hi, y_lo, 2 * (E1 + SH), ESW, P)

        @block.scalar
        def _(act):
            A = nc.scalar.activation
            copy = nc.scalar.copy

            def transposed_tokens(n):
                for i in range(4):
                    act.wait_ge(s_xT, 4 * n + i + 1)
                    made = bank[4 + i][:].rearrange("p (c k t) -> p k c t", c=2, k=KD)
                    for dst, done in ((xnT, s_xTe), (xT_hi, s_xh)):
                        copy(dst[:, :, 2 * i * P:(2 * i + 2) * P].rearrange("p k (c t) -> p k c t", c=2),
                             made).then_inc(done, 1)

            act.wait_ge(s_wqks, 16)
            copy(wqks_hi[:], wqks_sb[:]).then_inc(s_wh, 1)
            transposed_tokens(0)
            act.wait_ge(s_sh, 1)
            A(prob[:], left[:], ACT.Exp).then_inc(s_ex, 1)
            act.wait_ge(s_gD, 2)
            A(eT[:], sclip[:], ACT.Exp).then_inc(s_e, 1)
            for hf in range(2):
                act.wait_ge(s_gfull, 3 + hf)
                copy(kT[:, hf * HALF:(hf + 1) * HALF], G[hf][:]).then_inc(s_gA, 1)
            act.wait_ge(s_wvg, 16)
            copy(wvg_hi[:], wvg_sb[:]).then_inc(s_wh, 1)
            act.wait_ge(s_gfull, PRO)
            act.wait_ge(s_wqks, 32)
            copy(wqks_hi[:], wqks_sb[:]).then_inc(s_wh, 1)

            def tokens_copied(par, t, free):
                act.wait_ge(s_T, t)
                if free is not None:
                    act.wait_ge(s_gus, free)
                copy(xgT[:, par, :, :], XT[:, 0:KD * CAP].rearrange("p (k t) -> p k t", k=KD)).then_inc(s_Te, 1)

            def silu_s(par, gu, free):
                act.wait_ge(s_gus, gu)
                if free is not None:
                    act.wait_ge(s_hs, free)
                A(sil_s[:, par, :], GU[:, 0:CAP], ACT.Tanh, scale=0.5).then_inc(s_sl, 1)

            def body(pair):
                j = pair.j
                for c in range(TT):
                    n = pair.use("tr", c)
                    act.wait_ge(s_gfull, pair.full(n))
                    copy(ker[:, c, :, :], G[n % 2][:, 0:3 * P].rearrange("p (a b) -> p a b", a=3)).then_inc(s_gA, 1)

                def state(m, dst, src):
                    act.wait_ge(s_st, pair.at(14, m + 1))
                    copy(dst, src).then_inc(s_stc, 1)

                def expert_front(s):
                    tokens_copied(s % 2, j * STEPS + (s + 3), j * STEPS + (s + 1))

                def expert_back(s):
                    silu_s((s + 1) % 2, j * STEPS + (s + 2), j * STEPS + (s + 1))

                for c in range(TT):
                    if pair.experts:
                        expert_front(c)
                    if c < TT - 1:
                        state(c, sk_sb[:], ST[:, 0:P])
                    if c == 1 and not pair.first:
                        act.wait_ge(s_gfull, pair.at(NG, PRO))
                        act.wait_ge(s_wvg, pair.at(16, 16))
                        copy(wvg_hi[:], wvg_sb[:]).then_inc(s_wh, 1)
                    if c == 3 and not (pair.first or pair.last):
                        act.wait_ge(s_wqks, pair.at(16, 32))
                        copy(wqks_hi[:], wqks_sb[:]).then_inc(s_wh, 1)
                    if pair.experts:
                        expert_back(c)
                for i in range(4):
                    n = pair.use("v", i)
                    act.wait_ge(s_gfull, pair.full(n))
                    copy(v_sb[:, 2 * i:2 * i + 2, :], G[n % 2][:].rearrange("p (a b) -> p a b", a=2)).then_inc(s_gA, 1)
                act.wait_ge(s_sub, pair.at(1, 1))
                A(pv[:], ok[:], ACT.Exp).then_inc(s_pv, 1)
                if not pair.last:
                    for hf in range(2):
                        n = pair.use("k", hf)
                        act.wait_ge(s_gfull, pair.full(n))
                        copy(kT[:, hf * HALF:(hf + 1) * HALF], G[n % 2][:]).then_inc(s_gA, 1)
                    act.wait_ge(s_gD, pair.taken(pair.use("s", 1))[1])
                    act.wait_ge(s_eb, pair.at(1, 1))
                    A(eT[:], sclip[:], ACT.Exp).then_inc(s_e, 1)
                for i in range(4):
                    n = pair.use("g", i)
                    act.wait_ge(s_gfull, pair.full(n))
                    if i >= 2:
                        act.wait_ge(s_gD, pair.taken(n - 2)[1])
                    A(th[:, i % 2, :], G[n % 2][:], ACT.Tanh, scale=0.5).then_inc(s_th, 1)
                for c in range(TT):
                    if pair.experts:
                        expert_front(8 + c)
                    act.wait_ge(s_out, pair.at(16, 9 + c))
                    if c == 0:
                        act.wait_ge(s_gD, pair.taken(pair.use("g", 3))[1])
                    if c == 0 and not pair.first:
                        act.wait_ge(s_on, pair.at(1, 0))
                    copy(o_sb[:, c, :], OUT[:, 0:D])
                    A(ok[:, c, :], OUT[:, 0:P], ACT.Square, accum_out=ss[:, 2 * c:2 * c + 1])
                    A(th_rows[:, c, :], OUT[:, P:2 * P], ACT.Square,
                      accum_out=ss[:, 2 * c + 1:2 * c + 2]).then_inc(s_oA, 1)
                    if c < TT - 1:
                        state(7 + c, sv_sb[:], ST[:, 0:D])
                    if pair.experts:
                        expert_back(8 + c)

            body(Pair(0, 0))
            tokens_copied(0, 1, None)
            silu_s(0, 1, None)
            tokens_copied(1, 2, None)
            pair_bodies(act, body)

            def weights_hi(dn, u0, f, j, e):
                act.wait_ge(dn.w[e % 2], j * 16 + (u0 // 4 + e // 2 + 2) * 16)
                act.wait_ge(dn.y, j * 4 + (u0 + 2 * e + 1))
                n = 4 * f + D
                copy(w_hi[e % 2][:, 0:n], wex[:, e % 2, 0:n]).then_inc(dn.hi, 1)

            def dense_pass(dn, u0, ne, f):
                def units(j, last):
                    for u in range(4):
                        act.wait_ge(dn.gu, j * 4 + (u0 + u + 1))
                        act.wait_ge(dn.h, j * 4 + (u0 + u + 1))
                        A(sil[0:f, u % 2, :], bank[(u % 2) * 2][0:f, :], ACT.Silu).then_inc(dn.sil, 1)
                        if u == 0 or (u == 2 and not last):
                            weights_hi(dn, u0, f, j, u // 2 + 1)

                with act.Fori(0, ne // 2 - 1) as j:
                    units(j, False)
                units(ne // 2 - 1, True)

            act.wait_ge(s_att, 1)
            over = act.value_load(over_i[0:1, 0:1], min_val=0, max_val=1)
            with act.If(over > 0):
                weights_hi(fall, 0, F0, 0, 0)
                dense_pass(fall, 0, E0, F0)
            act.wait_ge(s_gw, 32)
            for k in range(KD):
                copy(w_hi[k][:, 0:3 * D], wqkv_v[:, k, :]).then_inc(s_wh, 1)
            transposed_tokens(1)
            act.wait_ge(s_lg, 2)
            A(prob[:, :, 0:E1], bank[3][:, 0:TT * E1].rearrange("p (c e) -> p c e", c=TT), ACT.Sigmoid).then_inc(s_ex, 1)
            for c in range(TT):
                b0, b1 = (0, 1) if c % 2 == 0 else (2, 7)
                act.wait_ge(s_qkv, c + 1)
                if c == 0:
                    act.wait_ge(s_rstd, 3)
                A(qkv_qk[:, c, :], bank[b0][:], ACT.Copy, scale=rstd[:, c:c + 1])
                for i, junk in enumerate((junk_q, junk_k)):
                    A(junk[:, c, :], bank[b0][:, i * D:(i + 1) * D], ACT.Square, scale=rstd[:, c:c + 1],
                      accum_out=ss[:, 2 * c + i:2 * c + i + 1])
                A(qkv_v[:, c, :], bank[b1][:, 0:D], ACT.Copy, scale=rstd[:, c:c + 1]).then_inc(s_qkve, 1)
            weights_hi(dense, 0, F1, 0, 0)
            act.wait_ge(s_rqk, 1)
            for c in range(TT):
                A(thq[:, c, :], qkv_qk[:, c, 0:D], ACT.Tanh, scale=rs[:, c:c + 1]).then_inc(s_thw, 1)
            for c in range(TT):
                A(wk[:, c, :], qkv_qk[:, c, D:2 * D], ACT.Exp, scale=rs[:, TT + c:TT + c + 1]).then_inc(s_thw, 1)
            act.wait_ge(s_thw, 2 * TT)
            for i, dst in enumerate((thT, wcT, kvT)):
                for q in range(4):
                    n = 4 * i + q
                    act.wait_ge(s_t3, n + 1)
                    copy(dst[:, :, 2 * q * P:(2 * q + 2) * P],
                         bank[n % 4][:].rearrange("p (k t) -> p k t", k=KD)).then_inc(s_t3e, 1)
            dense_pass(dense, 0, E1 + SH, F1)
            weights_hi(dense, 2 * (E1 + SH), P, 0, 0)
            dense_pass(dense, 2 * (E1 + SH), ESW, P)

        @block.vector
        def _(dve):
            V = nc.vector
            links = {"base": 0, "n": 0}

            def link(ins):
                links["n"] += 1
                ins.then_inc(s_dve, 1)
                dve.wait_ge(s_dve, links["base"] + links["n"])

            def wide(col, n):
                return col.unsqueeze(2).broadcast_to([P, col.shape[1], n])

            dve.sem_inc(s_hs, 1)
            dve.sem_inc(s_ye, 1)
            dve.sem_inc(s_cadd, 1)
            dve.sem_inc(s_yst[0], 16)
            dve.sem_inc(s_yst[1], 16)

            def layernorm(n):
                for c in range(TT):
                    last = V.bn_stats(stats[:, c, :], acc[:, c, :])
                link(last)
                for c in range(TT):
                    last = V.bn_aggr(mv[:, c, :], stats[:, c, :])
                link(last)
                V.tensor_scalar(veps[:], mv[:, :, 1], EPS_LN, None, ALU.add).then_inc(s_var, 1)
                dve.wait_ge(s_rstd, n + 1)
                for c in range(TT):
                    V.tensor_scalar(xn[:, c, :], acc[:, c, :], mv[:, c, 0:1], rstd[:, c:c + 1],
                                    ALU.subtract, ALU.mult).then_inc(s_xn, 1)

            def split_tokens(n):
                for i in range(4):
                    dve.wait_ge(s_xh, 4 * n + i + 1)
                    cols = slice(2 * i * P, (2 * i + 2) * P)
                    V.tensor_tensor(xT_lo[:, :, cols], xnT[:, :, cols], xT_hi[:, :, cols], ALU.subtract).then_inc(s_xl, 1)

            dve.wait_ge(s_x, 16)
            layernorm(0)
            split_tokens(0)

            dve.wait_ge(s_lg, 1)
            lg = bank[3][:].rearrange("p (c e) -> p c e", c=TT)
            link(V.tensor_reduce(rmax[:], lg, AX, ALU.max))
            V.tensor_tensor(left[:], lg, wide(rmax[:], E0), ALU.subtract).then_inc(s_sh, 1)

            def clip_s(wait, bk, hf):
                dve.wait_ge(s_gfull, wait)
                V.tensor_scalar(sclip[:, hf * HALF:(hf + 1) * HALF], bk[:], 32.0, -32.0,
                                ALU.min, ALU.max).then_inc(s_gD, 1)

            def place_q(wait, bk, hf):
                dve.wait_ge(s_gfull, wait)
                for h in range(2):
                    r = slice(64 * h, 64 * h + 64)
                    last = V.tensor_scalar(qbd[r, 4 * hf:4 * hf + 4, h, :],
                                           bk[r, :].rearrange("p (c t) -> p c t", c=4), 0.125, None, ALU.mult)
                last.then_inc(s_gD, 1)

            def running_sum():
                link(V.tensor_tensor_scan(zT[:], ones[:], eT[:], 0.0, ALU.mult, ALU.add))

            def reciprocal_z(c):
                V.reciprocal(rT[:, c * P:(c + 1) * P], zT[:, c * P:(c + 1) * P]).then_inc(s_rT, 1)

            dve.wait_ge(s_c, 12)
            for hf in range(2):
                clip_s(1 + hf, G[hf], hf)
            for hf in range(2):
                place_q(5 + hf, G[hf], hf)
            dve.wait_ge(s_ex, 1)
            link(V.tensor_reduce(rsum[:], prob[:], AX, ALU.add))
            link(V.reciprocal(rsum[:], rsum[:]))
            link(V.tensor_tensor(prob[:], prob[:], wide(rsum[:], E0), ALU.mult))
            for c in range(TT):
                last = V.max(top[:, c, :], prob[:, c, :])
            link(last)
            for c in range(TT):
                last = V.match_replace(left[:, c, :], top[:, c, :], prob[:, c, :], -1.0)
            link(last)
            V.tensor_scalar(chosen[:], left[:], 0.0, None, ALU.is_lt).then_inc(s_chosen, 1)
            dve.wait_ge(s_chosen, 1)
            link(V.tensor_tensor(comb0[:], prob[:], chosen[:], ALU.mult))
            dve.wait_ge(s_rank, 1)
            rank = bank[7][:].rearrange("p (c e) -> p c e", c=TT)
            link(V.tensor_scalar(fits[:], rank, float(CAP), None, ALU.is_lt))
            link(V.tensor_tensor(prob[:], comb0[:], fits[:], ALU.mult))
            link(V.tensor_tensor(over0[:], comb0[:], prob[:], ALU.subtract))
            link(V.tensor_tensor(left[:], rank, slot_of[:].unsqueeze(1).broadcast_to([P, TT, E0]), ALU.add))
            link(V.tensor_tensor(left[:], left[:], chosen[:], ALU.mult))
            link(V.tensor_tensor(comb0[:], chosen[:], fits[:], ALU.mult))
            link(V.tensor_tensor(left[:], left[:], comb0[:], ALU.mult))
            link(V.tensor_tensor(comb0[:], chosen[:], comb0[:], ALU.subtract))
            V.tensor_reduce(over_p[:], comb0[:].rearrange("p c e -> p (c e)"), AX, ALU.max).then_inc(s_flag, 1)
            for c in range(TT):
                last = V.max(top[:, c, :], left[:, c, :])
            link(last)
            link(V.scalar_tensor_tensor(w8[:], top[:], 0.0, junk_of[:], ALU.is_equal, ALU.mult))
            link(V.scalar_tensor_tensor(w8[:], top[:], -1.0, w8[:], ALU.add, ALU.add))
            V.tensor_scalar(row_i[:], w8[:], float(JUNK), None, ALU.min)
            V.tensor_copy(slot_i[:], w8[:]).then_inc(s_slot, 1)
            dve.wait_ge(s_e, 1)
            running_sum()
            for c in range(TT):
                reciprocal_z(c)
            dve.wait_ge(s_slot, 1)
            dve.wait_ge(s_zero, 32)
            dve.wait_ge(s_flag, 2)
            V.tensor_scalar(over_i[0:1, 0:1], bank[6][0:1, 0:1], 0.5, None, ALU.is_gt).then_inc(s_flagi, 1)
            link(V.tensor_copy(fits[:], prob[:]))

            def h_s(par, sl, free):
                dve.wait_ge(s_sl, sl)
                if free is not None:
                    dve.wait_ge(s_ys, free)
                V.scalar_tensor_tensor(sil_s[:, par, :], sil_s[:, par, :], 1.0, GU[:, 0:CAP], ALU.add, ALU.mult
                                       ).then_inc(s_w8, 1)

            def expert_h(par, sl, free, seen):
                h_s(par, sl, free)
                dve.wait_ge(s_w8, seen)
                V.tensor_tensor(hT_s[:, par, :], sil_s[:, par, :], GU[:, CAP:2 * CAP], ALU.mult).then_inc(s_hs, 1)

            def gate_and_add(pair, ot, wo_name):
                for i in range(4):
                    n = pair.use(ot, i)
                    dve.wait_ge(s_gfull, pair.full(n))
                    t = 2 * i * P
                    V.tensor_tensor(oT[:, :, t:t + 2 * P], G[n % 2][:].rearrange("p (h t) -> p h t", h=2),
                                    gT[:, :, t:t + 2 * P], ALU.mult).then_inc(s_gD, 1)
                for i in range(4):
                    n = pair.use(wo_name, i)
                    dve.wait_ge(s_gfull, pair.full(n))
                    a = acc[:, 2 * i:2 * i + 2, :]
                    V.tensor_tensor(a, a, G[n % 2][:].rearrange("p (c d) -> p c d", c=2), ALU.add).then_inc(s_gD, 1)

            def root_mean_square(pair, k):
                dve.wait_ge(s_oA, pair.at(TT, TT * k))
                link(V.tensor_tensor(ss[:], ss[:], rs[:], ALU.mult))
                link(V.tensor_tensor(ss[:], ss[:], rs[:], ALU.mult))
                V.tensor_scalar(ss[:], ss[:], 1.0 / 128, EPS_O, ALU.mult, ALU.add).then_inc(s_ms, 1)

            def normalise(pair, k):
                dve.wait_ge(s_pw, pair.at(1, k))
                link(V.tensor_tensor(sc16[:], pw[:], rs[:], ALU.mult))
                V.tensor_tensor(o_n[:].rearrange("p c (h v) -> p (c h) v", h=2),
                                o_sb[:].rearrange("p c (h v) -> p (c h) v", h=2),
                                wide(sc16[:], P), ALU.mult).then_inc(s_on, 1)

            def slot_weights(first, n):
                for k in range(first, first + n):
                    link(V.tensor_tensor(prob[:], left[:], wide(top[:, :, k], E0), ALU.is_equal))
                    link(V.tensor_tensor(prob[:], prob[:], fits[:], ALU.mult))
                    link(V.tensor_reduce(w8[:, :, k], prob[:], AX, ALU.add))
                if first + n == TOP0:
                    link(V.tensor_scalar(w8[:], w8[:], 0.5, None, ALU.mult))

            def body(pair):
                j = pair.j

                def mask(m):
                    dve.wait_ge(s_sc, pair.at(16, m + 1))
                    if m >= 2:
                        dve.wait_ge(s_out, pair.at(16, m - 1))
                    V.tensor_tensor(masked[:, m % 2, :], score_bank(pair, m)[:, 0:2 * P],
                                    causal[:].rearrange("p a b -> p (a b)"), ALU.mult).then_inc(s_mask, 1)

                def expert_back(s):
                    dve.wait_ge(s_ys, j * STEPS + (s + 2))
                    dve.wait_ge(s_yst[s % 2], j * (8 * 16) + (s // 2 + 1) * 16)
                    V.tensor_copy(y_sb[0:HC, s % 2, :, :], YB[0:HC, :].rearrange("p (h d) -> p h d", h=2)).then_inc(s_ye, 1)
                    expert_h((s + 1) % 2, j * STEPS + (s + 2), j * STEPS + (s + 1), j * STEPS + (s + 2))

                def add_results(first, n):
                    for i in range(first, first + n):
                        q, k, t = i // TOP0, i % TOP0, j * 4 + i // TOP0
                        if k % 4 == 0:
                            dve.wait_ge(s_yg[2 * (q % 2) + k // 4], j * 128 + (q // 2 + 1) * 64)
                        dve.wait_ge(s_cadd, j * 32 + (i + 1))
                        a = acc[:, bass.ds(t, 1), :]
                        V.scalar_tensor_tensor(a, yg[:, q % 2, k:k + 1, :], w8[:, bass.ds(t, 1), k], a,
                                               ALU.mult, ALU.add).then_inc(s_cadd, 1)

                mask(0)
                for c in range(TT):
                    if c < TT - 1:
                        mask(c + 1)
                    dve.wait_ge(s_out, pair.at(16, c + 1))
                    V.tensor_tensor(ok[:, c, :], OUT[:, 0:P], ker[:, c, 2, :], ALU.mult).then_inc(s_okD, 1)
                    if pair.experts:
                        expert_back(c)
                    if pair.first:
                        slot_weights(c, 1)
                    if c == 1 and not pair.first:
                        root_mean_square(pair, 0)
                dve.wait_ge(s_okD, pair.at(8, 8))
                slots = ok[:].rearrange("p c (h m) -> p (c h) m", h=2)
                link(V.tensor_reduce(mx[:], slots, AX, ALU.max))
                V.tensor_tensor(slots, slots, wide(mx[:], 64), ALU.subtract).then_inc(s_sub, 1)
                if pair.combine:
                    add_results(0, TOP0 // 2)
                if not pair.last:
                    for hf in range(2):
                        n = pair.use("s", hf)
                        clip_s(pair.full(n), G[n % 2], hf)
                if not pair.first:
                    normalise(pair, 0)
                dve.wait_ge(s_pv, pair.at(1, 1))
                link(V.tensor_reduce(sm[:], pv[:].rearrange("p c (h m) -> p (c h) m", h=2), AX, ALU.add))
                link(V.reciprocal(rs[:], sm[:]))
                if not pair.last:
                    for hf in range(2):
                        n = pair.use("q", hf)
                        place_q(pair.full(n), G[n % 2], hf)
                for i in range(2):
                    n = pair.use("pvT", i)
                    dve.wait_ge(s_gfull, pair.full(n))
                    for h in range(2):
                        r = slice(64 * h, 64 * h + 64)
                        last = V.tensor_tensor(pbd[r, 4 * i:4 * i + 4, h, :],
                                               G[n % 2][r, :].rearrange("p (c t) -> p c t", c=4),
                                               rT[r, i * HALF:(i + 1) * HALF].rearrange("p (c t) -> p c t", c=4), ALU.mult)
                    last.then_inc(s_gD, 1)
                if pair.first:
                    for n in range(pair.use("oT"), pair.use("g")):
                        dve.wait_ge(s_gfull, pair.full(n))
                        V.tensor_copy(mv[:, n - pair.use("oT"), 0:1], G[n % 2][:, 0:1]).then_inc(s_gD, 1)
                else:
                    gate_and_add(pair, "oT", "wo")
                if not pair.last:
                    dve.wait_ge(s_e, pair.at(1, 2))
                    running_sum()
                if pair.combine:
                    add_results(TOP0 // 2, TOP0 // 2)
                for i in range(4):
                    n = pair.use("g", i)
                    h, hf = i // 2, i % 2
                    dve.wait_ge(s_th, pair.at(4, i + 1))
                    V.scalar_tensor_tensor(gT[:, h, hf * HALF:(hf + 1) * HALF], th[:, i % 2, :], 1.0,
                                           G[n % 2][:], ALU.add, ALU.mult).then_inc(s_gD, 1)
                mask(8)
                for c in range(TT):
                    if c < TT - 1:
                        mask(9 + c)
                    if not pair.last:
                        reciprocal_z(c)
                    if pair.combine:
                        add_results(8 + 3 * c, 3)
                    if pair.experts:
                        expert_back(8 + c)
                if pair.last:
                    root_mean_square(pair, 1)
                    normalise(pair, 1)
                    gate_and_add(pair, "oT_end", "wo_end")
                    dve.wait_ge(s_gD, pair.taken(pair.use("wo_end", 3))[1])

            def looped(rounds, make):
                start = links["base"] + links["n"]
                probe = LINKS[make(0)]
                with dve.Fori(0, rounds) as j:
                    links["base"], links["n"] = j * probe + start, 0
                    body(make(j, True))
                    assert links["n"] == probe, links["n"]
                links["base"], links["n"] = 0, start + rounds * probe

            def make_experts(j, pair=False):
                return Pair(j, 1, experts=True) if pair else "experts"

            def make_combine(j, pair=False):
                return Pair(j, 1 + EXPERT_PAIRS, combine=True) if pair else "combine"

            LINKS = {"experts": 7, "combine": 7}

            body(Pair(0, 0))
            dve.wait_ge(s_listed, 16)
            V.tensor_copy(list_f[:], list_i[:]).then_inc(s_listf, 1)
            dve.wait_ge(s_lT, 1)
            V.tensor_copy(idx[0:HC, 0:P], YB[0:HC, 0:P]).then_inc(s_idx, 1)
            expert_h(0, 1, None, 1)
            dve.wait_ge(s_xnd, 16)
            looped(EXPERT_PAIRS, make_experts)
            looped(2, make_combine)
            body(Pair(0, NP - 1))
            for dn in (fall, dense):
                dve.sem_inc(dn.h, 2)
                dve.sem_inc(dn.acc, 2)
            dve.sem_inc(s_att, 1)

            def dense_pass(dn, comb, u0, ne, f, beside=None):
                def make_h(j, u):
                    dve.wait_ge(dn.sil, j * 4 + (u0 + u + 1))
                    dve.wait_ge(dn.y, j * 4 + (u0 + u + 2))
                    V.tensor_tensor(h_f32[0:f, u % 2, :], sil[0:f, u % 2, :], bank[(u % 2) * 2 + 1][0:f, :],
                                    ALU.mult).then_inc(dn.made, 1)
                    dve.wait_ge(dn.made, j * 8 + (2 * (u0 + u) + 1))
                    V.tensor_copy(h_hi[0:f, u % 2, :], h_f32[0:f, u % 2, :]).then_inc(dn.made, 1)
                    dve.wait_ge(dn.made, j * 8 + (2 * (u0 + u) + 2))
                    V.tensor_tensor(h_lo[0:f, u % 2, :], h_f32[0:f, u % 2, :], h_hi[0:f, u % 2, :],
                                    ALU.subtract).then_inc(dn.h, 1)

                def add(j, u):
                    dve.wait_ge(dn.y, j * 4 + (u0 + u + 4))
                    dve.wait_ge(dn.acc, j * 4 + (u0 + u + 1))
                    for c in range(4):
                        yb = bank[4 + (u % 2) * 2 + c // 2][:, (c % 2) * D:(c % 2 + 1) * D]
                        t = (u % 2) * 4 + c
                        if comb is not None:
                            last = V.scalar_tensor_tensor(acc[:, t, :], yb, comb[:, t, bass.ds(j * 2 + u // 2, 1)],
                                                          acc[:, t, :], ALU.mult, ALU.add)
                        else:
                            last = V.tensor_tensor(acc[:, t, :], acc[:, t, :], yb, ALU.add)
                    last.then_inc(dn.acc, 1)

                def units(j, last):
                    for u in range(4):
                        if u < 3 or not last:
                            make_h(j, u + 1)
                        add(j, u)
                        if beside and not last:
                            beside(j, u)

                make_h(0, 0)
                with dve.Fori(0, ne // 2 - 1) as j:
                    units(j, False)
                units(ne // 2 - 1, True)

            over = dve.value_load(over_i[0:1, 0:1], min_val=0, max_val=1)
            with dve.If(over > 0):
                dense_pass(fall, over0, 0, E0, F0)
                dve.wait_ge(fall.acc, 2 + 2 * E0)
            layernorm(1)
            dve.wait_ge(s_xn, 2 * TT)
            for c in range(TT):
                last = V.tensor_tensor_reduce(out=qkv_qk[:, c, 0:D], in0=xn[:, c, :], in1=xn[:, c, :], scale=1.0, scalar=0.0,
                                              op0=ALU.mult, op1=ALU.add, accum_out=ss[:, c:c + 1])
            link(last)
            V.tensor_scalar(veps[:], ss[:, 0:TT], 1.0 / D, EPS_RMS, ALU.mult, ALU.add).then_inc(s_var, 1)
            link(V.tensor_tensor(acc[:], acc[:], xn[:], ALU.add))
            split_tokens(1)

            dve.wait_ge(s_ex, 2)
            V.memset(prob[:, :, E1:E1 + 2], -1.0)
            for c in range(TT):
                last = V.max(top[:, c, :], prob[:, c, 0:E1])
            link(last)
            link(V.memset(top[:, :, TOP1:8], -1.0))
            for c in range(TT):
                last = V.match_replace(left[:, c, 0:E1 + 2], top[:, c, :], prob[:, c, 0:E1 + 2], 0.0)
            link(last)
            link(V.tensor_tensor(comb1, prob[:, :, 0:E1 + 2], left[:, :, 0:E1 + 2], ALU.subtract))
            link(V.tensor_reduce(rsum[:], comb1[:, :, 0:E1], AX, ALU.add))
            link(V.tensor_scalar(rsum[:], rsum[:], 1e-20, None, ALU.add))
            link(V.reciprocal(rsum[:], rsum[:]))
            link(V.tensor_tensor(comb1[:, :, 0:E1], comb1[:, :, 0:E1],
                                 rsum[:].unsqueeze(2).broadcast_to([P, TT, E1]), ALU.mult))
            V.memset(comb1[:, :, E1:E1 + SH], 1.0).then_inc(s_comb, 1)

            dve.wait_ge(s_qkve, TT)
            V.tensor_scalar(ss[:], ss[:], 1.0 / D, EPS_RMS, ALU.mult, ALU.add).then_inc(s_qms, 1)
            dve.wait_ge(s_qpw, 1)
            pqk = pw[:].rearrange("p (c a) -> p a c", a=2)
            V.tensor_scalar(rs[:, 0:TT], pqk[:, 0, :], 0.5, None, ALU.mult)
            V.tensor_copy(rs[:, TT:2 * TT], pqk[:, 1, :]).then_inc(s_rqk, 1)
            for q in range(4):
                two = slice(2 * q, 2 * q + 2)
                dve.wait_ge(s_thw, TT + 2 * q + 2)
                V.tensor_tensor(wv[:, two, :], wk[:, two, :], qkv_v[:, two, :], ALU.mult).then_inc(s_wvv, 1)
            for k in range(KD):
                dve.wait_ge(s_t3e, 8)
                V.tensor_tensor_scan(wcum[:, k, :], ones[:], wcT[:, k, :], 0.0, ALU.mult, ALU.add)
            for k in range(KD):
                dve.wait_ge(s_t3e, 12)
                last = V.tensor_tensor_scan(kvcum[:, k, :], ones[:], kvT[:, k, :], 0.0, ALU.mult, ALU.add)
            link(last)
            V.tensor_scalar(wcum, wcum, 1e-6, 2.0, ALU.add, ALU.mult).then_inc(s_yc, 1)
            wcum_row, kv_row, thT_row, y_hi_row, y_lo_row = (
                buf.rearrange("p k t -> p (k t)") for buf in (wcum, kvcum, thT, y_hi, y_lo))
            NY = KD * T // ((E1 + SH) // 2 - 1)

            def y_step(j, u):
                a = bass.ds(j * NY, NY)
                dve.wait_ge(s_yc, j * 5 + (u + 1))
                if u == 0:
                    V.reciprocal(wcum_row[:, a], wcum_row[:, a]).then_inc(s_yc, 1)
                elif u == 1:
                    V.tensor_tensor(kv_row[:, a], kv_row[:, a], wcum_row[:, a], ALU.mult).then_inc(s_yc, 1)
                elif u == 2:
                    V.scalar_tensor_tensor(kv_row[:, a], thT_row[:, a], 1.0, kv_row[:, a], ALU.add,
                                           ALU.mult).then_inc(s_yc, 1)
                else:
                    V.tensor_copy(y_hi_row[:, a], kv_row[:, a]).then_inc(s_yc, 1)
                    dve.wait_ge(s_yc, j * 5 + 5)
                    V.tensor_tensor(y_lo_row[:, a], kv_row[:, a], y_hi_row[:, a], ALU.subtract).then_inc(s_yc, 1)

            dense_pass(dense, comb1, 0, E1 + SH, F1, y_step)
            dense_pass(dense, None, 2 * (E1 + SH), ESW, P)


def kernel(**inputs):
    import numpy as np
    import concourse.bacc as bacc
    from concourse.bass_utils import run_bass_kernel_spmd

    a = {k: np.asarray(v) for k, v in inputs.items()}

    def by_k(w):
        return w.reshape(KD, P, -1).transpose(1, 0, 2)

    def by_pair(w):
        return w.reshape(KD, P, NP, -1).transpose(2, 1, 0, 3)

    def by_expert(gate, up, down, pad=0):
        gate, up, down = (np.concatenate([w, np.zeros((pad, *w.shape[1:]), w.dtype)]) for w in (gate, up, down))
        e, _, f = gate.shape
        row = [w.reshape(e, KD, P, f).transpose(0, 2, 1, 3).reshape(e, P, KD * f) for w in (gate, up)]
        low = np.zeros((e, P, D), down.dtype)
        low[:, :f] = down
        return np.concatenate([*row, low], axis=2)

    w13 = a["L0_ffn_w13"]
    swi = a["L1_attn_w_swiglu"]
    ff = swi.shape[0] // 2
    sg, su, sd = (a[f"L1_ffn_{n}"] for n in ("sg", "su", "sd"))
    shared = [w.reshape(D, SH, F1).transpose(1, 0, 2) for w in (sg, su)]
    arrays = {
        "x": a["L0_attn_hidden_states"].reshape(T, D),
        "wqks": np.stack([by_pair(a[f"L0_attn_{n}"]) for n in ("Ws", "Wk", "Wq")], axis=2),
        "wvg": np.stack([by_pair(a["L0_attn_Wv"]), by_pair(a["L0_attn_Wg"])], axis=3),
        "wo": a["L0_attn_Wo"].reshape(NP, 2, P, D).transpose(0, 2, 1, 3),
        "gnw": a["L0_attn_g_norm_weight"].reshape(P, 1),
        "gate0": by_k(a["L0_ffn_gate_w"].T),
        "w0": by_expert(w13[:, :F0].transpose(0, 2, 1), w13[:, F0:].transpose(0, 2, 1), a["L0_ffn_w2"].transpose(0, 2, 1),
                        EP - E0),
        "wqkv": by_k(a["L1_attn_w_qkv"].T),
        "wsw": by_expert(swi[ff:].reshape(ESW, P, D).transpose(0, 2, 1), swi[:ff].reshape(ESW, P, D).transpose(0, 2, 1),
                         a["L1_attn_w_out"].T.reshape(ESW, P, D)),
        "gate1": by_k(a["L1_ffn_gate_w"]),
        "w1": by_expert(*(np.concatenate([w, s]) for w, s in (
            (a["L1_ffn_wg"], shared[0]), (a["L1_ffn_wu"], shared[1]), (a["L1_ffn_wd"], sd.reshape(SH, F1, D))))),
    }
    nc = bacc.Bacc("TRN2", target_bir_lowering=False, num_devices=1)
    args, given = [], {}
    for name, array in arrays.items():
        given[f"in_{name}"] = np.ascontiguousarray(array)
        args.append(nc.dram_tensor(f"in_{name}", array.shape, mybir.dt.from_np(array.dtype), kind="ExternalInput").ap())
    args.append(nc.dram_tensor("result", (T, D), F32, kind="ExternalOutput").ap())
    build(nc, *args)
    r = run_bass_kernel_spmd(nc, [given], core_ids=[0])
    return r.results[0]["result"].reshape(1, T, D)
```
